# Optimizing a Trainium2 kernel written in Bass

```python
import numpy as np
import jax
import jax.numpy as jnp

def _softmax(x, axis=-1):
    return jax.nn.softmax(x, axis=axis)

def _gelu(x):
    return jax.nn.gelu(x, approximate=True)

def _silu(x):
    return jax.nn.silu(x)

def _sigmoid(x):
    return jax.nn.sigmoid(x)

def _layernorm(x, axis=-1, eps=1e-05):
    m = jnp.mean(x, axis=axis, keepdims=True)
    v = jnp.var(x, axis=axis, keepdims=True)
    return (x - m) / jnp.sqrt(v + eps)

def _scatter_add(tgt, idx, src, axis=0):
    return tgt.at[idx].add(src)

def _segment_sum(src, seg, n):
    return jax.ops.segment_sum(src, seg, n)
kernel_name = 'mk_conv_attn_hybrid_d4_conv_nhwc768_r4_7e69f8'

def setup_inputs(seed: int=0):
    np.random.seed(seed)
    _w = jnp.asarray

    def _rec_inputs():
        import jax
        import jax.numpy as jnp
        _gk = jax.random.key(seed)
        x = -0.0002221 + 1 * jax.random.normal(jax.random.fold_in(_gk, 1), (8, 16, 16, 192), jnp.float32)
        return x
    x = _rec_inputs()

    def _L0_conv_setup():
        import jax, jax.numpy as jnp
        import numpy as np
        B, H, W, D = (8, 16, 16, 192)
        HEADS, WS = (12, 14)
        HD = D // HEADS
        MLP = 4 * D
        LREL = 2 * WS - 1
        EPS = 1e-05

        def _layer_norm(x, w, b):
            mu = jnp.mean(x, axis=-1, keepdims=True)
            var = jnp.mean(jnp.square(x - mu), axis=-1, keepdims=True)
            return (x - mu) * jax.lax.rsqrt(var + EPS) * w + b
        key = jax.random.key(seed)
        ks = jax.random.split(key, 12)
        s = 0.02
        return {'x': jax.random.normal(ks[0], (B, H, W, D), jnp.float32), 'qkv_w': jax.random.normal(ks[1], (D, 3 * D), jnp.float32) * s, 'qkv_b': jax.random.normal(ks[2], (3 * D,), jnp.float32) * s, 'proj_w': jax.random.normal(ks[3], (D, D), jnp.float32) * s, 'proj_b': jax.random.normal(ks[4], (D,), jnp.float32) * s, 'rel_pos_h': jax.random.normal(ks[5], (LREL, HD), jnp.float32) * s, 'rel_pos_w': jax.random.normal(ks[6], (LREL, HD), jnp.float32) * s, 'norm1_w': jnp.ones((D,), jnp.float32), 'norm1_b': jnp.zeros((D,), jnp.float32), 'norm2_w': jnp.ones((D,), jnp.float32), 'norm2_b': jnp.zeros((D,), jnp.float32), 'fc1_w': jax.random.normal(ks[7], (D, MLP), jnp.float32) * s, 'fc1_b': jax.random.normal(ks[8], (MLP,), jnp.float32) * s, 'fc2_w': jax.random.normal(ks[9], (MLP, D), jnp.float32) * s, 'fc2_b': jax.random.normal(ks[10], (D,), jnp.float32) * s}
    _L0_conv_all = _L0_conv_setup()
    _L0_conv_in = {k: v for k, v in _L0_conv_all.items() if k in ('qkv_w', 'qkv_b', 'proj_w', 'proj_b', 'rel_pos_h', 'rel_pos_w', 'norm1_w', 'norm1_b', 'norm2_w', 'norm2_b', 'fc1_w', 'fc1_b', 'fc2_w', 'fc2_b')}
    del _L0_conv_all

    def _L1_conv_setup():
        import jax, jax.numpy as jnp
        import numpy as np
        NUM_HEADS = 12

        def _rel_lookup(rel_pos, size):
            idx = jnp.arange(size)[:, None] - jnp.arange(size)[None, :] + (size - 1)
            return rel_pos[idx]
        key = jax.random.key(seed)
        ks = jax.random.split(key, 7)
        B, H, W, C = (8, 32, 32, 192)
        return {'x': jax.random.normal(ks[0], (B, H, W, C), dtype=jnp.float32), 'w_qkv': jax.random.normal(ks[1], (C, 3 * C), dtype=jnp.float32) * 0.02, 'b_qkv': jax.random.normal(ks[2], (3 * C,), dtype=jnp.float32) * 0.02, 'w_proj': jax.random.normal(ks[3], (C, C), dtype=jnp.float32) * 0.02, 'b_proj': jax.random.normal(ks[4], (C,), dtype=jnp.float32) * 0.02, 'rel_pos_h': jax.random.normal(ks[5], (2 * H - 1, C // NUM_HEADS), dtype=jnp.float32) * 0.02, 'rel_pos_w': jax.random.normal(ks[6], (2 * W - 1, C // NUM_HEADS), dtype=jnp.float32) * 0.02}
    _L1_conv_all = _L1_conv_setup()
    _L1_conv_in = {k: v for k, v in _L1_conv_all.items() if k in ('w_qkv', 'b_qkv', 'w_proj', 'b_proj', 'rel_pos_h', 'rel_pos_w')}
    del _L1_conv_all

    def _L2_attn_setup():
        import jax, jax.numpy as jnp
        import numpy as np
        N_EMBED = 192
        N_HEAD = 12
        B, T = (4, 512)
        key = jax.random.key(seed)
        ks = jax.random.split(key, 5)
        sc = N_EMBED ** (-0.5)
        return {'x': jax.random.normal(ks[0], (B, T, N_EMBED), dtype=jnp.float32), 'W_kqv': jax.random.normal(ks[1], (N_EMBED, 3 * N_EMBED), dtype=jnp.float32) * sc, 'b_kqv': jax.random.normal(ks[2], (3 * N_EMBED,), dtype=jnp.float32) * 0.02, 'W_proj': jax.random.normal(ks[3], (N_EMBED, N_EMBED), dtype=jnp.float32) * sc, 'b_proj': jax.random.normal(ks[4], (N_EMBED,), dtype=jnp.float32) * 0.02}
    _L2_attn_all = _L2_attn_setup()
    _L2_attn_in = {k: v for k, v in _L2_attn_all.items() if k in ('W_kqv', 'b_kqv', 'W_proj', 'b_proj')}
    del _L2_attn_all

    def _L2_ffn_setup():
        import jax, jax.numpy as jnp
        import numpy as np
        DECAY = 0.9
        EPS = 0.01
        TOP_K = 2
        key = jax.random.key(seed)
        k1, k2, k3, k4 = jax.random.split(key, 4)
        B, S, H, I, E = (4, 512, 192, 512, 8)
        return {'hidden_states': jax.random.normal(k1, (B, S, H), jnp.float32), 'router_w': jax.random.normal(k2, (E, H), jnp.float32) * 0.02, 'w1': jax.random.normal(k3, (E, I, H), jnp.float32) * 0.02, 'w2': jax.random.normal(k4, (E, H, I), jnp.float32) * 0.02}
    _L2_ffn_all = _L2_ffn_setup()
    _L2_ffn_in = {k: v for k, v in _L2_ffn_all.items() if k in ('router_w', 'w1', 'w2')}
    del _L2_ffn_all

    def _L3_attn_setup():
        import jax, jax.numpy as jnp
        import numpy as np
        HEADS = 12
        key = jax.random.key(seed)
        k1, k2, k3, k4 = jax.random.split(key, 4)
        B, N, D = (8, 256, 192)
        x = jax.random.normal(k1, (B, N, D), dtype=jnp.float32)
        w_qkv = jax.random.normal(k2, (D, 3 * D), dtype=jnp.float32) * (1.0 / np.sqrt(D))
        w_out = jax.random.normal(k3, (D, D), dtype=jnp.float32) * (1.0 / np.sqrt(D))
        b_out = jax.random.normal(k4, (D,), dtype=jnp.float32) * 0.01
        return {'x': x, 'w_qkv': w_qkv, 'w_out': w_out, 'b_out': b_out}
    _L3_attn_all = _L3_attn_setup()
    _L3_attn_in = {k: v for k, v in _L3_attn_all.items() if k in ('w_qkv', 'w_out', 'b_out')}
    del _L3_attn_all

    def _L3_ffn_setup():
        import jax, jax.numpy as jnp
        import numpy as np
        DIM = 192
        NUM_EXPERTS = 4
        NUM_HEADS = 12
        HEAD_DIM = DIM // NUM_HEADS
        MLP_HID = 4 * DIM
        FC1_OUT = MLP_HID + 3 * DIM
        FC2_IN = MLP_HID + DIM
        FC2_OUT = 2 * DIM
        CAP_FACTOR = 0.5
        LN_EPS = 1e-06
        key = jax.random.key(seed)
        ks = jax.random.split(key, 4)
        B, N = (8, 256)
        return {'x': jax.random.normal(ks[0], (B, N, DIM), jnp.float32), 'w_router': jax.random.normal(ks[1], (NUM_EXPERTS, DIM), jnp.float32) * 0.02, 'gamma1': jnp.ones((DIM,), jnp.float32), 'beta1': jnp.zeros((DIM,), jnp.float32), 'w1': jax.random.normal(ks[2], (FC1_OUT, DIM), jnp.float32) * 0.02, 'b1': jnp.zeros((FC1_OUT,), jnp.float32), 'w2': jax.random.normal(ks[3], (FC2_OUT, FC2_IN), jnp.float32) * 0.02, 'b2': jnp.zeros((FC2_OUT,), jnp.float32)}
    _L3_ffn_all = _L3_ffn_setup()
    _L3_ffn_in = {k: v for k, v in _L3_ffn_all.items() if k in ('w_router', 'gamma1', 'beta1', 'w1', 'b1', 'w2', 'b2')}
    del _L3_ffn_all
    return {'x': x, 'L0_conv_qkv_w': _L0_conv_in['qkv_w'], 'L0_conv_qkv_b': _L0_conv_in['qkv_b'], 'L0_conv_proj_w': _L0_conv_in['proj_w'], 'L0_conv_proj_b': _L0_conv_in['proj_b'], 'L0_conv_rel_pos_h': _L0_conv_in['rel_pos_h'], 'L0_conv_rel_pos_w': _L0_conv_in['rel_pos_w'], 'L0_conv_norm1_w': _L0_conv_in['norm1_w'], 'L0_conv_norm1_b': _L0_conv_in['norm1_b'], 'L0_conv_norm2_w': _L0_conv_in['norm2_w'], 'L0_conv_norm2_b': _L0_conv_in['norm2_b'], 'L0_conv_fc1_w': _L0_conv_in['fc1_w'], 'L0_conv_fc1_b': _L0_conv_in['fc1_b'], 'L0_conv_fc2_w': _L0_conv_in['fc2_w'], 'L0_conv_fc2_b': _L0_conv_in['fc2_b'], 'L1_conv_w_qkv': _L1_conv_in['w_qkv'], 'L1_conv_b_qkv': _L1_conv_in['b_qkv'], 'L1_conv_w_proj': _L1_conv_in['w_proj'], 'L1_conv_b_proj': _L1_conv_in['b_proj'], 'L1_conv_rel_pos_h': _L1_conv_in['rel_pos_h'], 'L1_conv_rel_pos_w': _L1_conv_in['rel_pos_w'], 'L2_attn_W_kqv': _L2_attn_in['W_kqv'], 'L2_attn_b_kqv': _L2_attn_in['b_kqv'], 'L2_attn_W_proj': _L2_attn_in['W_proj'], 'L2_attn_b_proj': _L2_attn_in['b_proj'], 'L2_ffn_router_w': _L2_ffn_in['router_w'], 'L2_ffn_w1': _L2_ffn_in['w1'], 'L2_ffn_w2': _L2_ffn_in['w2'], 'L3_attn_w_qkv': _L3_attn_in['w_qkv'], 'L3_attn_w_out': _L3_attn_in['w_out'], 'L3_attn_b_out': _L3_attn_in['b_out'], 'L3_ffn_w_router': _L3_ffn_in['w_router'], 'L3_ffn_gamma1': _L3_ffn_in['gamma1'], 'L3_ffn_beta1': _L3_ffn_in['beta1'], 'L3_ffn_w1': _L3_ffn_in['w1'], 'L3_ffn_b1': _L3_ffn_in['b1'], 'L3_ffn_w2': _L3_ffn_in['w2'], 'L3_ffn_b2': _L3_ffn_in['b2']}

def reference(x, L0_conv_qkv_w, L0_conv_qkv_b, L0_conv_proj_w, L0_conv_proj_b, L0_conv_rel_pos_h, L0_conv_rel_pos_w, L0_conv_norm1_w, L0_conv_norm1_b, L0_conv_norm2_w, L0_conv_norm2_b, L0_conv_fc1_w, L0_conv_fc1_b, L0_conv_fc2_w, L0_conv_fc2_b, L1_conv_w_qkv, L1_conv_b_qkv, L1_conv_w_proj, L1_conv_b_proj, L1_conv_rel_pos_h, L1_conv_rel_pos_w, L2_attn_W_kqv, L2_attn_b_kqv, L2_attn_W_proj, L2_attn_b_proj, L2_ffn_router_w, L2_ffn_w1, L2_ffn_w2, L3_attn_w_qkv, L3_attn_w_out, L3_attn_b_out, L3_ffn_w_router, L3_ffn_gamma1, L3_ffn_beta1, L3_ffn_w1, L3_ffn_b1, L3_ffn_w2, L3_ffn_b2):
    import jax
    import jax.numpy as jnp

    def _L0_conv_ref(x, qkv_w, qkv_b, proj_w, proj_b, rel_pos_h, rel_pos_w, norm1_w, norm1_b, norm2_w, norm2_b, fc1_w, fc1_b, fc2_w, fc2_b):
        import jax, jax.numpy as jnp
        import numpy as np
        B, H, W, D = (8, 16, 16, 192)
        HEADS, WS = (12, 14)
        HD = D // HEADS
        MLP = 4 * D
        LREL = 2 * WS - 1
        EPS = 1e-05

        def _layer_norm(x, w, b):
            mu = jnp.mean(x, axis=-1, keepdims=True)
            var = jnp.mean(jnp.square(x - mu), axis=-1, keepdims=True)
            return (x - mu) * jax.lax.rsqrt(var + EPS) * w + b
        shortcut = x
        xn = _layer_norm(x, norm1_w, norm1_b)
        pad_h = (WS - H % WS) % WS
        pad_w = (WS - W % WS) % WS
        Hp, Wp = (H + pad_h, W + pad_w)
        xp = jnp.pad(xn, ((0, 0), (0, pad_h), (0, pad_w), (0, 0)))
        win = xp.reshape(B, Hp // WS, WS, Wp // WS, WS, D)
        win = win.transpose(0, 1, 3, 2, 4, 5).reshape(-1, WS, WS, D)
        Bn = win.shape[0]
        N = WS * WS
        qkv = win.reshape(Bn, N, D) @ qkv_w + qkv_b
        qkv = qkv.reshape(Bn, N, 3, HEADS, HD).transpose(2, 0, 3, 1, 4)
        qkv = qkv.reshape(3, Bn * HEADS, N, HD)
        q, k, v = (qkv[0], qkv[1], qkv[2])
        scale = HD ** (-0.5)
        attn = jnp.einsum('bqc,bkc->bqk', q * scale, k)
        coords = jnp.arange(WS)[:, None] - jnp.arange(WS)[None, :] + (WS - 1)
        Rh = rel_pos_h[coords]
        Rw = rel_pos_w[coords]
        r_q = q.reshape(-1, WS, WS, HD)
        rel_h = jnp.einsum('bhwc,hkc->bhwk', r_q, Rh)
        rel_w = jnp.einsum('bhwc,wkc->bhwk', r_q, Rw)
        attn = (attn.reshape(-1, WS, WS, WS, WS) + rel_h[:, :, :, :, None] + rel_w[:, :, :, None, :]).reshape(-1, N, N)
        attn = jax.nn.softmax(attn, axis=-1)
        out = jnp.einsum('bqk,bkc->bqc', attn, v)
        out = out.reshape(Bn, HEADS, WS, WS, HD).transpose(0, 2, 3, 1, 4).reshape(Bn, WS, WS, D)
        out = out @ proj_w + proj_b
        out = out.reshape(B, Hp // WS, Wp // WS, WS, WS, D)
        out = out.transpose(0, 1, 3, 2, 4, 5).reshape(B, Hp, Wp, D)[:, :H, :W, :]
        x = shortcut + out
        xn2 = _layer_norm(x, norm2_w, norm2_b)
        h = jax.nn.gelu(xn2 @ fc1_w + fc1_b, approximate=False)
        x = x + (h @ fc2_w + fc2_b)
        return x

    def _L1_conv_ref(x, w_qkv, b_qkv, w_proj, b_proj, rel_pos_h, rel_pos_w):
        import jax, jax.numpy as jnp
        import numpy as np
        NUM_HEADS = 12

        def _rel_lookup(rel_pos, size):
            idx = jnp.arange(size)[:, None] - jnp.arange(size)[None, :] + (size - 1)
            return rel_pos[idx]
        B, H, W, C = x.shape
        nh = NUM_HEADS
        hd = C // nh
        scale = hd ** (-0.5)
        qkv = x @ w_qkv + b_qkv
        qkv = qkv.reshape(B, H * W, 3, nh, hd).transpose(2, 0, 3, 1, 4)
        qkv = qkv.reshape(3, B * nh, H * W, hd)
        q, k, v = (qkv[0], qkv[1], qkv[2])
        attn = jnp.einsum('bqd,bkd->bqk', q * scale, k)
        Rh = _rel_lookup(rel_pos_h, H)
        Rw = _rel_lookup(rel_pos_w, W)
        r_q = q.reshape(B * nh, H, W, hd)
        rel_h = jnp.einsum('bhwc,hkc->bhwk', r_q, Rh)
        rel_w = jnp.einsum('bhwc,wkc->bhwk', r_q, Rw)
        attn = (attn.reshape(B * nh, H, W, H, W) + rel_h[:, :, :, :, None] + rel_w[:, :, :, None, :]).reshape(B * nh, H * W, H * W)
        attn = jax.nn.softmax(attn, axis=-1)
        out = jnp.einsum('bqk,bkd->bqd', attn, v)
        out = out.reshape(B, nh, H, W, hd).transpose(0, 2, 3, 1, 4).reshape(B, H, W, C)
        return out @ w_proj + b_proj

    def _L2_attn_ref(x, W_kqv, b_kqv, W_proj, b_proj):
        import jax, jax.numpy as jnp
        import numpy as np
        N_EMBED = 192
        N_HEAD = 12
        B, T = (4, 512)
        Bx, Tx, C = x.shape
        H = N_HEAD
        D = C // H
        kqv = x @ W_kqv + b_kqv
        k, q, v = jnp.split(kqv, 3, axis=-1)
        k = k.reshape(Bx, Tx, H, D).transpose(0, 2, 1, 3)
        q = q.reshape(Bx, Tx, H, D).transpose(0, 2, 1, 3)
        v = v.reshape(Bx, Tx, H, D).transpose(0, 2, 1, 3)
        scores = jnp.einsum('bhqd,bhkd->bhqk', q, k) * D ** (-0.5)
        causal = jnp.tril(jnp.ones((Tx, Tx), dtype=bool))
        scores = jnp.where(causal[None, None, :, :], scores, -jnp.inf)
        attn = jax.nn.softmax(scores, axis=-1)
        out = jnp.einsum('bhqk,bhkd->bhqd', attn, v)
        out = out.transpose(0, 2, 1, 3).reshape(Bx, Tx, C)
        return out @ W_proj + b_proj

    def _L2_ffn_ref(hidden_states, router_w, w1, w2):
        import jax, jax.numpy as jnp
        import numpy as np
        DECAY = 0.9
        EPS = 0.01
        TOP_K = 2
        B, S, H = hidden_states.shape
        E = router_w.shape[0]
        flat = hidden_states.reshape(B * S, H)
        logits = flat @ router_w.T
        probs = jax.nn.softmax(logits, axis=-1)
        topk_probs, topk_idx = jax.lax.top_k(probs, TOP_K)
        importance = jax.lax.stop_gradient(probs).sum(axis=0)
        running = jnp.ones((E,), dtype=flat.dtype)
        blended = running + (1.0 - DECAY) * (importance - running)
        running = blended + EPS
        balance = running[topk_idx]
        balanced = topk_probs / balance
        balanced = balanced / balanced.sum(axis=-1, keepdims=True)
        h = jnp.einsum('th,eih->tei', flat, w1)
        h = jax.nn.silu(h)
        outs = jnp.einsum('tei,ehi->teh', h, w2)
        sel = jnp.take_along_axis(outs, topk_idx[:, :, None], axis=1)
        combined = (sel * balanced[..., None]).sum(axis=1)
        return combined.reshape(B, S, H)

    def _L3_attn_ref(x, w_qkv, w_out, b_out):
        import jax, jax.numpy as jnp
        import numpy as np
        HEADS = 12
        B, N, D = x.shape
        h = HEADS
        dh = D // h
        scale = D ** (-0.5)
        qkv = x @ w_qkv
        q, k, v = jnp.split(qkv, 3, axis=-1)

        def split_heads(t):
            return t.reshape(B, N, h, dh).transpose(0, 2, 1, 3)
        q, k, v = (split_heads(q), split_heads(k), split_heads(v))
        dots = jnp.einsum('bhid,bhjd->bhij', q, k) * scale
        attn = jax.nn.softmax(dots, axis=-1)
        out = jnp.einsum('bhij,bhjd->bhid', attn, v)
        out = out.transpose(0, 2, 1, 3).reshape(B, N, D)
        return out @ w_out + b_out

    def _L3_ffn_ref(x, w_router, gamma1, beta1, w1, b1, w2, b2):
        import jax, jax.numpy as jnp
        import numpy as np
        DIM = 192
        NUM_EXPERTS = 4
        NUM_HEADS = 12
        HEAD_DIM = DIM // NUM_HEADS
        MLP_HID = 4 * DIM
        FC1_OUT = MLP_HID + 3 * DIM
        FC2_IN = MLP_HID + DIM
        FC2_OUT = 2 * DIM
        CAP_FACTOR = 0.5
        LN_EPS = 1e-06
        B, N, C = x.shape
        E = NUM_EXPERTS
        cap = int(CAP_FACTOR * N)
        m = np.array([C // 2 ** (E - 1 - e) for e in range(E)])
        in_mask = (np.arange(C)[None, :] < m[:, None]).astype(np.float32)
        in_mask = jnp.asarray(in_mask)
        out_mask = jnp.concatenate([in_mask, in_mask], axis=-1)
        logits = jnp.einsum('bnc,ec->bne', x, w_router)
        probs = jax.nn.softmax(logits, axis=-1)
        gate, idx = jax.lax.top_k(jnp.swapaxes(probs, 1, 2), cap)
        dispatch = jax.nn.one_hot(idx, N, dtype=x.dtype)
        combine = dispatch * gate[..., None]
        mu = jnp.mean(x, -1, keepdims=True)
        var = jnp.var(x, -1, keepdims=True)
        y = (x - mu) * jax.lax.rsqrt(var + LN_EPS) * gamma1 + beta1
        xg = jnp.einsum('becn,bnd->becd', dispatch, y)
        xg = xg * in_mask[None, :, None, :]
        h = jnp.einsum('becd,fd->becf', xg, w1) + b1
        h = jnp.einsum('becn,becf->bnf', dispatch, h)
        x_mlp, x_qkv = (h[..., :MLP_HID], h[..., MLP_HID:])
        qkv = x_qkv.reshape(B, N, 3, NUM_HEADS, HEAD_DIM).transpose(2, 0, 3, 1, 4)
        q, k, v = (qkv[0], qkv[1], qkv[2])
        scale = HEAD_DIM ** (-0.5)
        attn = jax.nn.softmax(jnp.einsum('bhqd,bhkd->bhqk', q, k) * scale, axis=-1)
        x_attn = jnp.einsum('bhqk,bhkd->bhqd', attn, v)
        x_attn = x_attn.transpose(0, 2, 1, 3).reshape(B, N, C)
        x_mlp = jax.nn.gelu(x_mlp, approximate=False)
        y2 = jnp.concatenate([x_mlp, x_attn], axis=-1)
        yg = jnp.einsum('becn,bnf->becf', dispatch, y2)
        o = jnp.einsum('becf,of->beco', yg, w2) + b2
        o = o * out_mask[None, :, None, :]
        z = jnp.einsum('becn,beco->bno', combine, o)
        x_mlp2, x_attn2 = (z[..., :C], z[..., C:])
        return x + x_mlp2 + x_attn2

    def _gn(v, G=32, eps=1e-05):
        B_, H_, W_, C_ = v.shape
        g = v.reshape(B_, H_, W_, G, C_ // G)
        m = jnp.mean(g, axis=(1, 2, 4), keepdims=True)
        s = jnp.var(g, axis=(1, 2, 4), keepdims=True)
        return ((g - m) / jnp.sqrt(s + eps)).reshape(v.shape)

    def _ln_c(v, eps=1e-06):
        m = jnp.mean(v, axis=-1, keepdims=True)
        s = jnp.var(v, axis=-1, keepdims=True)
        return (v - m) / jnp.sqrt(s + eps)

    def _ln_t(v, eps=1e-05):
        m = jnp.mean(v, axis=-1, keepdims=True)
        s = jnp.var(v, axis=-1, keepdims=True)
        return (v - m) / jnp.sqrt(s + eps)

    def _to_tokens(v):
        B_, H_, W_, C_ = v.shape
        return v.reshape(B_, H_ * W_, C_)

    def _from_tokens(t, like):
        return t.reshape(like.shape)
    x = _L0_conv_ref(x, L0_conv_qkv_w, L0_conv_qkv_b, L0_conv_proj_w, L0_conv_proj_b, L0_conv_rel_pos_h, L0_conv_rel_pos_w, L0_conv_norm1_w, L0_conv_norm1_b, L0_conv_norm2_w, L0_conv_norm2_b, L0_conv_fc1_w, L0_conv_fc1_b, L0_conv_fc2_w, L0_conv_fc2_b)
    x = x + _L1_conv_ref(_gn(x), L1_conv_w_qkv, L1_conv_b_qkv, L1_conv_w_proj, L1_conv_b_proj, L1_conv_rel_pos_h, L1_conv_rel_pos_w)
    t = _to_tokens(x)
    t = t + _L2_attn_ref(_ln_t(t), L2_attn_W_kqv, L2_attn_b_kqv, L2_attn_W_proj, L2_attn_b_proj)
    t = t + _L2_ffn_ref(_ln_t(t), L2_ffn_router_w, L2_ffn_w1, L2_ffn_w2)
    t = t + _L3_attn_ref(_ln_t(t), L3_attn_w_qkv, L3_attn_w_out, L3_attn_b_out)
    t = t + _L3_ffn_ref(_ln_t(t), L3_ffn_w_router, L3_ffn_gamma1, L3_ffn_beta1, L3_ffn_w1, L3_ffn_b1, L3_ffn_w2, L3_ffn_b2)
    x = _from_tokens(t, x)
    return x

_drawn_inputs = setup_inputs


def setup_inputs(seed=0):
    import zlib

    import numpy as np

    out = dict(_drawn_inputs(seed))
    spreads = {'L0_conv_norm1_w': (1.0, 0.6),
     'L0_conv_norm1_b': (0.0, 0.487),
     'L0_conv_norm2_w': (1.0, 0.6),
     'L0_conv_norm2_b': (0.0, 0.525),
     'L3_ffn_gamma1': (1.0, 0.6),
     'L3_ffn_beta1': (0.0, 0.8),
     'L3_ffn_b1': (0.0, 0.373),
     'L3_ffn_b2': (0.0, 0.324)}
    factors = {'L0_conv_qkv_w': 3.232,
     'L0_conv_qkv_b': 4.799,
     'L0_conv_rel_pos_h': 8.0,
     'L0_conv_rel_pos_w': 8.0,
     'L0_conv_fc1_b': 5.23,
     'L1_conv_w_qkv': 5.736,
     'L1_conv_b_qkv': 4.89,
     'L1_conv_w_proj': 3.869,
     'L1_conv_rel_pos_h': 8.0,
     'L1_conv_rel_pos_w': 8.0,
     'L3_attn_b_out': 6.129,
     'L2_attn_b_kqv': 2.888,
     'L2_attn_b_proj': 3.145}
    for name, (base, spread) in spreads.items():
        noise = np.random.default_rng([zlib.crc32(name.encode()), seed]).standard_normal(out[name].shape)
        drawn = base * np.exp(spread * noise) if base else spread * noise
        out[name] = jnp.asarray(drawn.astype(out[name].dtype))
    for name, factor in factors.items():
        out[name] = (out[name] * factor).astype(out[name].dtype)
    return out
```

```python
from contextlib import ExitStack

import numpy as np
import concourse.bass as bass
from concourse import mybir

F32 = mybir.dt.float32
BF16 = mybir.dt.bfloat16
ALU = mybir.AluOpType
ACT = mybir.ActivationFunctionType
AX = mybir.AxisListType

B, HH, WW, D = 8, 16, 16, 192
NTOK = HH * WW
HEADS, HD = 12, 16
QUADS, QH = 3, 4
IMGS = 2
TURNS = B // IMGS
T = IMGS * NTOK
TT = T // 128
CH = 96
MROW = 16
WS = 14
NPAD = WS * WS
MLP = 4 * D
E2, I2 = 8, 512
E3 = 4
CAP = NTOK // 2
SEGS = [(0, 24), (24, 48), (48, 96), (96, 192)]
MASKED = -1e30
VW = HD + 1


class Attn:

    def __init__(self, name, scale, rel=0, pad=False, causal=False):
        self.name, self.scale, self.rel, self.pad, self.causal = name, scale, rel, pad, causal
        self.keys = [(0, 128), (128, 128)] + ([(256, 98), (354, 98)] if pad else [])
        self.nk = NTOK + (NPAD if pad else 0)
        self.heads_per_unit = 1 if pad else 2
        self.units = QH // self.heads_per_unit


L0 = Attn("l0", HD ** -0.5, rel=WS, pad=True)
L1 = Attn("l1", HD ** -0.5, rel=HH)
L2 = Attn("l2", HD ** -0.5, causal=True)
L3 = Attn("l3", D ** -0.5)
L4 = Attn("l4", HD ** -0.5)


class Signals:

    def __init__(self, nc, ctx, loop, names, per):
        self.sem = {n: ctx.enter_context(nc.semaphore(f"{loop}_{n}")) for n in names}
        self.per = {n: per.get(n, 1) for n in names}
        self.made = dict.fromkeys(names, 0)


class Port:

    def __init__(self, eng, signals, turn):
        self.eng, self.s, self.turn = eng, signals, turn
        self.seen = dict.fromkeys(signals.sem, 0)

    def wait(self, name, n=1):
        self.seen[name] += n
        self.eng.wait_ge(self.s.sem[name], self.turn * self.s.per[name] + self.seen[name])

    def passed(self, name, n):
        self.seen[name] += n

    def inc(self, ins, name):
        self.s.made[name] += 1
        ins.then_inc(self.s.sem[name], 1)

    def link(self, ins, name):
        self.inc(ins, name)
        self.seen[name] += 1
        self.eng.wait_ge(self.s.sem[name], self.seen[name])

    def restart(self, name):
        self.eng.sem_clear(self.s.sem[name])


NAMES = ["dve_step", "pool_step", "act_step", "var_ready", "rstd_ready", "rows_ready", "turned", "xt0_ready",
         "xt1_ready", "qk_mm", "v_mm", "q_ready", "k_ready", "v_ready", "rel_mm", "rel_ready", "smax_mm",
         "max_done", "mt_mm", "qm_ready", "st_mm", "exp_done", "pv_mm", "at_ready", "proj_mm", "x_ready",
         "fc1_mm", "h_ready", "fc2_mm", "acc_done", "stat_ready", "stat_mm", "gate_mm", "gate_in", "gate_exp",
         "prow_in", "prow_mm", "turn_end"]


def program(nc, a, out, per):
    with ExitStack() as ctx:
        def sb(name, *shape):
            return ctx.enter_context(nc.sbuf_tensor(name, list(shape), F32))

        def sem(name):
            return ctx.enter_context(nc.semaphore(name))

        xall = sb("xall", 128, TURNS * TT, D)
        x = sb("x", 128, TT, D + 1)
        xn = sb("xn", 128, TT, D + 1)
        att = xn
        lx = sb("lx", 128, TT, D + 1)
        xg = sb("xg", 128, TT, D + 1)
        yb = sb("yb", 128, TT, D)
        xt = sb("xt", CH + 1, 2, T)
        qt = sb("qt", 128, QUADS, T)
        kt = sb("kt", 128, QUADS, T)
        relt = sb("relt", 128, QUADS, T)
        qm = sb("qm", 128, 2, NTOK)
        negmax = sb("negmax", 128, 2, 2, 128)
        v = sb("v", 128, TT, HEADS, VW)
        p = sb("p", 128, 2, 1024)
        hid = sb("hid", 128, 8, T)
        pall = sb("pall", 128, TURNS * TT, E2)
        stats = sb("stats", 128, TT, 6)
        mv = sb("mv", 128, TT, 2)
        ve = sb("ve", 128, 4)
        rstd = sb("rstd", 128, 4)
        nhalf = sb("nhalf", 128, 4)
        gsc = sb("gsc", CH + 1, 4)
        gbi = sb("gbi", CH + 1, 4)
        gst = sb("gst", CH, 2, 4)
        rsum = sb("rsum", 128, 2, HEADS)
        gl = sb("gl", 128, TT, E2)
        ge = sb("ge", 128, TT, E2)
        gm = sb("gm", 128, TT)
        gs = sb("gs", 128, TT)
        oh = sb("oh", 128, 3, TT, E2)
        cw = sb("cw", 128, TT, E2)
        imp = sb("imp", 128, E2)
        rrun = sb("rrun", 128, E2)
        p4 = sb("p4", 128, 2, IMGS, E3)
        prow = sb("prow", IMGS * E3, NTOK)
        left = sb("left", IMGS * E3, NTOK)
        srow = sb("srow", IMGS * E3, NTOK)
        top8 = sb("top8", IMGS * E3, 8)
        sel = sb("sel", 128, IMGS, 2, E3)
        gate = sb("gate", 128, IMGS, 2, E3)
        ones = sb("ones", 128, 128)
        order = sb("order", 128, E2)
        mask = yb[:, :, :].rearrange("p i d -> p (i d)")[:, 0:2 * NTOK + 128]
        mask16 = ctx.enter_context(nc.sbuf_tensor("mask16", [128, 2 * NTOK + 128 + 128], BF16))
        later, earlier, ident16 = mask16[:, 0:512], mask16[:, 512:640], mask16[:, 640:768]

        WL = 2 * QUADS * 128 + 2 * D
        lw = sb("lw", 128, 3 * 2 * WL)
        lw2 = sb("lw2", CH + 1, 2, 2, WL)
        wts = {n: lw[0:CH + 1, i * 2 * WL:(i + 1) * 2 * WL].rearrange("p (c n) -> p c n", c=2)
               for i, n in enumerate(("l0", "l1", "l2"))}
        wts |= {"l3": lw2[:, 0], "l4": lw2[:, 1]}
        moe2 = lw[:, 0:E2 * 4 * D].rearrange("p (e k n) -> p e k n", e=E2, k=4)
        rw = sb("rw", 128, 2 * E2 * I2)
        n0, n1 = 2 * WS * 128, 2 * HH * 128
        relw = {"l0": rw[:, 0:n0].rearrange("p (a h n) -> p a h n", a=2, h=WS),
                "l1": rw[:, n0:n0 + n1].rearrange("p (a h n) -> p a h n", a=2, h=HH)}
        moe1 = rw[0:CH, :].rearrange("p (c e i) -> p c e i", c=2, e=E2)
        fc1 = sb("fc1", CH + 1, 2, MLP)
        fc2 = sb("fc2", 128, MLP // 128, D)
        ffn1 = sb("ffn1", CH + 1, 2, MLP)
        ffn2 = sb("ffn2", 128, MLP // 128, 2, D)
        ffn2a = sb("ffn2a", CH + 1, 2, 2, D)
        cols = sb("cols", CH + 1, 2, 4)
        gb3 = sb("gb3", 128, 2, D)
        ident = sb("ident", 128, 128)
        e0 = sb("e0", 128, NTOK + NPAD)
        e1 = sb("e1", 128, NTOK)
        kpad = sb("kpad", 128, QUADS, NPAD)
        vpad = sb("vpad", 98, HEADS, VW)
        win = hid[0:4, 6:8, :].rearrange("p a n -> p (a n)")[:, 0:128 + T]
        fc2b = sb("fc2b", 1, D)
        ggrp = sb("ggrp", CH, CH)
        rout = sb("rout", CH, 2, E2 + E3)
        ps = ctx.enter_context(nc.psum_tensor("ps", [128, 8, 512], F32))

        ld_x, ld_a, ld_b, ld_moe = sem("ld_x"), sem("ld_a"), sem("ld_b"), sem("ld_moe")
        set_up, kpad_scaled, ffn2_summed = sem("set_up"), sem("kpad_scaled"), sem("ffn2_summed")
        imp_in, imp_mm, imp_step, imp_done, stored = (sem("imp_in"), sem("imp_mm"), sem("imp_step"),
                                                      sem("imp_done"), sem("stored"))
        sa = Signals(nc, ctx, "a", NAMES, per.get("a", {}))
        sbb = Signals(nc, ctx, "b", NAMES, per.get("b", {}))

        loads_a = [(lw[0:CH + 1, :], a["lw"]), (rw[:, 0:n0 + n1], a["relw"]), (fc1[:, :, :], a["fc1"]),
                   (fc2[:, :, :], a["fc2"]), (cols[:, :, :], a["cols"]), (ident[:, :], a["ident"]),
                   (e0[:, :], a["e0"]), (e1[:, :], a["e1"]), (kpad[:, :, :], a["kpad"]),
                   (vpad[:, :, :], a["vpad"]), (win, a["win"]), (fc2b[:, :], a["fc2b"]),
                   (mask, a["mask"]), (ggrp[:, :], a["ggrp"]), (rout[:, :, :], a["rout"])]
        loads_b = [(lw2[:, :, :, :], a["lw2"]), (ffn1[:, :, :], a["ffn1"]), (ffn2[:, :, :, :], a["ffn2"]),
                   (ffn2a[:, :, :, :], a["ffn2a"]), (gb3[:, :, :], a["gb3"])]

        def turn_x(t):
            return xall[:, bass.ds(t * TT, TT), :]

        block = ctx.enter_context(nc.Block())

        @block.sync
        def _(sp):
            sp.dma_start(xall[:, :, :], a["x"].rearrange("(t p) d -> p t d", p=128)).then_inc(ld_x, 16)
            for dst, src in loads_a:
                sp.dma_start(dst, src).then_inc(ld_a, 16)
            for dst, src in loads_b:
                sp.dma_start(dst, src).then_inc(ld_b, 16)
            sp.wait_ge(sa.sem["turn_end"], TURNS)
            sp.dma_start(moe1, a["moe1"]).then_inc(ld_moe, 16)
            sp.dma_start(moe2, a["moe2"]).then_inc(ld_moe, 16)
            with sp.Fori(0, TURNS) as t:
                sp.wait_ge(sbb.sem["turn_end"], t + 1)
                sp.dma_start(out.rearrange("(t p) d -> p t d", p=128)[:, bass.ds(t * TT, TT), :],
                             turn_x(t)).then_inc(stored, 16)
            sp.wait_ge(stored, 16 * TURNS)

        @block.tensor
        def _(pe):
            def mm(o, w, m, start=True, stop=True):
                return pe.matmul(o, w, m, start=start, stop=stop)

            def turn_over(q, src):
                for c in range(2):
                    n = CH + c
                    for i in range(TT):
                        last = pe.transpose(ps[0:n, 6 + c, i * 128:(i + 1) * 128],
                                            src[:, i, c * CH:c * CH + n], ident[:, :])
                    q.inc(last, "turned")

            def wait_xt(q):
                q.wait("xt0_ready")
                q.wait("xt1_ready")

            def qkv(q, l):
                w = wts[l.name]
                for s in range(2 * QUADS):
                    for c in range(2):
                        last = mm(ps[:, s, :], w[:, c, s * 128:(s + 1) * 128], xt[:, c, :], c == 0, c == 1)
                    q.inc(last, "qk_mm")
                for i in range(TT):
                    for c in range(2):
                        last = mm(ps[:, 6 + i // 2, (i % 2) * D:(i % 2 + 1) * D],
                                  xt[:, c, i * 128:(i + 1) * 128], w[:, c, 768:768 + D], c == 0, c == 1)
                    if i % 2:
                        q.inc(last, "v_mm")

            def rel_rows(q, l):
                w = relw[l.name]
                for s in range(QUADS):
                    q.wait("q_ready")
                    if l.pad:
                        mm(ps[:, s, :], win[:, 0:128], win[:, 128:128 + T])
                    for ax in range(2):
                        for h in range(HH):
                            def at(z):
                                z = z.rearrange("p (i h w) -> p i h w", i=IMGS, h=HH)
                                return z[:, :, h, :] if ax == 0 else z[:, :, :, h]
                            last = pe.matmul(at(ps[:, s, :]), w[:, ax, h % l.rel, :], at(qt[:, s, :]),
                                             start=not l.pad and ax == 0 and h == 0,
                                             stop=True, skip_group_check=True)
                    q.inc(last, "rel_mm")

            def attention(q, l):
                et = e0 if l.pad else e1
                nu, hu = l.units, l.heads_per_unit

                def smax(g, u):
                    im, s = g // QUADS, g % QUADS
                    if u:
                        q.wait("max_done")
                    for jj in range(hu):
                        j = u * hu + jj
                        r = slice(32 * j, 32 * j + 32)
                        for half in range(2):
                            t0 = im * NTOK + half * 128
                            parts = [(kt[r, s, im * NTOK:(im + 1) * NTOK], 0, NTOK)]
                            if l.pad:
                                parts.append((kpad[r, s, :], NTOK, NPAD))
                            for k, at, n in parts:
                                o = ps[:, half if l.pad else jj, at:at + n] if l.pad else \
                                    ps[:, jj, half * NTOK:(half + 1) * NTOK]
                                last = mm(o, qt[r, s, t0:t0 + 128], k, True, not (l.rel or l.causal))
                                if l.rel:
                                    last = mm(o, relt[r, s, t0:t0 + 128], et[r, at:at + n], False, True)
                                if l.causal:
                                    last = mm(o, ident16[:, :], later[:, half * 256:half * 256 + NTOK], False, True)
                    q.inc(last, "smax_mm")

                def turn_max(g):
                    q.wait("max_done")
                    for half in range(2):
                        last = pe.transpose(ps[:, 7, (g % 2) * NTOK + half * 128:(g % 2) * NTOK + half * 128 + 128],
                                            negmax[:, g % 2, half, :], ident[:, :])
                    q.inc(last, "mt_mm")

                def scores(g, u, n):
                    im, s = g // QUADS, g % QUADS
                    if u == 0:
                        q.wait("qm_ready")
                    for jj in range(hu):
                        j = u * hu + jj
                        r = slice(32 * j, 32 * j + 32)
                        for ki, (k0, nk) in enumerate(l.keys):
                            w = kt[r, s, im * NTOK + k0:im * NTOK + k0 + nk] if k0 < NTOK else \
                                kpad[r, s, k0 - NTOK:k0 - NTOK + nk]
                            at = (jj * 2 + ki) * NTOK
                            if l.causal:
                                q0 = 128 * ki
                                bank = ps[:, 2 + 2 * (n % 2) + jj, :]
                                mm(bank[:, at % 512:at % 512 + NTOK - q0], w, qm[r, g % 2, q0:NTOK], True, False)
                                last = mm(bank[:, at % 512:at % 512 + 128], ident16[:, :], earlier[:, :],
                                          False, True)
                                continue
                            o = ps[0:nk, 2 + 2 * (n % 2) + at // 512, at % 512:at % 512 + NTOK]
                            last = mm(o, w, qm[r, g % 2, :], True, not l.rel)
                            if l.rel:
                                last = mm(o, et[r, k0:k0 + nk], relt[r, s, im * NTOK:(im + 1) * NTOK], False, True)
                    q.inc(last, "st_mm")

                def values(g, u, n):
                    im, s = g // QUADS, g % QUADS
                    q.wait("exp_done")
                    if n == QUADS * nu:
                        q.wait("at_ready")
                    for jj in range(hu):
                        head = s * QH + u * hu + jj
                        for half in range(2):
                            o = ps[:, 6, (half * HEADS + head) * VW:(half * HEADS + head + 1) * VW]
                            keys = l.keys[0:half + 1] if l.causal else l.keys
                            for ki, (k0, nk) in enumerate(keys):
                                at = (jj * 2 + ki) * NTOK + (0 if l.causal and ki else half * 128)
                                vv = v[:, im * 2 + ki, head, :] if k0 < NTOK else vpad[:, head, :]
                                last = mm(o, p[0:nk, n % 2, at:at + 128], vv, ki == 0, ki == len(keys) - 1)
                    q.inc(last, "pv_mm")

                if not l.rel:
                    q.wait("q_ready", QUADS)
                else:
                    q.wait("rel_ready", QUADS)
                q.wait("k_ready", QUADS)
                q.wait("v_ready", 2)
                for u in range(nu):
                    smax(0, u)
                turn_max(0)
                groups = IMGS * QUADS
                for g in range(groups):
                    for u in range(nu):
                        n = g * nu + u
                        if g + 1 < groups:
                            smax(g + 1, u)
                        scores(g, u, n)
                        if n:
                            values((n - 1) // nu, (n - 1) % nu, n - 1)
                    if g + 1 < groups:
                        turn_max(g + 1)
                values(groups - 1, nu - 1, groups * nu - 1)

            def project(q, l):
                q.wait("at_ready")
                turn_over(q, att)
                wait_xt(q)
                w = wts[l.name]
                for i in range(TT):
                    for c in range(2):
                        last = mm(ps[:, i // 2, (i % 2) * D:(i % 2 + 1) * D],
                                  xt[:, c, i * 128:(i + 1) * 128], w[:, c, 768 + D:768 + 2 * D], c == 0, c == 1)
                    if i % 2:
                        q.inc(last, "proj_mm")

            def hidden(q, w):
                for m in range(MLP // 128):
                    for c in range(2):
                        last = mm(ps[:, m, :], w[:, c, m * 128:(m + 1) * 128], xt[:, c, :], c == 0, c == 1)
                    q.inc(last, "fc1_mm")

            def gate_logits(q, w):
                n = w.shape[2]
                for i in range(TT):
                    for c in range(2):
                        last = mm(ps[:, 0, i * n:(i + 1) * n], xt[0:CH, c, i * 128:(i + 1) * 128], w[:, c, :],
                                  c == 0, c == 1)
                q.inc(last, "gate_mm")

            pe.wait_ge(ld_a, 16 * len(loads_a))
            pe.wait_ge(set_up, 1)
            pe.wait_ge(kpad_scaled, 1)
            with pe.Fori(0, TURNS) as t:
                q = Port(pe, sa, t)
                q.wait("rows_ready")
                turn_over(q, xn)
                wait_xt(q)
                qkv(q, L0)
                rel_rows(q, L0)
                attention(q, L0)
                project(q, L0)
                q.wait("rows_ready")
                turn_over(q, xn)
                wait_xt(q)
                hidden(q, fc1)
                for i in range(TT):
                    o = ps[:, 6 + i // 2, (i % 2) * D:(i % 2 + 1) * D]
                    mm(o, ones[0:1, :], fc2b[:, :], True, False)
                    for m in range(MLP // 128):
                        if i == 0:
                            q.wait("h_ready")
                        last = mm(o, hid[:, m, i * 128:(i + 1) * 128], fc2[:, m, :], False, m == MLP // 128 - 1)
                    if i % 2:
                        q.inc(last, "fc2_mm")
                q.wait("rows_ready")
                turn_over(q, x)
                q.wait("stat_ready")
                q.inc(mm(ps[0:CH, 0, 0:4], ggrp[:, :], gst[:, 0, :]), "stat_mm")
                q.wait("stat_ready")
                q.inc(mm(ps[0:CH, 0, 4:8], ggrp[:, :], gst[:, 1, :]), "stat_mm")
                wait_xt(q)
                qkv(q, L1)
                rel_rows(q, L1)
                attention(q, L1)
                project(q, L1)
                q.wait("rows_ready")
                turn_over(q, xn)
                wait_xt(q)
                qkv(q, L2)
                attention(q, L2)
                project(q, L2)
                q.wait("rows_ready")
                turn_over(q, xn)
                wait_xt(q)
                gate_logits(q, rout[:, :, 0:E2])

            pe.wait_ge(ld_b, 16 * len(loads_b))
            pe.wait_ge(imp_in, 1)
            mm(ps[:, 0, 0:E2], ones[:, :], imp[:, :]).then_inc(imp_mm, 1)
            pe.wait_ge(ld_moe, 32)
            pe.wait_ge(ffn2_summed, 1)
            pe.wait_ge(imp_done, 1)
            with pe.Fori(0, TURNS) as t:
                q = Port(pe, sbb, t)
                q.wait("rows_ready")
                turn_over(q, xn)
                wait_xt(q)

                def up(e):
                    for m in range(4):
                        if e:
                            q.wait("h_ready")
                        for c in range(2):
                            last = mm(ps[:, m, :], moe1[:, c, e, m * 128:(m + 1) * 128], xt[0:CH, c, :],
                                      c == 0, c == 1)
                        q.inc(last, "fc1_mm")

                def down(e):
                    if e + 1 == E2:
                        q.wait("h_ready", 4)
                    if e >= 2:
                        q.wait("acc_done")
                    for i in range(TT):
                        o = ps[:, 4 + 2 * (e % 2) + i // 2, (i % 2) * D:(i % 2 + 1) * D]
                        for m in range(4):
                            last = mm(o, hid[:, 4 * (e % 2) + m, i * 128:(i + 1) * 128], moe2[:, e, m, :],
                                      m == 0, m == 3)
                    q.inc(last, "fc2_mm")

                up(0)
                for e in range(E2):
                    if e + 1 < E2:
                        up(e + 1)
                    down(e)
                q.passed("acc_done", 2)

                q.wait("rows_ready")
                turn_over(q, xn)
                wait_xt(q)
                qkv(q, L3)
                attention(q, L3)
                project(q, L3)

                q.wait("rows_ready")
                turn_over(q, lx)
                wait_xt(q)
                gate_logits(q, rout[:, :, E2:E2 + E3])
                q.wait("prow_in")
                for half in range(2):
                    last = pe.transpose(ps[0:IMGS * E3, 1, half * 128:(half + 1) * 128],
                                        p4[:, half, :, :].rearrange("p i e -> p (i e)"), ident[:, :])
                q.inc(last, "prow_mm")
                q.wait("prow_in")
                for half in range(2):
                    last = mm(ps[:, 2, half * 8:half * 8 + 8], srow[:, half * 128:(half + 1) * 128],
                              ident[0:8, 0:8])
                q.inc(last, "prow_mm")
                q.wait("rows_ready")
                turn_over(q, xg)
                wait_xt(q)
                hidden(q, ffn1)
                q.wait("h_ready", 6)
                qkv(q, L4)
                attention(q, L4)
                q.wait("at_ready")
                turn_over(q, att)
                wait_xt(q)
                for i in range(TT):
                    o = ps[:, i // 2, (i % 2) * D:(i % 2 + 1) * D]
                    for m in range(MLP // 128):
                        mm(o, hid[:, m, i * 128:(i + 1) * 128], ffn2[:, m, 0, :], m == 0, False)
                    for c in range(2):
                        last = mm(o, xt[:, c, i * 128:(i + 1) * 128], ffn2a[:, c, 0, :], False, c == 1)
                    if i % 2:
                        q.inc(last, "proj_mm")

        @block.scalar
        def _(act):
            def xt0(q, w=None):
                q.wait("turned", 1)
                q.passed("turned", 1)
                if w is None:
                    ins = act.activation(xt[0:CH, 0, :], ps[0:CH, 6, :], ACT.Copy)
                else:
                    ins = act.activation(xt[0:CH, 0, :], ps[0:CH, 6, :], ACT.Identity,
                                         scale=cols[0:CH, 0, w:w + 1], bias=cols[0:CH, 0, w + 1:w + 2])
                q.inc(ins, "xt0_ready")

            def attention(q, l):
                for s in range(QUADS):
                    q.wait("qk_mm")
                    q.inc(act.activation(qt[:, s, :], ps[:, s, :], ACT.Copy), "q_ready")
                q.passed("qk_mm", QUADS)
                for i in range(2):
                    q.wait("v_mm")
                    q.inc(act.activation(v[:, 2 * i:2 * i + 2, :, 0:HD],
                                         ps[:, 6 + i, 0:2 * D].rearrange("p (i h d) -> p i h d", i=2, h=HEADS),
                                         ACT.Copy), "v_ready")
                if l.rel:
                    for s in range(QUADS):
                        q.wait("rel_mm")
                        q.inc(act.activation(relt[:, s, :], ps[:, s, :], ACT.Copy), "rel_ready")
                n = IMGS * QUADS * l.units
                for u in range(n):
                    q.wait("st_mm")
                    if u >= 2:
                        q.wait("pv_mm")
                    src = ps[:, 2 + 2 * (u % 2):4 + 2 * (u % 2), :].rearrange("p b n -> p (b n)")
                    if l.pad:
                        act.activation(p[:, u % 2, 0:512], src[:, 0:512], ACT.Exp)
                        ins = act.activation(p[0:98, u % 2, 512:1024], src[0:98, 512:1024], ACT.Exp)
                    elif l.causal:
                        n3 = NTOK + 128
                        ins = act.activation(p[:, u % 2, :].rearrange("p (j n) -> p j n", j=2)[:, :, 0:n3],
                                             src.rearrange("p (j n) -> p j n", j=2)[:, :, 0:n3], ACT.Exp)
                    else:
                        ins = act.activation(p[:, u % 2, :], src, ACT.Exp)
                    q.inc(ins, "exp_done")
                q.passed("pv_mm", 2)

            def hidden(q, func):
                for m in range(MLP // 128):
                    q.wait("fc1_mm")
                    q.inc(act.activation(hid[:, m, :], ps[:, m, :], func), "h_ready")

            def gate_exp(q):
                q.wait("gate_in")
                q.inc(act.activation(ge[:, :, :], gl[:, :, :], ACT.Exp), "gate_exp")

            act.wait_ge(ld_a, 16 * len(loads_a))
            act.wait_ge(set_up, 1)
            with act.Fori(0, TURNS) as t:
                q = Port(act, sa, t)
                xt0(q, 0)
                attention(q, L0)
                xt0(q)
                xt0(q, 2)
                hidden(q, ACT.Gelu)
                q.wait("stat_ready", 3)
                for im in range(IMGS):
                    ins = act.activation(xt[0:CH, 0, im * NTOK:(im + 1) * NTOK],
                                         ps[0:CH, 6, im * NTOK:(im + 1) * NTOK], ACT.Identity,
                                         scale=gsc[0:CH, im:im + 1], bias=gbi[0:CH, im:im + 1])
                q.inc(ins, "xt0_ready")
                q.passed("turned", 2)
                attention(q, L1)
                xt0(q)
                xt0(q)
                attention(q, L2)
                xt0(q)
                xt0(q)
                gate_exp(q)
            with act.Fori(0, TURNS) as t:
                q = Port(act, sbb, t)
                xt0(q)
                for e in range(E2):
                    for m in range(4):
                        q.wait("fc1_mm")
                        if e >= 2 and m == 0:
                            q.wait("fc2_mm")
                        q.inc(act.activation(hid[:, 4 * (e % 2) + m, :], ps[:, m, :], ACT.Silu), "h_ready")
                q.passed("fc2_mm", 2)
                xt0(q)
                attention(q, L3)
                xt0(q)
                xt0(q)
                gate_exp(q)
                xt0(q)
                hidden(q, ACT.Gelu)
                attention(q, L4)
                xt0(q)

        @block.gpsimd
        def _(pool):
            pool.wait_ge(set_up, 1)
            for s, n in ((sa, 4), (sbb, 4)):
                with pool.Fori(0, TURNS) as t:
                    q = Port(pool, s, t)
                    for i in range(5 if s is sa else 4):
                        q.wait("var_ready")
                        q.inc(pool.tensor_tensor(rstd[:, :], ve[:, :], nhalf[:, :], ALU.pow), "rstd_ready")

        @block.vector
        def _(dve):
            def norm(q, src, dst, eps, signal=None):
                for i in range(TT):
                    ins = dve.bn_stats(stats[:, i, :], src[:, i, 0:D])
                q.link(ins, "dve_step")
                for i in range(TT):
                    ins = dve.bn_aggr(mv[:, i, :], stats[:, i, :])
                q.link(ins, "dve_step")
                q.inc(dve.tensor_scalar(ve[:, 0:TT], mv[:, :, 1], eps, None, ALU.add), "var_ready")
                q.wait("rstd_ready")
                for i in range(TT):
                    ins = dve.tensor_scalar(dst[:, i, 0:D], src[:, i, 0:D], mv[:, i, 0:1], rstd[:, i:i + 1],
                                            ALU.subtract, ALU.mult)
                if signal:
                    q.inc(ins, signal)
                else:
                    q.link(ins, "dve_step")

            def xt1(q, w=None):
                q.wait("turned", 2)
                if w is None:
                    ins = dve.tensor_copy(xt[:, 1, :], ps[0:CH + 1, 7, :])
                else:
                    ins = dve.tensor_scalar(xt[:, 1, :], ps[0:CH + 1, 7, :], cols[:, 1, w:w + 1],
                                            cols[:, 1, w + 1:w + 2], ALU.mult, ALU.add)
                q.inc(ins, "xt1_ready")

            def attention(q, l):
                q.passed("qk_mm", QUADS)
                for s in range(QUADS):
                    q.wait("qk_mm")
                    q.inc(dve.tensor_scalar(kt[:, s, :], ps[:, QUADS + s, :], l.scale, None, ALU.mult), "k_ready")
                nu, hu = l.units, l.heads_per_unit

                def row_max(g, u):
                    q.wait("smax_mm")
                    j = u * hu
                    if l.pad:
                        o = negmax[:, g % 2, :, 32 * j + MROW]
                        i = ps[:, 0:2, 0:l.nk]
                    else:
                        o = negmax[:, g % 2, :, :].rearrange("p h (j r) -> p j h r", j=QH)[:, j:j + hu, :, MROW]
                        i = ps[:, 0:2, :].rearrange("p j (h k) -> p j h k", h=2)
                    q.inc(dve.tensor_reduce(o, i, AX.X, ALU.max, negate=True), "max_done")

                def take_max(g):
                    im, s = g // QUADS, g % QUADS
                    q.wait("mt_mm")
                    q.inc(dve.tensor_tensor(qm[:, g % 2, :], qt[:, s, im * NTOK:(im + 1) * NTOK],
                                            ps[:, 7, (g % 2) * NTOK:(g % 2 + 1) * NTOK], ALU.add), "qm_ready")

                def divide(im):
                    q.wait("pv_mm", QUADS * nu)
                    o = ps[:, 6, 0:2 * HEADS * VW].rearrange("p (f h d) -> p f h d", f=2, h=HEADS)
                    q.link(dve.reciprocal(rsum[:, :, :], o[:, :, :, HD]), "dve_step")
                    r = rsum[:, :, :].unsqueeze(3).to_broadcast([128, 2, HEADS, HD])
                    q.inc(dve.tensor_tensor(att[:, 2 * im:2 * im + 2, 0:D].rearrange("p f (h d) -> p f h d", h=HEADS),
                                            o[:, :, :, 0:HD], r, ALU.mult), "at_ready")

                if not l.rel:
                    q.wait("q_ready", QUADS)
                else:
                    q.passed("q_ready", QUADS)
                for u in range(nu):
                    row_max(0, u)
                take_max(0)
                groups = IMGS * QUADS
                for g in range(groups):
                    if g + 1 < groups:
                        for u in range(nu):
                            row_max(g + 1, u)
                            if g == QUADS and u == 0:
                                divide(0)
                        take_max(g + 1)
                divide(1)

            def residual(q, name, dst_turn=None):
                for i in range(2):
                    q.wait(name)
                    dst = x[:, 2 * i:2 * i + 2, 0:D]
                    ins = dve.tensor_tensor(dst, ps[:, (6 if name == "fc2_mm" else 0) + i, 0:2 * D]
                                            .rearrange("p (i d) -> p i d", i=2), dst, ALU.add)
                q.link(ins, "dve_step")

            def probabilities(q, n):
                q.wait("gate_mm")
                lg = ps[:, 0, 0:TT * n].rearrange("p (i e) -> p i e", i=TT)
                q.link(dve.tensor_reduce(gm[:, :], lg, AX.X, ALU.max), "dve_step")
                q.inc(dve.tensor_tensor(gl[:, :, 0:n], lg, gm[:, :].unsqueeze(2).to_broadcast([128, TT, n]),
                                        ALU.subtract), "gate_in")
                q.wait("gate_exp")
                q.link(dve.tensor_reduce(gs[:, :], ge[:, :, 0:n], AX.X, ALU.add), "dve_step")
                q.link(dve.reciprocal(gs[:, :], gs[:, :]), "dve_step")
                return gs[:, :].unsqueeze(2).to_broadcast([128, TT, n])

            dve.memset(nhalf[:, :], -0.5)
            dve.memset(ones[:, :], 1.0)
            dve.memset(negmax[:, :, :, :], 0.0)
            for e in range(E2):
                dve.memset(order[:, e:e + 1], float(E2 - e))
            for z in (x, xn, lx, xg):
                dve.memset(z[:, :, D:D + 1], 1.0)
            dve.memset(xt[CH:CH + 1, 0, :], 1.0)
            dve.memset(gsc[CH:CH + 1, :], 1.0)
            dve.memset(gbi[CH:CH + 1, :], 0.0)
            dve.memset(gl[:, :, :], 0.0)
            dve.memset(v[:, :, :, HD:VW], 1.0).then_inc(set_up, 1)
            dve.wait_ge(ld_a, 16 * len(loads_a))
            dve.wait_ge(ld_x, 16)
            dve.tensor_copy(mask16[:, 0:640], mask)
            dve.tensor_copy(ident16, ident[:, :])
            dve.tensor_scalar(kpad[:, :, :], kpad[:, :, :], L0.scale, None, ALU.mult).then_inc(kpad_scaled, 1)
            with dve.Fori(0, TURNS) as t:
                q = Port(dve, sa, t)
                q.restart("dve_step")
                q.link(dve.tensor_copy(x[:, :, 0:D], turn_x(t)), "dve_step")
                norm(q, x, xn, 1e-5, "rows_ready")
                xt1(q, 0)
                attention(q, L0)
                xt1(q)
                residual(q, "proj_mm")
                norm(q, x, xn, 1e-5, "rows_ready")
                xt1(q, 2)
                for i in range(2):
                    q.wait("fc2_mm")
                    dst = x[:, 2 * i:2 * i + 2, 0:D]
                    ins = dve.tensor_tensor(dst, ps[:, 6 + i, 0:2 * D].rearrange("p (i d) -> p i d", i=2), dst,
                                            ALU.add)
                q.inc(ins, "rows_ready")

                q.wait("turned", 2)
                for c in range(2):
                    for im in range(IMGS):
                        ins = dve.bn_stats(stats[0:CH, 2 * c + im, :], ps[0:CH, 6 + c, im * NTOK:(im + 1) * NTOK])
                q.link(ins, "dve_step")
                for i in range(4):
                    ins = dve.bn_aggr(mv[0:CH, i, :], stats[0:CH, i, :])
                q.link(ins, "dve_step")
                q.inc(dve.tensor_copy(gst[:, 0, :], mv[0:CH, :, 0]), "stat_ready")
                q.wait("stat_mm")
                q.link(dve.tensor_tensor(gbi[0:CH, :], gst[:, 0, :], ps[0:CH, 0, 0:4], ALU.subtract), "dve_step")
                q.link(dve.tensor_tensor(gbi[0:CH, :], gbi[0:CH, :], gbi[0:CH, :], ALU.mult), "dve_step")
                q.inc(dve.tensor_tensor(gst[:, 1, :], gbi[0:CH, :], mv[0:CH, :, 1], ALU.add), "stat_ready")
                q.wait("stat_mm")
                q.inc(dve.tensor_scalar(ve[0:CH, :], ps[0:CH, 0, 4:8], 1e-5, None, ALU.add), "var_ready")
                q.wait("rstd_ready")
                q.link(dve.tensor_copy(gsc[0:CH, :], rstd[0:CH, :]), "dve_step")
                q.inc(dve.scalar_tensor_tensor(out=gbi[0:CH, :], in0=ps[0:CH, 0, 0:4], scalar=-1.0,
                                               in1=gsc[0:CH, :], op0=ALU.mult, op1=ALU.mult), "stat_ready")
                q.wait("stat_ready", 3)
                for im in range(IMGS):
                    ins = dve.tensor_scalar(xt[:, 1, im * NTOK:(im + 1) * NTOK],
                                            ps[0:CH + 1, 7, im * NTOK:(im + 1) * NTOK],
                                            gsc[:, 2 + im:3 + im], gbi[:, 2 + im:3 + im], ALU.mult, ALU.add)
                q.inc(ins, "xt1_ready")
                attention(q, L1)
                xt1(q)
                residual(q, "proj_mm")

                norm(q, x, xn, 1e-5, "rows_ready")
                xt1(q)
                attention(q, L2)
                xt1(q)
                residual(q, "proj_mm")
                dve.tensor_copy(turn_x(t), x[:, :, 0:D])
                norm(q, x, xn, 1e-5, "rows_ready")
                xt1(q)
                r = probabilities(q, E2)
                q.inc(dve.tensor_tensor(pall[:, bass.ds(t * TT, TT), :], ge[:, :, :], r, ALU.mult), "turn_end")

            dve.wait_ge(sa.sem["turn_end"], TURNS)
            dve.tensor_reduce(imp[:, :], pall[:, :, :].rearrange("p t e -> p e t"), AX.X, ALU.add)\
                .then_inc(imp_in, 1)
            dve.wait_ge(imp_mm, 1)
            dve.tensor_scalar(rrun[:, :], ps[:, 0, 0:E2], 1.0, 1.0 - 0.9, ALU.subtract, ALU.mult)\
                .then_inc(imp_step, 1)
            dve.wait_ge(imp_step, 1)
            dve.tensor_scalar(imp[:, :], rrun[:, :], 1.0, 0.01, ALU.add, ALU.add).then_inc(imp_step, 1)
            dve.wait_ge(imp_step, 2)
            dve.reciprocal(rrun[:, :], imp[:, :]).then_inc(imp_done, 1)
            dve.wait_ge(ld_b, 16 * len(loads_b))
            dve.tensor_tensor(ffn2[:, :, 0, :], ffn2[:, :, 0, :], ffn2[:, :, 1, :], ALU.add)
            dve.tensor_tensor(ffn2a[:, :, 0, :], ffn2a[:, :, 0, :], ffn2a[:, :, 1, :], ALU.add)\
                .then_inc(ffn2_summed, 1)
            dve.wait_ge(imp_done, 1)
            with dve.Fori(0, TURNS) as t:
                q = Port(dve, sbb, t)
                q.restart("dve_step")
                q.link(dve.tensor_copy(x[:, :, 0:D], turn_x(t)), "dve_step")
                norm(q, x, xn, 1e-5, "rows_ready")
                xt1(q)
                q.link(dve.tensor_copy(gl[:, :, :], pall[:, bass.ds(t * TT, TT), :]), "dve_step")
                q.link(dve.tensor_copy(cw[:, :, :], gl[:, :, :]), "dve_step")
                ob = order[:, :].unsqueeze(1).to_broadcast([128, TT, E2])
                for k in range(2):
                    q.link(dve.tensor_reduce(gm[:, :], cw[:, :, :], AX.X, ALU.max), "dve_step")
                    gmb = gm[:, :].unsqueeze(2).to_broadcast([128, TT, E2])
                    q.link(dve.tensor_tensor(oh[:, k], cw[:, :, :], gmb, ALU.is_equal), "dve_step")
                    q.link(dve.tensor_tensor(oh[:, k], oh[:, k], ob, ALU.mult), "dve_step")
                    q.link(dve.tensor_reduce(gm[:, :], oh[:, k], AX.X, ALU.max), "dve_step")
                    q.link(dve.tensor_tensor(oh[:, k], ob, gmb, ALU.is_equal), "dve_step")
                    if k == 0:
                        q.link(dve.scalar_tensor_tensor(out=cw[:, :, :], in0=oh[:, 0], scalar=-2.0,
                                                        in1=cw[:, :, :], op0=ALU.mult, op1=ALU.add), "dve_step")
                q.link(dve.tensor_tensor(oh[:, 2], oh[:, 0], oh[:, 1], ALU.add), "dve_step")
                q.link(dve.tensor_tensor(cw[:, :, :], oh[:, 2], gl[:, :, :], ALU.mult), "dve_step")
                q.link(dve.tensor_tensor(cw[:, :, :], cw[:, :, :],
                                         rrun[:, :].unsqueeze(1).to_broadcast([128, TT, E2]), ALU.mult), "dve_step")
                q.link(dve.tensor_reduce(gs[:, :], cw[:, :, :], AX.X, ALU.add), "dve_step")
                q.link(dve.reciprocal(gs[:, :], gs[:, :]), "dve_step")
                q.link(dve.tensor_tensor(cw[:, :, :], cw[:, :, :],
                                         gs[:, :].unsqueeze(2).to_broadcast([128, TT, E2]), ALU.mult), "dve_step")
                for e in range(E2):
                    q.wait("fc2_mm")
                    for i in range(TT):
                        dst = x[:, i, 0:D]
                        ins = dve.scalar_tensor_tensor(
                            out=dst, in0=ps[:, 4 + 2 * (e % 2) + i // 2, (i % 2) * D:(i % 2 + 1) * D],
                            scalar=cw[:, i, e:e + 1], in1=dst, op0=ALU.mult, op1=ALU.add)
                    q.inc(ins, "acc_done")
                    q.wait("acc_done")

                norm(q, x, xn, 1e-5, "rows_ready")
                xt1(q)
                attention(q, L3)
                xt1(q)
                residual(q, "proj_mm")

                norm(q, x, lx, 1e-5, "rows_ready")
                q.wait("rows_ready", 3)
                xt1(q)
                r = probabilities(q, E3)
                q.inc(dve.tensor_tensor(p4[:, :, :, :].rearrange("p f i e -> p i f e"),
                                        ge[:, :, 0:E3].rearrange("p (i f) e -> p i f e", i=IMGS),
                                        gs[:, :].rearrange("p (i f) -> p i f", i=IMGS).unsqueeze(3)
                                        .to_broadcast([128, IMGS, 2, E3]), ALU.mult), "prow_in")
                norm(q, lx, yb, 1e-6)
                q.wait("prow_mm")
                q.link(dve.tensor_copy(prow[:, :], ps[0:8, 1, 0:NTOK]), "dve_step")
                rows = [prow, left]
                for k in range(CAP // 8):
                    q.link(dve.max(top8[:, :], rows[k % 2][:, :]), "dve_step")
                    q.link(dve.match_replace(rows[(k + 1) % 2][:, :], top8[:, :], rows[k % 2][:, :], -1.0),
                           "dve_step")
                q.inc(dve.tensor_scalar(srow[:, :], rows[(CAP // 8) % 2][:, :], 0.0, None, ALU.is_lt), "prow_in")
                g3 = gb3[:, :, :].unsqueeze(2).to_broadcast([128, 2, TT, D])
                q.link(dve.tensor_tensor(yb[:, :, :], yb[:, :, :], g3[:, 0], ALU.mult), "dve_step")
                q.link(dve.tensor_tensor(yb[:, :, :], yb[:, :, :], g3[:, 1], ALU.add), "dve_step")
                q.wait("prow_mm")
                q.link(dve.tensor_copy(sel[:, :, :, :].rearrange("p i f e -> p f i e"),
                                       ps[:, 2, 0:16].rearrange("p (f i e) -> p f i e", f=2, i=IMGS)), "dve_step")
                q.link(dve.tensor_tensor(gate[:, :, :, :], sel[:, :, :, :],
                                         p4[:, :, :, :].rearrange("p f i e -> p i f e"), ALU.mult), "dve_step")
                for e in range(E3 - 2, -1, -1):
                    for z in (sel, gate):
                        ins = dve.tensor_tensor(z[:, :, :, e], z[:, :, :, e], z[:, :, :, e + 1], ALU.add)
                    q.link(ins, "dve_step")
                ssum = sel[:, :, :, :].rearrange("p i f e -> p (i f) e")
                gsum = gate[:, :, :, :].rearrange("p i f e -> p (i f) e")
                dve.tensor_copy(xg[:, :, D], ssum[:, :, 0])
                for e, (c0, c1) in enumerate(SEGS):
                    ins = dve.tensor_tensor(xg[:, :, c0:c1], yb[:, :, c0:c1],
                                            ssum[:, :, e:e + 1].to_broadcast([128, TT, c1 - c0]), ALU.mult)
                q.inc(ins, "rows_ready")
                xt1(q)
                attention(q, L4)
                xt1(q)
                q.link(dve.tensor_tensor(x[:, :, 0:D], x[:, :, 0:D], lx[:, :, 0:D], ALU.add), "dve_step")
                for i in range(2):
                    q.wait("proj_mm")
                    for e, (c0, c1) in enumerate(SEGS):
                        ins = dve.tensor_tensor(
                            yb[:, 2 * i:2 * i + 2, c0:c1],
                            ps[:, i, 0:2 * D].rearrange("p (i d) -> p i d", i=2)[:, :, c0:c1],
                            gsum[:, 2 * i:2 * i + 2, e:e + 1].to_broadcast([128, 2, c1 - c0]), ALU.mult)
                q.link(ins, "dve_step")
                q.inc(dve.tensor_tensor(turn_x(t), x[:, :, 0:D], yb[:, :, :], ALU.add), "turn_end")
                q.wait("turn_end")

        return {"a": sa.made, "b": sbb.made}


def attention_weights(w, b, proj, proj_b, scale):
    o = np.zeros((CH + 1, 2, 2 * QUADS * 128 + 2 * D), np.float32)
    qk = o[:, :, 0:2 * QUADS * 128].reshape(CH + 1, 2, 2, HEADS, 32)
    for c in range(2):
        rows = slice(c * CH, (c + 1) * CH)
        qk[0:CH, c, :, :, 0:HD] = w[rows, 0:2 * D].reshape(CH, 2, HEADS, HD)
        o[0:CH, c, 768:768 + D] = w[rows, 2 * D:3 * D]
        if proj is not None:
            o[0:CH, c, 768 + D:] = proj[rows]
    qk[CH, 0, 1, :, MROW] = 1.0 / scale
    if b is not None:
        qk[CH, 1, :, :, 0:HD] = b[0:2 * D].reshape(2, HEADS, HD)
        o[CH, 1, 768:768 + D] = b[2 * D:3 * D]
    if proj_b is not None:
        o[CH, 1, 768 + D:] = proj_b
    return o


def by_chunk(w, b=None):
    o = np.zeros((CH + (b is not None), 2, w.shape[1]), np.float32)
    o[0:CH] = w.reshape(2, CH, -1).transpose(1, 0, 2)
    if b is not None:
        o[CH, 1] = b
    return o


def rel_weights(rh, rw, n):
    o = np.zeros((QH, 32, 2, n, QH, 32), np.float32)
    idx = np.arange(n)[:, None] - np.arange(n)[None, :] + n - 1
    for j in range(QH):
        o[j, 0:HD, 0, :, j, 0:n] = rh[idx].transpose(2, 0, 1)
        o[j, 0:HD, 1, :, j, n:2 * n] = rw[idx].transpose(2, 0, 1)
    return o.reshape(128, -1)


def constants():
    h, w = np.divmod(np.arange(NTOK), WW)
    window = (h // WS) * 2 + w // WS
    e1 = np.zeros((32, NTOK), np.float32)
    e1[h, np.arange(NTOK)] = 1
    e1[HH + w, np.arange(NTOK)] = 1
    e0 = np.zeros((32, NTOK + NPAD), np.float32)
    e0[h % WS, np.arange(NTOK)] = 1
    e0[WS + w % WS, np.arange(NTOK)] = 1
    a, b = np.divmod(np.arange(NPAD), WS)
    e0[a, NTOK + np.arange(NPAD)] = 1
    e0[WS + b, NTOK + np.arange(NPAD)] = 1
    for n in range(4):
        real_h, real_w = (WS if n // 2 == 0 else HH - WS), (WS if n % 2 == 0 else WW - WS)
        e0[2 * WS + n, 0:NTOK] = window != n
        e0[2 * WS + n, NTOK:] = (a < real_h) & (b < real_w)
    win = np.zeros((4, 128 + T), np.float32)
    for n in range(4):
        win[n, [32 * j + 2 * WS + n for j in range(QH)]] = 1
        win[n, 128:] = np.tile(np.where(window == n, MASKED, 0), IMGS)
    i = np.arange(128)
    k = np.arange(NTOK)
    mask = np.concatenate([np.where(k[None, :] > i[:, None], MASKED, 0),
                           np.where(k[None, :] > i[:, None] + 128, MASKED, 0),
                           np.where(i[:, None] > i[None, :], MASKED, 0)], 1).astype(np.float32)
    c = np.arange(CH) // 6
    return {"e0": np.tile(e0, (QH, 1)), "e1": np.tile(e1, (QH, 1)), "win": win, "mask": mask,
            "ident": np.eye(128, dtype=np.float32),
            "ggrp": np.where(c[:, None] == c[None, :], 1 / 6, 0).astype(np.float32)}


def kernel(**inputs):
    import concourse.bacc as bacc
    from concourse.bass_utils import run_bass_kernel_spmd as run

    i = {n: np.asarray(z) for n, z in inputs.items()}
    a = constants()
    a["x"] = i["x"].reshape(B * NTOK, D)
    l0 = attention_weights(i["L0_conv_qkv_w"], i["L0_conv_qkv_b"], i["L0_conv_proj_w"], i["L0_conv_proj_b"], L0.scale)
    l1 = attention_weights(i["L1_conv_w_qkv"], i["L1_conv_b_qkv"], i["L1_conv_w_proj"], i["L1_conv_b_proj"], L1.scale)
    perm = np.r_[D:2 * D, 0:D, 2 * D:3 * D]
    l2 = attention_weights(i["L2_attn_W_kqv"][:, perm], i["L2_attn_b_kqv"][perm], i["L2_attn_W_proj"],
                           i["L2_attn_b_proj"], L2.scale)
    l3 = attention_weights(i["L3_attn_w_qkv"], None, i["L3_attn_w_out"], i["L3_attn_b_out"], L3.scale)
    w1t = i["L3_ffn_w1"].T
    l4 = attention_weights(w1t[:, MLP:], i["L3_ffn_b1"][MLP:], None, None, L4.scale)
    a["lw"] = np.stack([l0, l1, l2], 1).reshape(CH + 1, -1)
    a["lw2"] = np.stack([l3, l4], 1)
    a["relw"] = np.concatenate([rel_weights(i["L0_conv_rel_pos_h"], i["L0_conv_rel_pos_w"], WS),
                                rel_weights(i["L1_conv_rel_pos_h"], i["L1_conv_rel_pos_w"], HH)], 1)
    a["fc1"] = by_chunk(i["L0_conv_fc1_w"], i["L0_conv_fc1_b"])
    a["fc2"] = i["L0_conv_fc2_w"].reshape(MLP // 128, 128, D).transpose(1, 0, 2)
    a["fc2b"] = i["L0_conv_fc2_b"].reshape(1, D)
    cols = np.zeros((CH + 1, 2, 4), np.float32)
    cols[CH, :, 0::2] = 1
    for n, name in enumerate(("norm1_w", "norm1_b", "norm2_w", "norm2_b")):
        cols[0:CH, :, n] = i["L0_conv_" + name].reshape(2, CH).T
    a["cols"] = cols
    kpad = np.zeros((QUADS, QH, 32, NPAD), np.float32)
    kpad[:, :, 0:HD] = i["L0_conv_qkv_b"][D:2 * D].reshape(QUADS, QH, HD, 1)
    kpad[:, :, MROW] = 1 / L0.scale
    a["kpad"] = kpad.reshape(QUADS, 128, NPAD).transpose(1, 0, 2)
    vpad = np.ones((98, HEADS, VW), np.float32)
    vpad[:, :, 0:HD] = i["L0_conv_qkv_b"][2 * D:].reshape(1, HEADS, HD)
    a["vpad"] = vpad
    a["rout"] = np.concatenate([by_chunk(i["L2_ffn_router_w"].T), by_chunk(i["L3_ffn_w_router"].T)], 2)
    a["moe1"] = i["L2_ffn_w1"].transpose(2, 0, 1).reshape(2, CH, E2, I2).transpose(1, 0, 2, 3)
    a["moe2"] = i["L2_ffn_w2"].transpose(0, 2, 1).reshape(E2, 4, 128, D).transpose(2, 0, 1, 3)
    a["ffn1"] = by_chunk(w1t[:, 0:MLP], i["L3_ffn_b1"][0:MLP])
    w2t = i["L3_ffn_w2"].T.reshape(MLP + D, 2, D)
    a["ffn2"] = w2t[0:MLP].reshape(MLP // 128, 128, 2, D).transpose(1, 0, 2, 3)
    f2a = np.zeros((CH + 1, 2, 2, D), np.float32)
    f2a[0:CH] = w2t[MLP:].reshape(2, CH, 2, D).transpose(1, 0, 2, 3)
    f2a[CH, 1] = i["L3_ffn_b2"].reshape(2, D)
    a["ffn2a"] = f2a
    a["gb3"] = np.broadcast_to(np.stack([i["L3_ffn_gamma1"], i["L3_ffn_beta1"]])[None], (128, 2, D))
    a = {n: np.ascontiguousarray(z) for n, z in a.items()}

    per = {}
    for _ in range(2):
        nc = bacc.Bacc("TRN2", target_bir_lowering=False, num_devices=1)
        aps = {n: nc.dram_tensor("in_" + n, z.shape, F32, kind="ExternalInput").ap() for n, z in a.items()}
        out = nc.dram_tensor("out", (B * NTOK, D), F32, kind="ExternalOutput").ap()
        per = program(nc, aps, out, per)
    r = run(nc, [{"in_" + n: z for n, z in a.items()}], core_ids=[0])
    return r.results[0]["out"].reshape(B, HH, WW, D)
```

```python
from contextlib import ExitStack

import numpy as np
import concourse.bass as bass
from concourse import mybir

F32 = mybir.dt.float32
BF16 = mybir.dt.bfloat16
ALU = mybir.AluOpType
ACT = mybir.ActivationFunctionType
AX = mybir.AxisListType

B, HH, WW, D = 8, 16, 16, 192
NTOK = HH * WW
HEADS, HD = 12, 16
QUADS, QH = 3, 4
IMGS = 2
TURNS = B // IMGS
T = IMGS * NTOK
TT = T // 128
CH = 96
WS = 14
NPAD = WS * WS
RR = 16
INNER = WS * WS
EDGE = NTOK - INNER
HALF0 = INNER // 2
EB = 2 * WS
MLP = 4 * D
NM = MLP // 128
E2, I2 = 8, 512
E3 = 4
CAP = NTOK // 2
SEGS = [(0, 24), (24, 48), (48, 96), (96, 192)]
MASKED = -1e30
VW = HD + 1
WL = 2 * QUADS * 128 + 2 * D


class Attn:

    def __init__(self, name, scale, rel=0, pad=False, causal=False):
        self.name, self.scale, self.rel, self.pad, self.causal = name, scale, rel, pad, causal
        self.tiles = [(h, e) for h in range(HEADS) for e in range(2)] if pad else [(h, 0) for h in range(HEADS)]
        self.ring = 2 if pad else 3


L0 = Attn("l0", HD ** -0.5, rel=WS, pad=True)
L1 = Attn("l1", HD ** -0.5, rel=HH)
L2 = Attn("l2", HD ** -0.5, causal=True)
L3 = Attn("l3", D ** -0.5)
L4 = Attn("l4", HD ** -0.5)


class Signals:

    def __init__(self, nc, ctx, loop, names, per):
        self.sem = {n: ctx.enter_context(nc.semaphore(f"{loop}_{n}")) for n in names}
        self.per = {n: per.get(n, 1) for n in names}
        self.made = dict.fromkeys(names, 0)


class Port:

    def __init__(self, signals, turn):
        self.s, self.turn = signals, turn
        self.seen = dict.fromkeys(signals.sem, 0)
        self.base = dict(self.seen)

    def next(self, name, n=1):
        self.seen[name] += n
        return self.s.sem[name], self.turn * self.s.per[name] + self.seen[name]

    def passed(self, name, n):
        self.seen[name] += n

    def mark(self):
        self.base = dict(self.seen)

    def behind(self, name, n):
        return self.base[name] + n > self.seen[name]

    def to(self, name, n):
        return self.next(name, self.base[name] + n - self.seen[name])

    def ended(self, names, n):
        for name in names:
            self.seen[name] = self.base[name] + n

    def adds(self, name):
        self.s.made[name] += 1
        return self.s.sem[name], 1

    def own(self, name):
        self.seen[name] += 1
        return self.s.sem[name], self.seen[name]


NAMES = ["dve_step", "pool_step", "var_ready", "rstd_ready", "rows_ready", "turned", "xt0_ready",
         "xt1_ready", "q01_mm", "q2k0_mm", "k12_mm", "v_mm", "q01_ready", "q2k0_ready", "k12_ready", "v_ready", "rel_mm",
         "rel0_ready", "rel1_ready", "edge_ready", "sc_mm", "max_done", "exp_done", "pt_mm", "pt_done", "pv_mm",
         "at_ready", "proj_mm", "fc1_mm", "h_ready", "fc2_mm", "acc_done", "stat_ready", "stat_mm", "gate_mm",
         "gate_in", "gate_exp", "prow_in", "prow_mm", "turn_end", "waited"]


def slot(steps, attend, side, hops):
    at = 0
    for i in range(steps):
        attend(i)
        while at < hops and at * steps < (i + 1) * hops:
            next(side, None)
            at += 1
    for _ in side:
        pass


def image(z):
    return z.rearrange("p (h w) -> p h w", h=HH)


def by_window(z, packed):
    parts = [(slice(0, WS), slice(0, WS), 0), (slice(0, WS), slice(WS, WW), INNER),
             (slice(WS, HH), slice(0, WW), INNER + EB)]
    out = []
    for hs, ws, at in parts:
        n = (hs.stop - hs.start) * (ws.stop - ws.start)
        if len(z.shape) == 2:
            out.append((z.rearrange("p (h w) -> p h w", h=HH)[:, hs, ws],
                        packed[:, at:at + n].rearrange("p (h w) -> p h w", h=hs.stop - hs.start)))
        else:
            out.append((z.rearrange("p s (h w) -> p s h w", h=HH)[:, :, hs, ws],
                        packed[:, :, at:at + n].rearrange("p s (h w) -> p s h w", h=hs.stop - hs.start)))
    return out


def program(nc, a, out, per):
    with ExitStack() as ctx:
        def sb(name, *shape, dt=F32):
            return ctx.enter_context(nc.sbuf_tensor(name, list(shape), dt))

        def sem(name):
            return ctx.enter_context(nc.semaphore(name))

        xall = sb("xall", 128, TURNS * TT, D)
        x = sb("x", 128, TT, D + 1)
        xn = sb("xn", 128, TT, D + 1)
        att = sb("att", 128, 3, D + 1)
        xt = sb("xt", CH + 1, 2, T)
        xp = sb("xp", CH + 1, 2, NTOK)
        qn = sb("qn", 128, QUADS, NTOK)
        qt = sb("qt", 128, IMGS, QUADS, NTOK)
        kz = sb("kz", 128, IMGS, 2, QUADS, NTOK)
        relt = sb("relt", 128, IMGS, QUADS, NTOK)
        ke = sb("ke", 128, IMGS, 2, QUADS, EDGE)
        negmax = sb("negmax", 128, 3, 2)
        v = sb("v", 128, IMGS, 3, HEADS, VW)
        p = sb("p", 128, 3, 512)
        pt = sb("pt", 128, 3, 512)
        pall = sb("pall", 128, TURNS * TT, E2)
        stats = sb("stats", 128, TT, 6)
        mv = sb("mv", 128, TT, 2)
        ve = sb("ve", 128, 4)
        rstd = sb("rstd", 128, 4)
        nhalf = sb("nhalf", 128, 4)
        gsc = sb("gsc", CH + 1, 2)
        gbi = sb("gbi", CH + 1, 2)
        gst = sb("gst", CH, 2, 2)
        rsum = sb("rsum", 128, 3, HEADS)
        gl = sb("gl", 128, TT, E2)
        ge = sb("ge", 128, TT, E2)
        gm = sb("gm", 128, TT)
        gs = sb("gs", 128, TT)
        oh = sb("oh", 128, 3, TT, E2)
        cw = sb("cw", 128, TT, E2)
        imp = sb("imp", 128, E2)
        rrun = sb("rrun", 128, E2)
        p4 = sb("p4", 128, 2, E3)
        prow = sb("prow", E3, NTOK)
        left = sb("left", E3, NTOK)
        srow = sb("srow", E3, NTOK)
        top8 = sb("top8", E3, 8)
        sel = sb("sel", 128, 2, E3)
        gate = sb("gate", 128, IMGS, 2, E3)
        ones = sb("ones", 128, 128)
        order = sb("order", 128, E2)
        tri16 = sb("tri16", 128, 128, dt=BF16)
        ident16 = sb("ident16", 128, 128, dt=BF16)

        zone = sb("zone", 128, 4248)
        hid = zone[:, 0:NM * NTOK].rearrange("p (m t) -> p m t", m=NM)
        hids = [hid, relt[:, :, :, :].rearrange("p i s t -> p (i s) t")]
        z0 = NM * NTOK
        kpadz = zone[:, z0:z0 + 6 * NPAD].rearrange("p (c s k) -> p c s k", c=2, s=QUADS)
        hid2 = zone[:, 0:8 * T].rearrange("p (m t) -> p m t", m=8)
        lx = zone[:, z0:z0 + 772].rearrange("p (i d) -> p i d", i=TT)
        xg = zone[:, z0 + 772:z0 + 1544].rearrange("p (i d) -> p i d", i=TT)
        yb = zone[:, z0 + 1544:z0 + 2312].rearrange("p (i d) -> p i d", i=TT)

        lw = sb("lw", 128, 3 * 2 * WL)
        lw2 = sb("lw2", CH + 1, 2, 2, WL)
        wts = {n: lw[0:CH + 1, i * 2 * WL:(i + 1) * 2 * WL].rearrange("p (c n) -> p c n", c=2)
               for i, n in enumerate(("l0", "l1", "l2"))}
        wts |= {"l3": lw2[:, 0], "l4": lw2[:, 1]}
        moe2 = lw[:, 0:E2 * 4 * D].rearrange("p (e k n) -> p e k n", e=E2, k=4)
        rw = sb("rw", 128, 2 * E2 * I2)
        n0, n1 = 2 * WS * QH * RR, 2 * HH * QH * RR
        relw = {"l0": rw[:, 0:n0].rearrange("p (a h n) -> p a h n", a=2, h=WS),
                "l1": rw[:, n0:n0 + n1].rearrange("p (a h n) -> p a h n", a=2, h=HH)}
        ez0, ez1, eze = (rw[:, n0 + n1 + i * QH * NTOK:n0 + n1 + (i + 1) * QH * NTOK]
                         .rearrange("p (c k) -> p c k", c=QH) for i in range(3))
        moe1 = rw[0:CH, :].rearrange("p (c e i) -> p c e i", c=2, e=E2)
        fc1 = sb("fc1", CH + 1, 2, MLP)
        fc2 = sb("fc2", 128, NM, D)
        ffn1 = sb("ffn1", CH + 1, 2, MLP)
        ffn2 = sb("ffn2", 128, NM, 2, D)
        ffn2a = sb("ffn2a", CH + 1, 2, 2, D)
        cols = sb("cols", CH + 1, 2, 4)
        gb3 = sb("gb3", 128, 2, D)
        ident = sb("ident", 128, 128)
        par = sb("par", 128, 2, 2)
        vpad = sb("vpad", 98, HEADS, VW)
        winrow = sb("winrow", 128, EDGE)
        tri = sb("tri", 128, 128)
        fc2b = sb("fc2b", 1, D)
        ggrp = sb("ggrp", CH, CH)
        rout = sb("rout", CH, 2, E2 + E3)
        ps = ctx.enter_context(nc.psum_tensor("ps", [128, 8, 512], F32))

        ld_x, ld_a, ld_b, ld_moe = sem("ld_x"), sem("ld_a"), sem("ld_b"), sem("ld_moe")
        set_up, const_ready, set_b, ffn2_summed = sem("set_up"), sem("const_ready"), sem("set_b"), sem("ffn2_summed")
        imp_in, imp_mm, imp_step, imp_done, stored = (sem("imp_in"), sem("imp_mm"), sem("imp_step"),
                                                      sem("imp_done"), sem("stored"))
        sa = Signals(nc, ctx, "a", NAMES, per.get("a", {}))
        sm = Signals(nc, ctx, "m", ["dve_step", "var_ready", "rstd_ready", "rows_ready", "turned", "xt0_ready",
                                    "xt1_ready", "fc1_mm", "h_ready", "fc2_mm", "acc_done", "turn_end", "waited"],
                     per.get("m", {}))
        sbb = Signals(nc, ctx, "b", NAMES, per.get("b", {}))

        loads_a = [(lw[0:CH + 1, :], a["lw"]), (rw[:, 0:n0 + n1], a["relw"]), (fc1[:, :, :], a["fc1"]),
                   (fc2[:, :, :], a["fc2"]), (cols[:, :, :], a["cols"]), (ident[:, :], a["ident"]),
                   (ez0, a["ez0"]), (ez1, a["ez1"]), (eze, a["eze"]), (kpadz, a["kpadz"]), (par[:, :, :], a["par"]),
                   (vpad[:, :, :], a["vpad"]), (winrow[:, :], a["winrow"]), (tri[:, :], a["tri"]),
                   (fc2b[:, :], a["fc2b"]), (ggrp[:, :], a["ggrp"]), (rout[:, :, :], a["rout"])]
        loads_b = [(lw2[:, :, :, :], a["lw2"]), (ffn1[:, :, :], a["ffn1"]), (ffn2[:, :, :, :], a["ffn2"]),
                   (ffn2a[:, :, :, :], a["ffn2a"]), (gb3[:, :, :], a["gb3"])]

        def turn_x(t):
            return xall[:, bass.ds(t * TT, TT), :]

        def image_x(t, im):
            return xall[:, bass.ds(t * TT + im * 2, 2), :]

        block = ctx.enter_context(nc.Block())

        @block.sync
        def _(sp):
            sp.dma_start(xall[:, :, :], a["x"].rearrange("(t p) d -> p t d", p=128)).then_inc(ld_x, 16)
            for dst, src in loads_a:
                sp.dma_start(dst, src).then_inc(ld_a, 16)
            for dst, src in loads_b:
                sp.dma_start(dst, src).then_inc(ld_b, 16)
            sp.wait_ge(sa.sem["turn_end"], TURNS * IMGS)
            sp.dma_start(moe1, a["moe1"]).then_inc(ld_moe, 16)
            sp.dma_start(moe2, a["moe2"]).then_inc(ld_moe, 16)
            with sp.Fori(0, TURNS) as t:
                sp.wait_ge(sbb.sem["turn_end"], (t + 1) * IMGS)
                sp.dma_start(out.rearrange("(t p) d -> p t d", p=128)[:, bass.ds(t * TT, TT), :],
                             turn_x(t)).then_inc(stored, 16)
            sp.wait_ge(stored, 16 * TURNS)

        @block.tensor
        def _(pe):
            def mm(o, w, m, start=True, stop=True):
                return pe.matmul(o, w, m, start=start, stop=stop)

            def turn_over(q, tiles):
                for c in range(2):
                    n = CH + c
                    at = 0
                    for z in tiles:
                        m = z.shape[0]
                        last = pe.transpose(ps[0:n, 6 + c, at:at + m], z[:, c * CH:c * CH + n], ident[0:m, 0:m])
                        at += m
                    last.then_inc(*q.adds("turned"))

            def rows(z, im):
                return [z[:, 2 * im + i, :] for i in range(2)]

            def att_rows(l):
                return [att[0:HALF0, 0, :], att[0:HALF0, 1, :], att[0:EDGE, 2, :]] if l.pad else \
                    [att[:, i, :] for i in range(2)]

            def wait_xt(q):
                pe.wait_ge(*q.next("xt0_ready"))
                pe.wait_ge(*q.next("xt1_ready"))

            def qkv(q, l, im):
                w = wts[l.name]
                xi = xt[:, :, im * NTOK:(im + 1) * NTOK]

                def quad(s, bank, at):
                    for c in range(2):
                        last = mm(ps[:, bank, at:at + NTOK], w[:, c, s * 128:(s + 1) * 128], xi[:, c, :],
                                  c == 0, c == 1)
                    return last
                wait_xt(q)
                quad(0, 6, 0)
                quad(1, 6, NTOK).then_inc(*q.adds("q01_mm"))
                quad(2, 7, 0)
                quad(3, 7, NTOK).then_inc(*q.adds("q2k0_mm"))
                yield
                pe.wait_ge(*q.next("q01_ready"))
                quad(4, 6, 0)
                quad(5, 6, NTOK).then_inc(*q.adds("k12_mm"))
                pe.wait_ge(*q.next("q2k0_ready"))
                if l.pad:
                    tiles = [xp[:, c, at:min(at + HALF0, NTOK)] for at in range(0, NTOK, HALF0) for c in range(2)]
                else:
                    tiles = [xi[:, c, i * 128:(i + 1) * 128] for i in range(2) for c in range(2)]
                for i in range(2):
                    for c in range(2):
                        z = tiles[2 * i + c]
                        m = HALF0 if l.pad else 128
                        last = mm(ps[0:m, 7, i * D:(i + 1) * D], z, w[:, c, 768:768 + D], c == 0, c == 1)
                last.then_inc(*q.adds("v_mm"))
                yield
                pe.wait_ge(*q.next("k12_ready"))
                pe.wait_ge(*q.next("v_ready"))
                if l.pad:
                    pe.sem_inc(*q.adds("waited"))
                    for c in range(2):
                        last = mm(ps[0:EDGE, 6, 0:D], tiles[4 + c], w[:, c, 768:768 + D], c == 0, c == 1)
                    last.then_inc(*q.adds("v_mm"))
                    yield
                    pe.wait_ge(*q.next("v_ready"))
                if l.rel:
                    rwt = relw[l.name]
                    qi = (qn if l.pad else qt[:, im]).rearrange("p s (h w) -> p s h w", h=HH)
                    for half in range(2):
                        oh_, ow = (ps[64 * a:64 * a + 64, 6 + half, 0:QUADS * 128] for a in range(2))
                        oh_ = oh_.rearrange("p (s h w) -> p s h w", s=QUADS, h=8)
                        ow = ow.rearrange("p (s h w) -> p s h w", s=QUADS, h=HH)
                        for k in range(8):
                            at = 8 * half + k
                            pe.matmul(oh_[:, :, k, :], rwt[:, 0, at % l.rel, :], qi[:, :, at, :],
                                      start=k == 0, stop=True, skip_group_check=True)
                        for k in range(8):
                            at = 8 * half + k
                            last = pe.matmul(ow[:, :, :, k], rwt[:, 1, at % l.rel, :], qi[:, :, :, at],
                                             start=k == 0, stop=True, skip_group_check=True)
                        last.then_inc(*q.adds("rel_mm"))
                    yield

            def attention(q, l, im):
                n = len(l.tiles)
                ez = ez0 if l.pad else ez1

                def where(head):
                    j = head % QH
                    return slice(64 * (j // 2), 64 * (j // 2) + 64), head // QH, j % 2

                def scores(i):
                    head, edge = l.tiles[i]
                    r, s, c = where(head)
                    if i >= l.ring:
                        if q.behind("exp_done", i - l.ring + 1):
                            pe.wait_ge(*q.to("exp_done", i - l.ring + 1))
                    bank = ps[:, i % l.ring, :]
                    rl, qi, ki, j = relt[:, im, s, :], qt[r, im, s, :], kz[r, im, c, s, :], head % QH
                    if edge:
                        pe.sem_inc(*q.adds("waited"))
                        o = bank[0:EDGE, :]
                        mm(o[:, 0:EDGE], qi[:, INNER:], ke[r, im, c, s, :], True, False)
                        mm(o[:, 0:EDGE], rl[:, INNER:], eze[:, j, 0:EDGE], False, True)
                        mm(o[:, EDGE:NTOK], qi[:, INNER:], kpadz[r, c, s, :], True, False)
                        last = mm(o[:, EDGE:NTOK], rl[:, INNER:], eze[:, j, EDGE:NTOK], False, True)
                    elif l.pad:
                        for half in range(2):
                            o = bank[0:HALF0, half * INNER:(half + 1) * INNER]
                            hs = slice(HALF0 * half, HALF0 * half + HALF0)
                            mm(o, qi[:, hs], image(ki)[:, 0:WS, 0:WS], True, False)
                            last = mm(o, rl[:, hs], image(ez[:, j, :])[:, 0:WS, 0:WS], False, True)
                    elif l.causal:
                        mm(bank[:, 0:NTOK], qi[:, 128:256], ki, True, False)
                        mm(bank[:, 128:256], ident16[:, :], tri16[:, :], False, True)
                        mm(bank[:, NTOK:NTOK + 128], qi[:, 0:128], ki[:, 0:128], True, False)
                        last = mm(bank[:, NTOK:NTOK + 128], ident16[:, :], tri16[:, :], False, True)
                    else:
                        for half in range(2):
                            o = bank[:, half * NTOK:(half + 1) * NTOK]
                            hs = slice(128 * half, 128 * half + 128)
                            last = mm(o, qi[:, hs], ki, True, not l.rel)
                            if l.rel:
                                last = mm(o, rl[:, hs], ez[:, j, :], False, True)
                    last.then_inc(*q.adds("sc_mm"))

                def blocks(i):
                    head, edge = l.tiles[i]
                    if edge:
                        return [(EDGE, 0, 0, EDGE, 2, v[0:EDGE, im, 2, head, :]),
                                (EDGE, EDGE, EDGE, 98, 2, vpad[:, head, :]),
                                (EDGE, EDGE + 98, 2 * EDGE, 98, 2, vpad[:, head, :])]
                    if l.causal:
                        return [(128, NTOK, NTOK, 128, 0, v[:, im, 0, head, :]),
                                (128, 0, 0, 128, 1, v[:, im, 0, head, :]),
                                (128, 128, 128, 128, 1, v[:, im, 1, head, :])]
                    m = HALF0 if l.pad else 128
                    return [(m, (2 * half + k) * m, (2 * half + k) * m, m, half, v[0:m, im, k, head, :])
                            for half in range(2) for k in range(2)]

                def turn_p(i):
                    if q.behind("exp_done", i + 1):
                        pe.wait_ge(*q.to("exp_done", i + 1))
                    if i >= 2:
                        if q.behind("pt_done", i - 1):
                            pe.wait_ge(*q.to("pt_done", i - 1))
                    if l.tiles[i][1]:
                        pe.sem_inc(*q.adds("waited"))
                    for m, at, to, nk, _, _ in blocks(i):
                        last = pe.transpose(ps[0:nk, 3 + i % 2, to:to + m], p[0:m, i % 3, at:at + nk],
                                            ident[0:m, 0:m])
                    last.then_inc(*q.adds("pt_mm"))

                def values(i):
                    head, edge = l.tiles[i]
                    if q.behind("pt_done", i + 1):
                        pe.wait_ge(*q.to("pt_done", i + 1))
                    if edge:
                        pe.sem_inc(*q.adds("waited"))
                    bl = blocks(i)
                    for n_, (m, _, to, nk, tile, vv) in enumerate(bl):
                        at = (tile % 2 * HEADS + head) * VW
                        o = ps[0:m, 2 if tile == 2 else 5, at:at + VW]
                        last = mm(o, pt[0:nk, i % 3, to:to + m], vv, n_ == 0 or bl[n_ - 1][4] != tile,
                                  n_ == len(bl) - 1 or bl[n_ + 1][4] != tile)
                    last.then_inc(*q.adds("pv_mm"))

                def step(i):
                    if i == 0:
                        if l.pad:
                            pe.wait_ge(*q.next("rel0_ready"))
                            pe.wait_ge(*q.next("rel1_ready"))
                            pe.wait_ge(*q.next("edge_ready"))
                        elif l.rel:
                            pe.wait_ge(*q.next("rel0_ready"))
                            pe.wait_ge(*q.next("rel1_ready"))
                        q.mark()
                    if i < n:
                        scores(i)
                    if 2 <= i < n + 2:
                        turn_p(i - 2)
                    if 3 <= i:
                        values(i - 3)
                    if i == n + 2:
                        q.ended(("exp_done", "pt_done"), n)
                return step

            def run(q, l, im, side, hops):
                slot(len(l.tiles) + 3, attention(q, l, im), side, hops)

            def project(q, l, im):
                pe.wait_ge(*q.next("at_ready"))
                turn_over(q, att_rows(l))
                yield
                wait_xt(q)
                w = wts[l.name]
                for i in range(2):
                    t0 = im * NTOK + i * 128
                    for c in range(2):
                        last = mm(ps[:, 6, i * D:(i + 1) * D], xt[:, c, t0:t0 + 128], w[:, c, 768 + D:768 + 2 * D],
                                  c == 0, c == 1)
                last.then_inc(*q.adds("proj_mm"))
                yield

            def hidden(q, w, im):
                wait_xt(q)
                for m in range(NM):
                    if m >= 4 and m % 2 == 0:
                        pe.wait_ge(*q.next("h_ready"))
                    for c in range(2):
                        last = mm(ps[:, 6 + m // 2 % 2, m % 2 * NTOK:(m % 2 + 1) * NTOK],
                                  w[:, c, m * 128:(m + 1) * 128], xt[:, c, im * NTOK:(im + 1) * NTOK], c == 0, c == 1)
                    if m % 2:
                        last.then_inc(*q.adds("fc1_mm"))
                yield
                pe.wait_ge(*q.next("h_ready", 2))

            def gate_logits(q, w, im):
                n = w.shape[2]
                wait_xt(q)
                for i in range(2):
                    t0 = im * NTOK + i * 128
                    for c in range(2):
                        last = mm(ps[:, 6, i * n:(i + 1) * n], xt[0:CH, c, t0:t0 + 128], w[:, c, :], c == 0, c == 1)
                last.then_inc(*q.adds("gate_mm"))
                yield

            def side_a0(q, im):
                pe.wait_ge(*q.next("rows_ready"))
                turn_over(q, rows(xn, im))
                yield
                yield from qkv(q, L0, im)

            def side_a1(q, im):
                yield from project(q, L0, im)
                pe.wait_ge(*q.next("rows_ready"))
                turn_over(q, rows(xn, im))
                yield
                yield from hidden(q, fc1, im)
                for i in range(2):
                    o = ps[:, 6, i * D:(i + 1) * D]
                    mm(o, ones[0:1, :], fc2b[:, :], True, False)
                    for m in range(NM):
                        last = mm(o, hid[:, m, i * 128:(i + 1) * 128], fc2[:, m, :], False, m == NM - 1)
                last.then_inc(*q.adds("fc2_mm"))
                yield
                pe.wait_ge(*q.next("rows_ready"))
                turn_over(q, rows(x, im))
                yield
                pe.wait_ge(*q.next("stat_ready"))
                mm(ps[0:CH, 6, NTOK:NTOK + 2], ggrp[:, :], gst[:, 0, :]).then_inc(*q.adds("stat_mm"))
                yield
                pe.wait_ge(*q.next("stat_ready"))
                mm(ps[0:CH, 6, NTOK + 2:NTOK + 4], ggrp[:, :], gst[:, 1, :]).then_inc(*q.adds("stat_mm"))
                q.passed("stat_ready", 1)
                yield
                yield from qkv(q, L1, im)

            def side_a2(q, im):
                yield from project(q, L1, im)
                pe.wait_ge(*q.next("rows_ready"))
                turn_over(q, rows(xn, im))
                yield
                yield from qkv(q, L2, im)

            def side_a3(q, im):
                yield from project(q, L2, im)
                pe.wait_ge(*q.next("rows_ready"))
                turn_over(q, rows(xn, im))
                yield
                yield from gate_logits(q, rout[:, :, 0:E2], im)

            def side_b0(q, im):
                pe.wait_ge(*q.next("rows_ready"))
                turn_over(q, rows(xn, im))
                yield
                yield from qkv(q, L3, im)

            def side_b1(q, im):
                yield from project(q, L3, im)
                pe.wait_ge(*q.next("rows_ready"))
                turn_over(q, rows(lx, im))
                yield
                yield from gate_logits(q, rout[:, :, E2:E2 + E3], im)
                pe.wait_ge(*q.next("prow_in"))
                pe.sem_inc(*q.adds("waited"))
                for half in range(2):
                    last = pe.transpose(ps[0:E3, 6, 64 + half * 128:64 + (half + 1) * 128], p4[:, half, :],
                                        ident[:, :])
                last.then_inc(*q.adds("prow_mm"))
                for _ in range(5):
                    yield
                pe.wait_ge(*q.next("prow_in"))
                pe.sem_inc(*q.adds("waited"))
                for half in range(2):
                    last = mm(ps[:, 6, half * E3:(half + 1) * E3], srow[:, half * 128:(half + 1) * 128],
                              ident[0:E3, 0:E3])
                last.then_inc(*q.adds("prow_mm"))
                yield
                pe.wait_ge(*q.next("rows_ready"))
                turn_over(q, rows(xg, im))
                yield
                yield from hidden(q, ffn1, im)
                q.passed("xt0_ready", -1)
                q.passed("xt1_ready", -1)
                yield from qkv(q, L4, im)

            def side_b2(q, im):
                pe.wait_ge(*q.next("at_ready"))
                turn_over(q, att_rows(L4))
                yield
                wait_xt(q)
                for i in range(2):
                    o = ps[:, 6, i * D:(i + 1) * D]
                    for m in range(NM):
                        mm(o, hids[im][:, m, i * 128:(i + 1) * 128], ffn2[:, m, 0, :], m == 0, False)
                    for c in range(2):
                        t0 = im * NTOK + i * 128
                        last = mm(o, xt[:, c, t0:t0 + 128], ffn2a[:, c, 0, :], False, c == 1)
                last.then_inc(*q.adds("proj_mm"))
                yield

            pe.wait_ge(ld_a, 16 * len(loads_a))
            pe.wait_ge(set_up, 1)
            pe.wait_ge(const_ready, 1)
            with pe.Fori(0, TURNS) as t:
                q = Port(sa, t)
                for _ in side_a0(q, 0):
                    pass
                run(q, L0, 0, side_a0(q, 1), 5)
                run(q, L0, 1, side_a1(q, 0), 11)
                run(q, L1, 0, side_a1(q, 1), 11)
                run(q, L1, 1, side_a2(q, 0), 5)
                run(q, L2, 0, side_a2(q, 1), 5)
                run(q, L2, 1, side_a3(q, 0), 4)
                for _ in side_a3(q, 1):
                    pass
            pe.wait_ge(imp_in, 1)
            mm(ps[:, 0, 0:E2], ones[:, :], imp[:, :]).then_inc(imp_mm, 1)
            pe.wait_ge(ld_moe, 32)
            pe.wait_ge(imp_done, 1)
            with pe.Fori(0, TURNS) as t:
                q = Port(sm, t)
                pe.wait_ge(*q.next("rows_ready"))
                for c in range(2):
                    for i in range(TT):
                        n = CH + c
                        last = pe.transpose(ps[0:n, 6 + c, i * 128:(i + 1) * 128], xn[:, i, c * CH:c * CH + n],
                                            ident[:, :])
                    last.then_inc(*q.adds("turned"))
                wait_xt(q)

                def up(e):
                    for m in range(4):
                        if e:
                            pe.wait_ge(*q.next("h_ready"))
                        for c in range(2):
                            last = mm(ps[:, m, :], moe1[:, c, e, m * 128:(m + 1) * 128], xt[0:CH, c, :],
                                      c == 0, c == 1)
                        last.then_inc(*q.adds("fc1_mm"))

                def down(e):
                    if e + 1 == E2:
                        pe.wait_ge(*q.next("h_ready", 4))
                    if e >= 2:
                        pe.wait_ge(*q.next("acc_done"))
                    for i in range(TT):
                        o = ps[:, 4 + 2 * (e % 2) + i // 2, (i % 2) * D:(i % 2 + 1) * D]
                        for m in range(4):
                            last = mm(o, hid2[:, 4 * (e % 2) + m, i * 128:(i + 1) * 128], moe2[:, e, m, :],
                                      m == 0, m == 3)
                    last.then_inc(*q.adds("fc2_mm"))

                up(0)
                for e in range(E2):
                    if e + 1 < E2:
                        up(e + 1)
                    down(e)
                q.passed("acc_done", 2)

            pe.wait_ge(ld_b, 16 * len(loads_b))
            pe.wait_ge(ffn2_summed, 1)
            with pe.Fori(0, TURNS) as t:
                q = Port(sbb, t)
                for _ in side_b0(q, 0):
                    pass
                run(q, L3, 0, side_b0(q, 1), 3)
                run(q, L3, 1, side_b1(q, 0), 14)
                run(q, L4, 0, side_b1(q, 1), 14)
                run(q, L4, 1, side_b2(q, 0), 2)
                for _ in side_b2(q, 1):
                    pass

        @block.scalar
        def _(act):
            def xt0(q, im, w=None, l=None):
                act.wait_ge(*q.next("turned", 1))
                q.passed("turned", 1)
                dst, src = xt[0:CH, 0, im * NTOK:(im + 1) * NTOK], ps[0:CH, 6, 0:NTOK]
                sc = {} if w is None else {"scale": cols[0:CH, 0, w:w + 1], "bias": cols[0:CH, 0, w + 1:w + 2]}
                f = ACT.Copy if w is None else ACT.Identity
                if l is L0:
                    for z, pk in by_window(dst, src):
                        ins = act.activation(z, pk, f)
                else:
                    ins = act.activation(dst, src, f, **sc)
                    if w == 0:
                        for z, pk in by_window(src, xp[0:CH, 0, :]):
                            ins = act.activation(pk, z, f, **sc)
                ins.then_inc(*q.adds("xt0_ready"))

            def qkv(q, l, im):
                sc = 1 if l is L3 else 0
                act.wait_ge(*q.next("q01_mm"))
                dst = qn[:, :, :] if l.pad else qt[:, im]
                act.activation(dst[:, 0:2, :].rearrange("p s t -> p (s t)"), ps[:, 6, :], ACT.Copy).then_inc(*q.adds("q01_ready"))
                yield
                act.wait_ge(*q.next("k12_mm"))
                for c in range(2):
                    ins = act.activation(kz[:, im, c, 1:3, :].rearrange("p s t -> p (s t)"), ps[:, 6, :], ACT.Copy,
                                         scale=par[:, sc, c:c + 1])
                ins.then_inc(*q.adds("k12_ready"))
                yield
                if l.pad:
                    yield
                if l.rel:
                    for half in range(2):
                        act.wait_ge(*q.next("rel_mm"))
                        src = ps[0:64, 6 + half, 0:QUADS * 128].rearrange("p (s t) -> p s t", s=QUADS)
                        dst = relt[0:64, im, :, half * 128:(half + 1) * 128]
                        if l.pad:
                            n = 8 - 2 * half
                            src = src.rearrange("p s (h w) -> p s h w", h=8)[:, :, 0:n, 0:WS]
                            dst = relt[0:64, im, :, 8 * half * WS:(8 * half + n) * WS]
                            dst = dst.rearrange("p s (h w) -> p s h w", h=n)
                        ins = act.activation(dst, src, ACT.Copy)
                    ins.then_inc(*q.adds("rel0_ready"))
                    yield

            def attention(q, l):
                n = len(l.tiles)

                def step(i):
                    if i == 0:
                        q.mark()
                    if i < n:
                        if q.behind("max_done", i + 1):
                            act.wait_ge(*q.to("max_done", i + 1))
                        if i >= 3:
                            if q.behind("pt_mm", i - 2):
                                act.wait_ge(*q.to("pt_mm", i - 2))
                        bank = ps[:, i % l.ring, :]
                        if l.tiles[i][1]:
                            parts = [(EDGE, 0, NTOK, 0)]
                        elif l.pad:
                            parts = [(HALF0, 0, INNER, 0), (HALF0, INNER, INNER, 1)]
                        elif l.causal:
                            parts = [(128, 0, NTOK, 0), (128, NTOK, 128, 1)]
                        else:
                            parts = [(128, 0, NTOK, 0), (128, NTOK, NTOK, 1)]
                        for m, at, k, c in parts:
                            ins = act.activation(p[0:m, i % 3, at:at + k], bank[0:m, at:at + k], ACT.Exp,
                                                 bias=negmax[0:m, i % 3, c:c + 1])
                        ins.then_inc(*q.adds("exp_done"))
                    if i == n + 2:
                        q.ended(("max_done", "pt_mm"), n)
                return step

            def run(q, l, im, side, hops):
                slot(len(l.tiles) + 3, attention(q, l), side, hops)

            def hidden(q, z, func):
                for m in range(0, NM, 2):
                    act.wait_ge(*q.next("fc1_mm"))
                    act.activation(z[:, m:m + 2, :].rearrange("p m t -> p (m t)"), ps[:, 6 + m // 2 % 2, :],
                                   func).then_inc(*q.adds("h_ready"))
                yield

            def gate_exp(q, im):
                act.wait_ge(*q.next("gate_in"))
                act.activation(ge[:, 2 * im:2 * im + 2, :], gl[:, 2 * im:2 * im + 2, :], ACT.Exp).then_inc(*q.adds("gate_exp"))
                yield

            def side_a0(q, im):
                xt0(q, im, 0)
                yield
                yield from qkv(q, L0, im)

            def side_a1(q, im):
                xt0(q, im, None, L0)
                yield
                yield
                xt0(q, im, 2)
                yield
                yield from hidden(q, hid, ACT.Gelu)
                yield
                yield
                yield
                act.wait_ge(*q.next("stat_ready", 3))
                act.activation(xt[0:CH, 0, im * NTOK:(im + 1) * NTOK], ps[0:CH, 6, 0:NTOK], ACT.Identity,
                               scale=gsc[0:CH, 0:1], bias=gbi[0:CH, 0:1]).then_inc(*q.adds("xt0_ready"))
                q.passed("turned", 2)
                yield
                yield from qkv(q, L1, im)

            def side_a2(q, im):
                xt0(q, im)
                yield
                yield
                xt0(q, im)
                yield
                yield from qkv(q, L2, im)

            def side_a3(q, im):
                xt0(q, im)
                yield
                yield
                xt0(q, im)
                yield
                yield from gate_exp(q, im)

            def side_b0(q, im):
                xt0(q, im)
                yield
                yield from qkv(q, L3, im)

            def side_b1(q, im):
                xt0(q, im)
                yield
                yield
                xt0(q, im)
                yield
                yield from gate_exp(q, im)
                for _ in range(5):
                    yield
                yield
                xt0(q, im)
                yield
                yield from hidden(q, hids[im], ACT.Gelu)
                yield from qkv(q, L4, im)

            def side_b2(q, im):
                xt0(q, im)
                yield
                yield

            act.wait_ge(ld_a, 16 * len(loads_a))
            act.wait_ge(set_up, 1)
            with act.Fori(0, TURNS) as t:
                q = Port(sa, t)
                for _ in side_a0(q, 0):
                    pass
                run(q, L0, 0, side_a0(q, 1), 5)
                run(q, L0, 1, side_a1(q, 0), 11)
                run(q, L1, 0, side_a1(q, 1), 11)
                run(q, L1, 1, side_a2(q, 0), 5)
                run(q, L2, 0, side_a2(q, 1), 5)
                run(q, L2, 1, side_a3(q, 0), 4)
                for _ in side_a3(q, 1):
                    pass
            with act.Fori(0, TURNS) as t:
                q = Port(sm, t)
                act.wait_ge(*q.next("turned", 1))
                q.passed("turned", 1)
                act.activation(xt[0:CH, 0, :], ps[0:CH, 6, :], ACT.Copy).then_inc(*q.adds("xt0_ready"))
                for e in range(E2):
                    for m in range(4):
                        act.wait_ge(*q.next("fc1_mm"))
                        if e >= 2 and m == 0:
                            act.wait_ge(*q.next("fc2_mm"))
                        act.activation(hid2[:, 4 * (e % 2) + m, :], ps[:, m, :], ACT.Silu).then_inc(*q.adds("h_ready"))
                q.passed("fc2_mm", 2)
            act.wait_ge(set_b, 1)
            with act.Fori(0, TURNS) as t:
                q = Port(sbb, t)
                for _ in side_b0(q, 0):
                    pass
                run(q, L3, 0, side_b0(q, 1), 3)
                run(q, L3, 1, side_b1(q, 0), 14)
                run(q, L4, 0, side_b1(q, 1), 14)
                run(q, L4, 1, side_b2(q, 0), 2)
                for _ in side_b2(q, 1):
                    pass

        @block.gpsimd
        def _(pool):
            def rstds(q, n):
                for _ in range(n):
                    pool.wait_ge(*q.next("var_ready"))
                    pool.tensor_tensor(rstd[:, :], ve[:, :], nhalf[:, :], ALU.pow).then_inc(*q.adds("rstd_ready"))

            def pack(q, im):
                pool.wait_ge(*q.next("q01_ready"))
                pool.wait_ge(*q.next("q2k0_ready"))
                pool.sem_inc(*q.adds("waited"))
                for z, pk in by_window(qn[:, :, :], qt[:, im, :, :]):
                    pool.tensor_copy(pk, z)
                pool.wait_ge(*q.next("k12_ready"))
                pool.sem_inc(*q.adds("waited"))
                for c in range(2):
                    z = kz[:, im, c, :, :].rearrange("p s (h w) -> p s h w", h=HH)
                    pool.tensor_copy(ke[:, im, c, :, 0:EB].rearrange("p s (h w) -> p s h w", h=WS),
                                     z[:, :, 0:WS, WS:WW])
                    ins = pool.tensor_copy(ke[:, im, c, :, EB:EDGE], kz[:, im, c, :, WS * WW:NTOK])
                ins.then_inc(*q.adds("edge_ready"))

            pool.wait_ge(ld_a, 16 * len(loads_a))
            pool.wait_ge(set_up, 1)
            with pool.Fori(0, TURNS) as t:
                q = Port(sa, t)
                for im in range(IMGS):
                    rstds(q, 1)
                    pack(q, im)
                rstds(q, 2 * 2 + 1 * 2 + 1 * 2)
            with pool.Fori(0, TURNS) as t:
                rstds(Port(sm, t), 1)
            with pool.Fori(0, TURNS) as t:
                rstds(Port(sbb, t), 1 * 2 + 2 * 2)

        @block.vector
        def _(dve):
            def norm(q, tiles, src, dst, eps, signal=None):
                i0 = tiles[0]
                for i in tiles:
                    ins = dve.bn_stats(stats[:, i, :], src[:, i, 0:D])
                ins.then_inc(*q.adds("dve_step"))
                dve.wait_ge(*q.own("dve_step"))
                for i in tiles:
                    ins = dve.bn_aggr(mv[:, i, :], stats[:, i, :])
                ins.then_inc(*q.adds("dve_step"))
                dve.wait_ge(*q.own("dve_step"))
                dve.tensor_scalar(ve[:, i0:i0 + len(tiles)], mv[:, i0:i0 + len(tiles), 1], eps, None, ALU.add).then_inc(*q.adds("var_ready"))
                dve.wait_ge(*q.next("rstd_ready"))
                for i in tiles:
                    ins = dve.tensor_scalar(dst[:, i, 0:D], src[:, i, 0:D], mv[:, i, 0:1], rstd[:, i:i + 1],
                                            ALU.subtract, ALU.mult)
                if signal:
                    ins.then_inc(*q.adds(signal))
                else:
                    ins.then_inc(*q.adds("dve_step"))
                    dve.wait_ge(*q.own("dve_step"))

            def tiles_of(im):
                return [2 * im, 2 * im + 1]

            def xt1(q, im, w=None, l=None):
                dve.wait_ge(*q.next("turned", 2))
                dst, src = xt[:, 1, im * NTOK:(im + 1) * NTOK], ps[0:CH + 1, 7, 0:NTOK]

                def move(o, i):
                    if w is None:
                        return dve.tensor_copy(o, i)
                    return dve.tensor_scalar(o, i, cols[:, 1, w:w + 1], cols[:, 1, w + 1:w + 2], ALU.mult, ALU.add)
                if l is L0:
                    for z, pk in by_window(dst, src):
                        ins = move(z, pk)
                else:
                    ins = move(dst, src)
                    if w == 0:
                        for z, pk in by_window(src, xp[:, 1, :]):
                            ins = move(pk, z)
                ins.then_inc(*q.adds("xt1_ready"))

            def qkv(q, l, im):
                sc = 1 if l is L3 else 0
                dve.wait_ge(*q.next("q2k0_mm"))
                dve.tensor_copy((qn if l.pad else qt[:, im])[:, 2, :], ps[:, 7, 0:NTOK])
                for c in range(2):
                    ins = dve.tensor_scalar(kz[:, im, c, 0, :], ps[:, 7, NTOK:T], par[:, sc, c:c + 1], None, ALU.mult)
                ins.then_inc(*q.adds("q2k0_ready"))
                yield
                dve.wait_ge(*q.next("v_mm"))
                m = HALF0 if l.pad else 128
                dve.tensor_copy(v[0:m, im, 0:2, :, 0:HD],
                                ps[0:m, 7, 0:2 * D].rearrange("p (i h d) -> p i h d", i=2, h=HEADS)).then_inc(*q.adds("v_ready"))
                yield
                if l.pad:
                    dve.wait_ge(*q.next("v_mm"))
                    dve.tensor_copy(v[0:EDGE, im, 2, :, 0:HD],
                                    ps[0:EDGE, 6, 0:D].rearrange("p (h d) -> p h d", h=HEADS)).then_inc(*q.adds("v_ready"))
                    yield
                if l.rel:
                    dve.wait_ge(*q.next("rel_mm"))
                    c0, c1 = (ps[64:128, b, 0:QUADS * 128].rearrange("p (s h w) -> p s h w", s=QUADS, h=HH)
                              for b in (6, 7))
                    if not l.pad:
                        dst = relt[64:128, im, :, :].rearrange("p s (h w) -> p s h w", h=HH)
                        dve.tensor_copy(dst[:, :, :, 0:8], c0)
                        dve.wait_ge(*q.next("rel_mm"))
                        ins = dve.tensor_copy(dst[:, :, :, 8:16], c1)
                    else:
                        inner = relt[64:128, im, :, 0:INNER].rearrange("p s (h w) -> p s h w", h=WS)
                        dve.tensor_copy(inner[:, :, :, 0:8], c0[:, :, 0:WS, :])
                        dve.wait_ge(*q.next("rel_mm"))
                        dve.tensor_copy(inner[:, :, :, 8:WS], c1[:, :, 0:WS, 0:WS - 8])

                        def edge(r, z, hs, ws, below):
                            at, n, w = (INNER + EB, 2, WW) if below else (INNER, WS, 2)
                            dst = relt[r, im, :, at:at + n * w].rearrange("p s (h w) -> p s h w", h=n)[:, :, hs, ws]
                            wr = winrow[r, at - INNER:at - INNER + n * w].rearrange("p (h w) -> p h w", h=n)
                            wr = wr[:, hs, ws].unsqueeze(1).to_broadcast([64, QUADS] + list(z.shape[2:]))
                            return dve.tensor_tensor(dst, z, wr, ALU.add)
                        up, lo = slice(64, 128), slice(0, 64)
                        edge(up, c0[:, :, WS:, :], slice(0, 2), slice(0, 8), True)
                        edge(up, c1[:, :, WS:, :], slice(0, 2), slice(8, 16), True)
                        edge(up, c1[:, :, 0:WS, WS - 8:], slice(0, WS), slice(0, 2), False)
                        dve.wait_ge(*q.next("rel0_ready"))
                        r0, r1 = (ps[lo, b, 0:QUADS * 128].rearrange("p (s h w) -> p s h w", s=QUADS, h=8)
                                  for b in (6, 7))
                        edge(lo, r0[:, :, :, WS:], slice(0, 8), slice(0, 2), False)
                        edge(lo, r1[:, :, 0:6, WS:], slice(8, WS), slice(0, 2), False)
                        ins = edge(lo, r1[:, :, 6:8, :], slice(0, 2), slice(0, WW), True)
                    ins.then_inc(*q.adds("rel1_ready"))
                    yield

            def attention(q, l):
                n = len(l.tiles)

                def row_max(i):
                    if q.behind("sc_mm", i + 1):
                        dve.wait_ge(*q.to("sc_mm", i + 1))
                    bank = ps[:, i % l.ring, :]
                    if l.tiles[i][1]:
                        parts = [(EDGE, bank[0:EDGE, 0:NTOK], 0, 1)]
                    elif l.pad:
                        parts = [(HALF0, bank[0:HALF0, 0:2 * INNER].rearrange("p (h k) -> p h k", h=2), 0, 2)]
                    elif l.causal:
                        parts = [(128, bank[:, 0:NTOK], 0, 1), (128, bank[:, NTOK:NTOK + 128], 1, 1)]
                    else:
                        parts = [(128, bank.rearrange("p (h k) -> p h k", h=2), 0, 2)]
                    for m, z, c, k in parts:
                        ins = dve.tensor_reduce(negmax[0:m, i % 3, c:c + k], z, AX.X, ALU.max, negate=True)
                    ins.then_inc(*q.adds("max_done"))

                def keep_turned(i):
                    if q.behind("pt_mm", i + 1):
                        dve.wait_ge(*q.to("pt_mm", i + 1))
                    if i >= 3:
                        if q.behind("pv_mm", i - 2):
                            dve.wait_ge(*q.to("pv_mm", i - 2))
                    bank = ps[:, 3 + i % 2, :]
                    if l.tiles[i][1]:
                        dve.tensor_copy(pt[0:EDGE, i % 3, 0:EDGE], bank[0:EDGE, 0:EDGE])
                        ins = dve.tensor_copy(pt[0:98, i % 3, EDGE:3 * EDGE], bank[0:98, EDGE:3 * EDGE])
                    else:
                        m, k = (HALF0, 4 * HALF0) if l.pad else (128, NTOK + 128 if l.causal else T)
                        ins = dve.tensor_copy(pt[0:m, i % 3, 0:k], bank[0:m, 0:k])
                    ins.then_inc(*q.adds("pt_done"))

                def divide():
                    if q.behind("pv_mm", n):
                        dve.wait_ge(*q.to("pv_mm", n))
                    m = HALF0 if l.pad else 128
                    todo = [(m, ps[0:m, 5, 0:2 * HEADS * VW].rearrange("p (f h d) -> p f h d", f=2, h=HEADS), 0, 2)]
                    if l.pad:
                        todo.append((EDGE, ps[0:EDGE, 2, 0:HEADS * VW].rearrange("p (f h d) -> p f h d", f=1,
                                                                                 h=HEADS), 2, 1))
                    for m, o, f, k in todo:
                        ins = dve.reciprocal(rsum[0:m, f:f + k, :], o[:, :, :, HD])
                    ins.then_inc(*q.adds("dve_step"))
                    dve.wait_ge(*q.own("dve_step"))
                    for m, o, f, k in todo:
                        r = rsum[0:m, f:f + k, :].unsqueeze(3).to_broadcast([m, k, HEADS, HD])
                        ins = dve.tensor_tensor(att[0:m, f:f + k, 0:D].rearrange("p f (h d) -> p f h d", h=HEADS),
                                                o[:, :, :, 0:HD], r, ALU.mult)
                    ins.then_inc(*q.adds("at_ready"))

                def step(i):
                    if i == 0:
                        q.mark()
                    if i < n:
                        row_max(i)
                    if 2 <= i < n + 2:
                        keep_turned(i - 2)
                    if i == n + 2:
                        divide()
                        q.ended(("sc_mm", "pt_mm", "pv_mm"), n)
                return step

            def run(q, l, im, side, hops):
                slot(len(l.tiles) + 3, attention(q, l), side, hops)

            def residual(q, name, im):
                dve.wait_ge(*q.next(name))
                dst = x[:, 2 * im:2 * im + 2, 0:D]
                return dve.tensor_tensor(dst, ps[:, 6, 0:2 * D].rearrange("p (i d) -> p i d", i=2), dst, ALU.add)

            def probabilities(q, n, im):
                i2 = slice(2 * im, 2 * im + 2)
                dve.wait_ge(*q.next("gate_mm"))
                lg = ps[:, 6, 0:2 * n].rearrange("p (i e) -> p i e", i=2)
                dve.tensor_reduce(gm[:, i2], lg, AX.X, ALU.max).then_inc(*q.adds("dve_step"))
                dve.wait_ge(*q.own("dve_step"))
                dve.tensor_tensor(gl[:, i2, 0:n], lg, gm[:, i2].unsqueeze(2).to_broadcast([128, 2, n]),
                                  ALU.subtract).then_inc(*q.adds("gate_in"))
                dve.wait_ge(*q.next("gate_exp"))
                dve.tensor_reduce(gs[:, i2], ge[:, i2, 0:n], AX.X, ALU.add).then_inc(*q.adds("dve_step"))
                dve.wait_ge(*q.own("dve_step"))
                dve.reciprocal(gs[:, i2], gs[:, i2]).then_inc(*q.adds("dve_step"))
                dve.wait_ge(*q.own("dve_step"))
                return gs[:, i2].unsqueeze(2).to_broadcast([128, 2, n])

            def side_a0(q, im):
                dve.sem_inc(*q.adds("waited"))
                dve.tensor_copy(x[:, 2 * im:2 * im + 2, 0:D], image_x(q.turn, im)).then_inc(*q.adds("dve_step"))
                dve.wait_ge(*q.own("dve_step"))
                norm(q, tiles_of(im), x, xn, 1e-5, "rows_ready")
                xt1(q, im, 0)
                yield
                yield from qkv(q, L0, im)

            def side_a1(q, im):
                xt1(q, im, None, L0)
                yield
                residual(q, "proj_mm", im).then_inc(*q.adds("dve_step"))
                dve.wait_ge(*q.own("dve_step"))
                norm(q, tiles_of(im), x, xn, 1e-5, "rows_ready")
                yield
                xt1(q, im, 2)
                yield
                yield
                residual(q, "fc2_mm", im).then_inc(*q.adds("rows_ready"))
                yield
                dve.wait_ge(*q.next("turned", 2))
                for c in range(2):
                    ins = dve.bn_stats(stats[0:CH, c, :], ps[0:CH, 6 + c, 0:NTOK])
                ins.then_inc(*q.adds("dve_step"))
                dve.wait_ge(*q.own("dve_step"))
                for c in range(2):
                    ins = dve.bn_aggr(mv[0:CH, c, :], stats[0:CH, c, :])
                ins.then_inc(*q.adds("dve_step"))
                dve.wait_ge(*q.own("dve_step"))
                dve.tensor_copy(gst[:, 0, :], mv[0:CH, 0:2, 0]).then_inc(*q.adds("stat_ready"))
                yield
                gmean, gvar = ps[0:CH, 6, NTOK:NTOK + 2], ps[0:CH, 6, NTOK + 2:NTOK + 4]
                dve.wait_ge(*q.next("stat_mm"))
                dve.tensor_tensor(gbi[0:CH, :], gst[:, 0, :], gmean, ALU.subtract).then_inc(*q.adds("dve_step"))
                dve.wait_ge(*q.own("dve_step"))
                dve.tensor_tensor(gbi[0:CH, :], gbi[0:CH, :], gbi[0:CH, :], ALU.mult).then_inc(*q.adds("dve_step"))
                dve.wait_ge(*q.own("dve_step"))
                dve.tensor_tensor(gst[:, 1, :], gbi[0:CH, :], mv[0:CH, 0:2, 1], ALU.add).then_inc(*q.adds("stat_ready"))
                yield
                dve.wait_ge(*q.next("stat_mm"))
                dve.tensor_scalar(ve[0:CH, 0:2], gvar, 1e-5, None, ALU.add).then_inc(*q.adds("var_ready"))
                dve.wait_ge(*q.next("rstd_ready"))
                dve.tensor_copy(gsc[0:CH, :], rstd[0:CH, 0:2]).then_inc(*q.adds("dve_step"))
                dve.wait_ge(*q.own("dve_step"))
                dve.scalar_tensor_tensor(out=gbi[0:CH, :], in0=gmean, scalar=-1.0, in1=gsc[0:CH, :],
                                         op0=ALU.mult, op1=ALU.mult).then_inc(*q.adds("stat_ready"))
                dve.wait_ge(*q.next("stat_ready", 3))
                dve.tensor_scalar(xt[:, 1, im * NTOK:(im + 1) * NTOK], ps[0:CH + 1, 7, 0:NTOK],
                                  gsc[:, 1:2], gbi[:, 1:2], ALU.mult, ALU.add).then_inc(*q.adds("xt1_ready"))
                yield
                yield from qkv(q, L1, im)

            def side_a2(q, im):
                xt1(q, im)
                yield
                residual(q, "proj_mm", im).then_inc(*q.adds("dve_step"))
                dve.wait_ge(*q.own("dve_step"))
                norm(q, tiles_of(im), x, xn, 1e-5, "rows_ready")
                yield
                xt1(q, im)
                yield
                yield from qkv(q, L2, im)

            def side_a3(q, im):
                xt1(q, im)
                yield
                residual(q, "proj_mm", im).then_inc(*q.adds("dve_step"))
                dve.wait_ge(*q.own("dve_step"))
                dve.tensor_copy(image_x(q.turn, im), x[:, 2 * im:2 * im + 2, 0:D])
                norm(q, tiles_of(im), x, xn, 1e-5, "rows_ready")
                yield
                xt1(q, im)
                yield
                r = probabilities(q, E2, im)
                dve.tensor_tensor(pall[:, bass.ds(q.turn * TT + 2 * im, 2), :], ge[:, 2 * im:2 * im + 2, :], r,
                                  ALU.mult).then_inc(*q.adds("turn_end"))
                yield

            def side_b0(q, im):
                dve.sem_inc(*q.adds("waited"))
                dve.tensor_copy(x[:, 2 * im:2 * im + 2, 0:D], image_x(q.turn, im)).then_inc(*q.adds("dve_step"))
                dve.wait_ge(*q.own("dve_step"))
                norm(q, tiles_of(im), x, xn, 1e-5, "rows_ready")
                xt1(q, im)
                yield
                yield from qkv(q, L3, im)

            def side_b1(q, im):
                i2 = slice(2 * im, 2 * im + 2)
                xt1(q, im)
                yield
                residual(q, "proj_mm", im).then_inc(*q.adds("dve_step"))
                dve.wait_ge(*q.own("dve_step"))
                norm(q, tiles_of(im), x, lx, 1e-5, "rows_ready")
                yield
                xt1(q, im)
                yield
                r = probabilities(q, E3, im)
                dve.tensor_tensor(p4[:, :, :], ge[:, i2, 0:E3], r, ALU.mult).then_inc(*q.adds("prow_in"))
                yield
                dve.wait_ge(*q.next("rows_ready", 3 if im == 0 else 2))
                norm(q, tiles_of(im), lx, yb, 1e-6)
                dve.wait_ge(*q.next("prow_mm"))
                dve.tensor_copy(prow[:, :], ps[0:E3, 6, 64:64 + NTOK]).then_inc(*q.adds("dve_step"))
                dve.wait_ge(*q.own("dve_step"))
                rws = [prow, left]
                for k in range(CAP // 8):
                    dve.max(top8[:, :], rws[k % 2][:, :]).then_inc(*q.adds("dve_step"))
                    dve.wait_ge(*q.own("dve_step"))
                    dve.match_replace(rws[(k + 1) % 2][:, :], top8[:, :], rws[k % 2][:, :], -1.0).then_inc(*q.adds("dve_step"))
                    dve.wait_ge(*q.own("dve_step"))
                    if k % 4 == 3:
                        yield
                dve.tensor_scalar(srow[:, :], rws[(CAP // 8) % 2][:, :], 0.0, None, ALU.is_lt).then_inc(*q.adds("prow_in"))
                g3 = gb3[:, :, :].unsqueeze(2).to_broadcast([128, 2, 2, D])
                dve.tensor_tensor(yb[:, i2, :], yb[:, i2, :], g3[:, 0], ALU.mult).then_inc(*q.adds("dve_step"))
                dve.wait_ge(*q.own("dve_step"))
                dve.tensor_tensor(yb[:, i2, :], yb[:, i2, :], g3[:, 1], ALU.add).then_inc(*q.adds("dve_step"))
                dve.wait_ge(*q.own("dve_step"))
                yield
                dve.wait_ge(*q.next("prow_mm"))
                dve.tensor_copy(sel[:, :, :], ps[:, 6, 0:2 * E3].rearrange("p (f e) -> p f e", f=2)).then_inc(*q.adds("dve_step"))
                dve.wait_ge(*q.own("dve_step"))
                g = gate[:, im]
                dve.tensor_tensor(g, sel[:, :, :], p4[:, :, :], ALU.mult).then_inc(*q.adds("dve_step"))
                dve.wait_ge(*q.own("dve_step"))
                for e in range(E3 - 2, -1, -1):
                    for z in (sel[:, :, :], g):
                        ins = dve.tensor_tensor(z[:, :, e], z[:, :, e], z[:, :, e + 1], ALU.add)
                    ins.then_inc(*q.adds("dve_step"))
                    dve.wait_ge(*q.own("dve_step"))
                dve.tensor_copy(xg[:, i2, D], sel[:, :, 0])
                for e, (c0, c1) in enumerate(SEGS):
                    ins = dve.tensor_tensor(xg[:, i2, c0:c1], yb[:, i2, c0:c1],
                                            sel[:, :, e:e + 1].to_broadcast([128, 2, c1 - c0]), ALU.mult)
                ins.then_inc(*q.adds("rows_ready"))
                yield
                xt1(q, im)
                yield
                yield
                yield from qkv(q, L4, im)

            def side_b2(q, im):
                i2 = slice(2 * im, 2 * im + 2)
                xt1(q, im)
                dve.tensor_tensor(x[:, i2, 0:D], x[:, i2, 0:D], lx[:, i2, 0:D], ALU.add).then_inc(*q.adds("dve_step"))
                dve.wait_ge(*q.own("dve_step"))
                yield
                dve.wait_ge(*q.next("proj_mm"))
                for e, (c0, c1) in enumerate(SEGS):
                    ins = dve.tensor_tensor(yb[:, i2, c0:c1],
                                            ps[:, 6, 0:2 * D].rearrange("p (i d) -> p i d", i=2)[:, :, c0:c1],
                                            gate[:, im, :, e:e + 1].to_broadcast([128, 2, c1 - c0]), ALU.mult)
                ins.then_inc(*q.adds("dve_step"))
                dve.wait_ge(*q.own("dve_step"))
                dve.tensor_tensor(image_x(q.turn, im), x[:, i2, 0:D], yb[:, i2, :], ALU.add).then_inc(*q.adds("turn_end"))
                dve.wait_ge(*q.next("turn_end"))
                yield

            dve.memset(nhalf[:, :], -0.5)
            dve.memset(ve[:, :], 1.0)
            dve.memset(ones[:, :], 1.0)
            for e in range(E2):
                dve.memset(order[:, e:e + 1], float(E2 - e))
            for z in (x, xn, att):
                dve.memset(z[:, :, D:D + 1], 1.0)
            dve.memset(xt[CH:CH + 1, 0, :], 0.0)
            dve.memset(xp[CH:CH + 1, 0, :], 0.0)
            dve.memset(gsc[CH:CH + 1, :], 1.0)
            dve.memset(gbi[CH:CH + 1, :], 0.0)
            dve.memset(gl[:, :, :], 0.0)
            dve.memset(v[:, :, :, :, HD:VW], 1.0).then_inc(set_up, 1)
            dve.wait_ge(ld_a, 16 * len(loads_a))
            dve.wait_ge(ld_x, 16)
            dve.tensor_copy(tri16[:, :], tri[:, :])
            dve.tensor_copy(ident16[:, :], ident[:, :])
            dve.tensor_scalar(kpadz, kpadz, L0.scale, None, ALU.mult).then_inc(const_ready, 1)
            with dve.Fori(0, TURNS) as t:
                q = Port(sa, t)
                dve.sem_clear(q.s.sem["dve_step"])
                for _ in side_a0(q, 0):
                    pass
                run(q, L0, 0, side_a0(q, 1), 5)
                run(q, L0, 1, side_a1(q, 0), 11)
                run(q, L1, 0, side_a1(q, 1), 11)
                run(q, L1, 1, side_a2(q, 0), 5)
                run(q, L2, 0, side_a2(q, 1), 5)
                run(q, L2, 1, side_a3(q, 0), 4)
                for _ in side_a3(q, 1):
                    pass

            dve.wait_ge(sa.sem["turn_end"], TURNS * IMGS)
            dve.tensor_reduce(imp[:, :], pall[:, :, :].rearrange("p t e -> p e t"), AX.X, ALU.add)\
                .then_inc(imp_in, 1)
            dve.wait_ge(imp_mm, 1)
            dve.tensor_scalar(rrun[:, :], ps[:, 0, 0:E2], 1.0, 1.0 - 0.9, ALU.subtract, ALU.mult)\
                .then_inc(imp_step, 1)
            dve.wait_ge(imp_step, 1)
            dve.tensor_scalar(imp[:, :], rrun[:, :], 1.0, 0.01, ALU.add, ALU.add).then_inc(imp_step, 1)
            dve.wait_ge(imp_step, 2)
            dve.reciprocal(rrun[:, :], imp[:, :]).then_inc(imp_done, 1)
            dve.wait_ge(ld_b, 16 * len(loads_b))
            dve.tensor_tensor(ffn2[:, :, 0, :], ffn2[:, :, 0, :], ffn2[:, :, 1, :], ALU.add)
            dve.tensor_tensor(ffn2a[:, :, 0, :], ffn2a[:, :, 0, :], ffn2a[:, :, 1, :], ALU.add)\
                .then_inc(ffn2_summed, 1)
            dve.wait_ge(imp_done, 1)
            ob = order[:, :].unsqueeze(1).to_broadcast([128, TT, E2])
            with dve.Fori(0, TURNS) as t:
                q = Port(sm, t)
                dve.sem_clear(q.s.sem["dve_step"])
                dve.tensor_copy(x[:, :, 0:D], turn_x(t)).then_inc(*q.adds("dve_step"))
                dve.wait_ge(*q.own("dve_step"))
                norm(q, range(TT), x, xn, 1e-5, "rows_ready")
                dve.wait_ge(*q.next("turned", 2))
                dve.tensor_copy(xt[:, 1, :], ps[0:CH + 1, 7, :]).then_inc(*q.adds("xt1_ready"))
                dve.tensor_copy(gl[:, :, :], pall[:, bass.ds(t * TT, TT), :]).then_inc(*q.adds("dve_step"))
                dve.wait_ge(*q.own("dve_step"))
                dve.tensor_copy(cw[:, :, :], gl[:, :, :]).then_inc(*q.adds("dve_step"))
                dve.wait_ge(*q.own("dve_step"))
                for k in range(2):
                    dve.tensor_reduce(gm[:, :], cw[:, :, :], AX.X, ALU.max).then_inc(*q.adds("dve_step"))
                    dve.wait_ge(*q.own("dve_step"))
                    gmb = gm[:, :].unsqueeze(2).to_broadcast([128, TT, E2])
                    dve.tensor_tensor(oh[:, k], cw[:, :, :], gmb, ALU.is_equal).then_inc(*q.adds("dve_step"))
                    dve.wait_ge(*q.own("dve_step"))
                    dve.tensor_tensor(oh[:, k], oh[:, k], ob, ALU.mult).then_inc(*q.adds("dve_step"))
                    dve.wait_ge(*q.own("dve_step"))
                    dve.tensor_reduce(gm[:, :], oh[:, k], AX.X, ALU.max).then_inc(*q.adds("dve_step"))
                    dve.wait_ge(*q.own("dve_step"))
                    dve.tensor_tensor(oh[:, k], ob, gmb, ALU.is_equal).then_inc(*q.adds("dve_step"))
                    dve.wait_ge(*q.own("dve_step"))
                    if k == 0:
                        dve.scalar_tensor_tensor(out=cw[:, :, :], in0=oh[:, 0], scalar=-2.0,
                                                  in1=cw[:, :, :], op0=ALU.mult, op1=ALU.add).then_inc(*q.adds("dve_step"))
                        dve.wait_ge(*q.own("dve_step"))
                dve.tensor_tensor(oh[:, 2], oh[:, 0], oh[:, 1], ALU.add).then_inc(*q.adds("dve_step"))
                dve.wait_ge(*q.own("dve_step"))
                dve.tensor_tensor(cw[:, :, :], oh[:, 2], gl[:, :, :], ALU.mult).then_inc(*q.adds("dve_step"))
                dve.wait_ge(*q.own("dve_step"))
                dve.tensor_tensor(cw[:, :, :], cw[:, :, :],
                                   rrun[:, :].unsqueeze(1).to_broadcast([128, TT, E2]), ALU.mult).then_inc(*q.adds("dve_step"))
                dve.wait_ge(*q.own("dve_step"))
                dve.tensor_reduce(gs[:, :], cw[:, :, :], AX.X, ALU.add).then_inc(*q.adds("dve_step"))
                dve.wait_ge(*q.own("dve_step"))
                dve.reciprocal(gs[:, :], gs[:, :]).then_inc(*q.adds("dve_step"))
                dve.wait_ge(*q.own("dve_step"))
                dve.tensor_tensor(cw[:, :, :], cw[:, :, :],
                                   gs[:, :].unsqueeze(2).to_broadcast([128, TT, E2]), ALU.mult).then_inc(*q.adds("dve_step"))
                dve.wait_ge(*q.own("dve_step"))
                for e in range(E2):
                    dve.wait_ge(*q.next("fc2_mm"))
                    for i in range(TT):
                        dst = x[:, i, 0:D]
                        ins = dve.scalar_tensor_tensor(
                            out=dst, in0=ps[:, 4 + 2 * (e % 2) + i // 2, (i % 2) * D:(i % 2 + 1) * D],
                            scalar=cw[:, i, e:e + 1], in1=dst, op0=ALU.mult, op1=ALU.add)
                    ins.then_inc(*q.adds("acc_done"))
                    dve.wait_ge(*q.next("acc_done"))
                dve.sem_inc(*q.adds("waited"))
                dve.tensor_copy(turn_x(t), x[:, :, 0:D]).then_inc(*q.adds("turn_end"))
                dve.wait_ge(*q.next("turn_end"))

            for z in (lx, xg):
                dve.memset(z[:, :, D:D + 1], 1.0)
            dve.memset(gl[:, :, :], 0.0).then_inc(set_b, 1)
            dve.wait_ge(set_b, 1)
            with dve.Fori(0, TURNS) as t:
                q = Port(sbb, t)
                dve.sem_clear(q.s.sem["dve_step"])
                for _ in side_b0(q, 0):
                    pass
                run(q, L3, 0, side_b0(q, 1), 3)
                run(q, L3, 1, side_b1(q, 0), 14)
                run(q, L4, 0, side_b1(q, 1), 14)
                run(q, L4, 1, side_b2(q, 0), 2)
                for _ in side_b2(q, 1):
                    pass

        return {"a": sa.made, "m": sm.made, "b": sbb.made}


def attention_weights(w, b, proj, proj_b):
    o = np.zeros((CH + 1, 2, 2 * QUADS * 128 + 2 * D), np.float32)
    qk = o[:, :, 0:2 * QUADS * 128].reshape(CH + 1, 2, 2, HEADS, 32)
    for c in range(2):
        rows = slice(c * CH, (c + 1) * CH)
        qk[0:CH, c, :, :, 0:HD] = w[rows, 0:2 * D].reshape(CH, 2, HEADS, HD)
        o[0:CH, c, 768:768 + D] = w[rows, 2 * D:3 * D]
        if proj is not None:
            o[0:CH, c, 768 + D:] = proj[rows]
    if b is not None:
        qk[CH, 1, :, :, 0:HD] = b[0:2 * D].reshape(2, HEADS, HD)
        o[CH, 1, 768:768 + D] = b[2 * D:3 * D]
    if proj_b is not None:
        o[CH, 1, 768 + D:] = proj_b
    return o


def by_chunk(w, b=None):
    o = np.zeros((CH + (b is not None), 2, w.shape[1]), np.float32)
    o[0:CH] = w.reshape(2, CH, -1).transpose(1, 0, 2)
    if b is not None:
        o[CH, 1] = b
    return o


def rel_weights(rh, rw, n):
    o = np.zeros((QH, 32, 2, n, QH, RR), np.float32)
    idx = np.arange(n)[:, None] - np.arange(n)[None, :] + n - 1
    for j in range(QH):
        for axis, table in enumerate((rh, rw)):
            o[j, 0:HD, axis, :, j, 0:n] = table[idx].transpose(2, 0, 1)
    return o.reshape(128, -1)


def constants():
    h, w = np.divmod(np.arange(NTOK), WW)
    window = (h // WS) * 2 + w // WS
    t = np.arange(NTOK)
    e1, e0 = np.zeros((2, 2, RR, NTOK), np.float32)
    e1[0, h, t] = e1[1, w, t] = 1
    e0[0, h % WS, t] = e0[1, w % WS, t] = 1
    edge = np.concatenate([t.reshape(HH, WW)[0:WS, WS:].ravel(), t[WS * WW:]])
    a, b = np.divmod(np.arange(NPAD), WS)
    ee = np.zeros((2, RR, EDGE + NPAD), np.float32)
    ee[:, :, 0:EDGE] = e0[:, :, edge]
    ee[0, a, EDGE + np.arange(NPAD)] = ee[1, b, EDGE + np.arange(NPAD)] = 1
    winrow = np.zeros((2, QH, RR, EDGE), np.float32)
    for n in range(4):
        row = n // 2, WS + n % 2
        real_h, real_w = (WS if n // 2 == 0 else HH - WS), (WS if n % 2 == 0 else WW - WS)
        ee[row][0:EDGE] = window[edge] != n
        ee[row][EDGE:] = (a < real_h) & (b < real_w)
        winrow[n // 2, :, WS + n % 2] = np.where(window[edge] == n, MASKED, 0)
    i = np.arange(128)
    c = np.arange(CH) // 6
    even = (i // 32 % 2 == 0).astype(np.float32)
    par = np.stack([even, 1 - even], 1)
    par = np.stack([par * np.float32(L0.scale), par * np.float32(L3.scale)], 1).astype(np.float32)
    return {"ez0": by_head(e0), "ez1": by_head(e1), "eze": by_head(ee), "winrow": winrow.reshape(128, EDGE),
            "par": par, "tri": np.where(i[None, :] > i[:, None], MASKED, 0).astype(np.float32),
            "ident": np.eye(128, dtype=np.float32),
            "ggrp": np.where(c[:, None] == c[None, :], 1 / 6, 0).astype(np.float32)}


def by_head(z):
    o = np.zeros((2, QH, RR, QH, z.shape[2]), np.float32)
    for j in range(QH):
        o[:, j, :, j] = z
    return o.reshape(128, -1)


def kernel(**inputs):
    import concourse.bacc as bacc
    from concourse.bass_utils import run_bass_kernel_spmd as run

    i = {n: np.asarray(z) for n, z in inputs.items()}
    a = constants()
    a["x"] = i["x"].reshape(B * NTOK, D)
    l0 = attention_weights(i["L0_conv_qkv_w"], i["L0_conv_qkv_b"], i["L0_conv_proj_w"], i["L0_conv_proj_b"])
    l1 = attention_weights(i["L1_conv_w_qkv"], i["L1_conv_b_qkv"], i["L1_conv_w_proj"], i["L1_conv_b_proj"])
    perm = np.r_[D:2 * D, 0:D, 2 * D:3 * D]
    l2 = attention_weights(i["L2_attn_W_kqv"][:, perm], i["L2_attn_b_kqv"][perm], i["L2_attn_W_proj"],
                           i["L2_attn_b_proj"])
    l3 = attention_weights(i["L3_attn_w_qkv"], None, i["L3_attn_w_out"], i["L3_attn_b_out"])
    w1t = i["L3_ffn_w1"].T
    l4 = attention_weights(w1t[:, MLP:], i["L3_ffn_b1"][MLP:], None, None)
    a["lw"] = np.stack([l0, l1, l2], 1).reshape(CH + 1, -1)
    a["lw2"] = np.stack([l3, l4], 1)
    a["relw"] = np.concatenate([rel_weights(i["L0_conv_rel_pos_h"], i["L0_conv_rel_pos_w"], WS),
                                rel_weights(i["L1_conv_rel_pos_h"], i["L1_conv_rel_pos_w"], HH)], 1)
    a["fc1"] = by_chunk(i["L0_conv_fc1_w"], i["L0_conv_fc1_b"])
    a["fc2"] = i["L0_conv_fc2_w"].reshape(MLP // 128, 128, D).transpose(1, 0, 2)
    a["fc2b"] = i["L0_conv_fc2_b"].reshape(1, D)
    cols = np.zeros((CH + 1, 2, 4), np.float32)
    cols[CH, :, 0::2] = 1
    for n, name in enumerate(("norm1_w", "norm1_b", "norm2_w", "norm2_b")):
        cols[0:CH, :, n] = i["L0_conv_" + name].reshape(2, CH).T
    a["cols"] = cols
    kpad = np.zeros((QUADS, QH, 32, 2, NPAD), np.float32)
    for j in range(QH):
        kpad[:, j, 0:HD, j % 2] = i["L0_conv_qkv_b"][D:2 * D].reshape(QUADS, QH, HD, 1)[:, j]
    a["kpadz"] = kpad.reshape(QUADS, 128, 2, NPAD).transpose(1, 2, 0, 3)
    vpad = np.ones((98, HEADS, VW), np.float32)
    vpad[:, :, 0:HD] = i["L0_conv_qkv_b"][2 * D:].reshape(1, HEADS, HD)
    a["vpad"] = vpad
    a["rout"] = np.concatenate([by_chunk(i["L2_ffn_router_w"].T), by_chunk(i["L3_ffn_w_router"].T)], 2)
    a["moe1"] = i["L2_ffn_w1"].transpose(2, 0, 1).reshape(2, CH, E2, I2).transpose(1, 0, 2, 3)
    a["moe2"] = i["L2_ffn_w2"].transpose(0, 2, 1).reshape(E2, 4, 128, D).transpose(2, 0, 1, 3)
    a["ffn1"] = by_chunk(w1t[:, 0:MLP], i["L3_ffn_b1"][0:MLP])
    w2t = i["L3_ffn_w2"].T.reshape(MLP + D, 2, D)
    a["ffn2"] = w2t[0:MLP].reshape(MLP // 128, 128, 2, D).transpose(1, 0, 2, 3)
    f2a = np.zeros((CH + 1, 2, 2, D), np.float32)
    f2a[0:CH] = w2t[MLP:].reshape(2, CH, 2, D).transpose(1, 0, 2, 3)
    f2a[CH, 1] = i["L3_ffn_b2"].reshape(2, D)
    a["ffn2a"] = f2a
    a["gb3"] = np.broadcast_to(np.stack([i["L3_ffn_gamma1"], i["L3_ffn_beta1"]])[None], (128, 2, D))
    a = {n: np.ascontiguousarray(z) for n, z in a.items()}

    per = {}
    for _ in range(2):
        nc = bacc.Bacc("TRN2", target_bir_lowering=False, num_devices=1)
        aps = {n: nc.dram_tensor("in_" + n, z.shape, F32, kind="ExternalInput").ap() for n, z in a.items()}
        out = nc.dram_tensor("out", (B * NTOK, D), F32, kind="ExternalOutput").ap()
        per = program(nc, aps, out, per)
    r = run(nc, [{"in_" + n: z for n, z in a.items()}], core_ids=[0])
    return r.results[0]["out"].reshape(B, HH, WW, D)
```

```python
from contextlib import ExitStack
from itertools import chain

import numpy as np
import concourse.bass as bass
from concourse import mybir

F32 = mybir.dt.float32
BF16 = mybir.dt.bfloat16
ALU = mybir.AluOpType
ACT = mybir.ActivationFunctionType
AX = mybir.AxisListType

B, HH, WW, D = 8, 16, 16, 192
NTOK = HH * WW
HEADS, HD = 12, 16
QUADS, QH = 3, 4
IMGS = 2
TURNS = B // IMGS
T = IMGS * NTOK
TT = T // 128
CH = 96
WS = 14
NPAD = WS * WS
RR = 16
INNER = WS * WS
EDGE = NTOK - INNER
HALF0 = INNER // 2
EB = 2 * WS
MLP = 4 * D
NM = MLP // 128
E2, I2 = 8, 512
EARLY = 5
E3 = 4
CAP = NTOK // 2
HOPS_B1 = 13
SEGS = [(0, 24), (24, 48), (48, 96), (96, 192)]
MASKED = -1e30
RING = 2
TURN_LAG, PV_LAG = 2, 3
P_RING = 3
VW = 2 * HD
WL = 2 * QUADS * 128 + D


class Attn:

    def __init__(self, name, scale, rel=0, pad=False, causal=False, act_keeps=False):
        self.name, self.scale, self.rel, self.pad, self.causal = name, scale, rel, pad, causal
        self.tiles = [(h, e) for h in range(HEADS) for e in range(2)] if pad else [(h, 0) for h in range(HEADS)]
        self.act_keeps = act_keeps


L0 = Attn("l0", HD ** -0.5, rel=WS, pad=True)
L1 = Attn("l1", HD ** -0.5, rel=HH)
L2 = Attn("l2", HD ** -0.5, causal=True, act_keeps=True)
L3 = Attn("l3", D ** -0.5, act_keeps=True)
L4 = Attn("l4", HD ** -0.5, act_keeps=True)


LAYERS = L0, L1, L2, L3


class Signals:

    def __init__(self, nc, ctx, loop, names, per):
        self.sem = {n: ctx.enter_context(nc.semaphore(f"{loop}_{n}")) for n in names}
        self.per = {n: per.get(n, 1) for n in names}
        self.made = dict.fromkeys(names, 0)


class Port:

    def __init__(self, signals):
        self.s = signals
        self.seen = dict.fromkeys(signals.sem, 0)
        self.base = dict(self.seen)
        self.stage(0, 0)
        self.starting = True

    def stage(self, turn, coming=None, rounds=0, looping=False):
        self.turn, self.coming, self.rounds, self.looping = turn, coming, rounds, looping
        self.starting = False
        self.seen["dve_step"] = 0

    def next(self, name, n=1):
        self.seen[name] += n
        return self.s.sem[name], self.rounds * self.s.per[name] + self.seen[name]

    def passed(self, name, n):
        self.seen[name] += n

    def mark(self):
        self.base = dict(self.seen)

    def behind(self, name, n):
        return self.base[name] + n > self.seen[name]

    def to(self, name, n):
        return self.next(name, self.base[name] + n - self.seen[name])

    def ended(self, names, n):
        for name in names:
            self.seen[name] = self.base[name] + n

    def adds(self, name):
        self.s.made[name] += self.looping
        return self.s.sem[name], 1

    def own(self, name):
        self.seen[name] += 1
        return self.s.sem[name], self.seen[name]


NAMES = ["dve_step", "var_ready", "rstd_ready", "rows_ready", "turned", "xt0_ready", "xt1_ready", "q01_mm", "q2k0_mm",
         "k12_mm", "v_mm", "q01_ready", "q2k0_ready", "k12_ready", "v_ready", "rel_mm", "rel0_ready",
         "rel1_ready", "edge_ready", "sc_mm", "max_done", "exp_done", "pt_mm", "pt_done", "pv_mm", "at_ready",
         "back_mm", "div_done", "proj_mm", "fc1_mm", "h_ready", "fc2_mm", "acc_done", "stat_ready", "stat_mm",
         "gate_mm", "gate_in", "gate_exp", "choice_in", "choice_mm", "turn_end", "waited"]


def slot(steps, attend, side, hops):
    at = 0
    for i in range(steps):
        attend(i)
        while at < hops and at * steps < (i + 1) * hops:
            next(side, None)
            at += 1
    for _ in side:
        pass


def start_a(q, run, jobs):
    a0 = jobs[0]
    for _ in a0(q, 0):
        pass
    run(q, L0, 0, a0(q, 1), 6)


def round_a(q, run, jobs, more):
    a0, a1, a2, a3 = jobs
    run(q, L0, 1, a1(q, 0), 12)
    run(q, L1, 0, a1(q, 1), 12)
    run(q, L1, 1, a2(q, 0), 7)
    run(q, L2, 0, a2(q, 1), 7)
    if more:
        run(q, L2, 1, chain(a3(q, 0), a0(q, 0)), 11)
        run(q, L0, 0, chain(a3(q, 1), a0(q, 1)), 11)
    else:
        run(q, L2, 1, a3(q, 0), 5)
        for _ in a3(q, 1):
            pass


def start_b(q, run, jobs):
    b0 = jobs[0]
    for _ in b0(q, 0):
        pass
    run(q, L3, 0, b0(q, 1), 4)


def round_b(q, run, jobs, more):
    b0, b1, b2 = jobs
    run(q, L3, 1, b1(q, 0), HOPS_B1)
    run(q, L4, 0, b1(q, 1), HOPS_B1)
    if more:
        run(q, L4, 1, chain(b2(q, 0), b0(q, 0)), 7)
        run(q, L3, 0, chain(b2(q, 1), b0(q, 1)), 7)
    else:
        run(q, L4, 1, b2(q, 0), 3)
        for _ in b2(q, 1):
            pass


def image(z):
    return z.rearrange("p (h w) -> p h w", h=HH)


def by_window(z, packed):
    parts = [(slice(0, WS), slice(0, WS), 0), (slice(0, WS), slice(WS, WW), INNER),
             (slice(WS, HH), slice(0, WW), INNER + EB)]
    out = []
    for hs, ws, at in parts:
        n = (hs.stop - hs.start) * (ws.stop - ws.start)
        if len(z.shape) == 2:
            out.append((z.rearrange("p (h w) -> p h w", h=HH)[:, hs, ws],
                        packed[:, at:at + n].rearrange("p (h w) -> p h w", h=hs.stop - hs.start)))
        else:
            out.append((z.rearrange("p s (h w) -> p s h w", h=HH)[:, :, hs, ws],
                        packed[:, :, at:at + n].rearrange("p s (h w) -> p s h w", h=hs.stop - hs.start)))
    return out


def program(nc, a, out, per):
    with ExitStack() as ctx:
        def sb(name, *shape, dt=F32):
            return ctx.enter_context(nc.sbuf_tensor(name, list(shape), dt))

        def sem(name):
            return ctx.enter_context(nc.semaphore(name))

        xall = sb("xall", 128, TURNS * TT, D)
        x = sb("x", 128, TT, D + 1)
        xn = sb("xn", 128, TT, D + 1)
        ou = sb("ou", 128, QUADS, NTOK)
        att = sb("att", 128, 2, D + 1)
        xt = sb("xt", CH + 1, 2, T)
        xp = sb("xp", CH + 1, 2, NTOK)
        qn = sb("qn", 128, QUADS, NTOK)
        qt = sb("qt", 128, IMGS, QUADS, NTOK)
        kz = sb("kz", 128, IMGS, 2, QUADS, NTOK)
        relt = sb("relt", 128, IMGS, QUADS, NTOK)
        ke = sb("ke", 128, IMGS, 2, QUADS, EDGE)
        negmax = sb("negmax", 128, P_RING, 2)
        v = sb("v", 128, IMGS, 3, HEADS, VW)
        p = sb("p", 128, P_RING, 512)
        pt = sb("pt", 128, PV_LAG, 512)
        pall = sb("pall", 128, TURNS * TT, E2)
        stats = sb("stats", 128, TT, 6)
        mv = sb("mv", 128, TT, 2)
        ve = sb("ve", 128, 4)
        rstd = sb("rstd", 128, 4)
        nhalf = sb("nhalf", 128, 4)
        gsc = sb("gsc", CH + 1, 2)
        gbi = sb("gbi", CH + 1, 2)
        gst = sb("gst", CH, 2, 2)
        gl = sb("gl", 128, TT, E2)
        ge = sb("ge", 128, TT, E2)
        gm = sb("gm", 128, TT)
        gs = sb("gs", 128, TT)
        oh = sb("oh", 128, 3, TT, E2)
        cw = sb("cw", 128, TT, E2)
        imp = sb("imp", 128, E2)
        rrun = sb("rrun", 128, E2)
        rsum = sb("rsum", 128, 2, HEADS)
        p4 = sb("p4", 128, 2, E3)
        ahead = sb("ahead", 128, E3, 6, 128, dt=BF16)
        ties = sb("ties", 128, 2, NTOK)
        ones16 = sb("ones16", 128, 1, dt=BF16)
        sel = sb("sel", 128, 2, E3)
        gate = sb("gate", 128, IMGS, 2, E3)
        ones = sb("ones", 128, 128)
        order = sb("order", 128, E2)
        tri16 = sb("tri16", 128, 128, dt=BF16)
        ident16 = sb("ident16", 128, 128, dt=BF16)

        zone = sb("zone", 128, 4248)
        hid = zone[:, 0:NM * NTOK].rearrange("p (m t) -> p m t", m=NM)
        hids = [hid, relt[:, :, :, :].rearrange("p i s t -> p (i s) t")]
        z0 = NM * NTOK
        kpadz = zone[:, z0:z0 + 6 * NPAD].rearrange("p (c s k) -> p c s k", c=2, s=QUADS)
        hid2 = zone[:, 0:8 * T].rearrange("p (m t) -> p m t", m=8)
        lx = zone[:, z0:z0 + 772].rearrange("p (i d) -> p i d", i=TT)
        xg = zone[:, z0 + 772:z0 + 1544].rearrange("p (i d) -> p i d", i=TT)
        yb = zone[:, z0 + 1544:z0 + 2312].rearrange("p (i d) -> p i d", i=TT)

        lw = sb("lw", 128, max(3 * 2 * WL, E2 * 4 * D))
        wp = sb("wp", CH + 1, len(LAYERS), 2, D)
        lw2 = sb("lw2", CH + 1, 2, 2, WL)
        wts = {n: lw[0:CH + 1, i * 2 * WL:(i + 1) * 2 * WL].rearrange("p (c n) -> p c n", c=2)
               for i, n in enumerate(("l0", "l1", "l2"))}
        wts |= {"l3": lw2[:, 0], "l4": lw2[:, 1]}
        moe2 = lw[:, 0:E2 * 4 * D].rearrange("p (e k n) -> p e k n", e=E2, k=4)
        rw = sb("rw", 128, 2 * E2 * I2)
        n0, n1 = 2 * WS * QH * RR, 2 * HH * QH * RR
        relw = {"l0": rw[:, 0:n0].rearrange("p (a h n) -> p a h n", a=2, h=WS),
                "l1": rw[:, n0:n0 + n1].rearrange("p (a h n) -> p a h n", a=2, h=HH)}
        ez0, ez1, eze = (rw[:, n0 + n1 + i * QH * NTOK:n0 + n1 + (i + 1) * QH * NTOK]
                         .rearrange("p (c k) -> p c k", c=QH) for i in range(3))
        moe1 = rw[0:CH, :].rearrange("p (c e i) -> p c e i", c=2, e=E2)
        fc1 = sb("fc1", CH + 1, 2, MLP)
        fc2 = sb("fc2", 128, NM, D)
        n2, n3 = 2 * MLP, 2 * MLP + NM * 2 * D
        ffn1 = rw[0:CH + 1, 0:n2].rearrange("p (c n) -> p c n", c=2)
        ffn2 = rw[:, n2:n3].rearrange("p (m f n) -> p m f n", m=NM, f=2)
        ffn2a = rw[0:CH + 1, n3:n3 + 4 * D].rearrange("p (c f n) -> p c f n", c=2, f=2)
        cols = sb("cols", CH + 1, 2, 4)
        gb3 = sb("gb3", 128, 2, D)
        ident = sb("ident", 128, 128)
        par = sb("par", 128, 2, 2)
        vpad = sb("vpad", 98, HEADS, VW)
        winrow = sb("winrow", 128, EDGE)
        tri = sb("tri", 128, 128)
        fc2b = sb("fc2b", 1, D)
        ggrp = sb("ggrp", CH, CH)
        rout = sb("rout", CH, 2, E2 + E3)
        ps = ctx.enter_context(nc.psum_tensor("ps", [128, 8, 512], F32))

        ld_x, ld_x_rest, ld_qkv, ld_rel, ld_rest, ld_b, ld_moe, ld_late, ld_ffn = (
            sem(n) for n in ("ld_x", "ld_x_rest", "ld_qkv", "ld_rel", "ld_rest", "ld_b", "ld_moe", "ld_late",
                          "ld_ffn"))
        set_up, const_ready, set_b, ffn2_summed = sem("set_up"), sem("const_ready"), sem("set_b"), sem("ffn2_summed")
        imp_in, imp_mm, imp_step, imp_done, stored = (sem("imp_in"), sem("imp_mm"), sem("imp_step"),
                                                      sem("imp_done"), sem("stored"))
        sa = Signals(nc, ctx, "a", NAMES, per.get("a", {}))
        sm = Signals(nc, ctx, "m", ["dve_step", "var_ready", "rstd_ready", "rows_ready", "turned", "xt0_ready",
                                    "xt1_ready", "fc1_mm", "h_ready", "fc2_mm", "acc_done", "turn_end", "waited"],
                     per.get("m", {}))
        sbb = Signals(nc, ctx, "b", NAMES, per.get("b", {}))

        loads_qkv = [(ident[:, :], a["ident"]), (cols[:, :, :], a["cols"]), (par[:, :, :], a["par"]),
                     (wts["l0"], a["lw0"])]
        loads_rel = [(rw[:, 0:n0], a["relw0"]), (winrow[:, :], a["winrow"]), (ez0, a["ez0"]), (eze, a["eze"]),
                     (kpadz, a["kpadz"]), (vpad[:, :, :], a["vpad"]), (tri[:, :], a["tri"])]
        loads_rest = [(fc1[:, :, :], a["fc1"]), (fc2[:, :, :], a["fc2"]), (fc2b[:, :], a["fc2b"]),
                      (ggrp[:, :], a["ggrp"]), (wts["l1"], a["lw1"]), (rw[:, n0:n0 + n1], a["relw1"]),
                      (ez1, a["ez1"]), (wts["l2"], a["lw2"]), (rout[:, :, :], a["rout"]),
                      (wp[:, :, :, :], a["wp"])]
        loads_b = [(lw2[:, :, :, :], a["lwb"]), (gb3[:, :, :], a["gb3"]), (ties[:, :, :], a["ties"])]
        loads_ffn = [(ffn1, a["ffn1"]), (ffn2, a["ffn2"]), (ffn2a, a["ffn2a"])]

        def turn_x(t):
            return xall[:, bass.ds(t * TT, TT), :]

        def image_x(t, im):
            return xall[:, bass.ds(t * TT + im * 2, 2), :]

        block = ctx.enter_context(nc.Block())

        @block.sync
        def _(sp):
            tokens = a["x"].rearrange("(t p) d -> p t d", p=128)
            sp.dma_start(xall[:, 0:TT, :], tokens[:, 0:TT, :]).then_inc(ld_x, 16)
            for dst, src in loads_qkv:
                sp.dma_start(dst, src).then_inc(ld_qkv, 16)
            for dst, src in loads_rel:
                sp.dma_start(dst, src).then_inc(ld_rel, 16)
            for dst, src in loads_rest:
                sp.dma_start(dst, src).then_inc(ld_rest, 16)
            sp.dma_start(xall[:, TT:, :], tokens[:, TT:, :]).then_inc(ld_x_rest, 16)
            for dst, src in loads_b:
                sp.dma_start(dst, src).then_inc(ld_b, 16)
            sp.wait_ge(sa.sem["proj_mm"], (TURNS - 1) * 3 * IMGS + 2 * IMGS)
            sp.dma_start(moe1, a["moe1"]).then_inc(ld_moe, 16)
            sp.dma_start(moe2[:, 0:EARLY], a["moe2"][:, 0:EARLY]).then_inc(ld_moe, 16)
            sp.wait_ge(sa.sem["proj_mm"], TURNS * 3 * IMGS)
            sp.dma_start(moe2[:, EARLY:], a["moe2"][:, EARLY:]).then_inc(ld_late, 16)
            sp.wait_ge(sm.sem["turn_end"], TURNS)
            for dst, src in loads_ffn:
                sp.dma_start(dst, src).then_inc(ld_ffn, 16)
            with sp.Fori(0, TURNS) as t:
                sp.wait_ge(sbb.sem["turn_end"], (t + 1) * IMGS)
                sp.dma_start(out.rearrange("(t p) d -> p t d", p=128)[:, bass.ds(t * TT, TT), :],
                             turn_x(t)).then_inc(stored, 16)
            sp.wait_ge(stored, 16 * TURNS)

        @block.tensor
        def _(pe):
            def mm(o, w, m, start=True, stop=True):
                return pe.matmul(o, w, m, start=start, stop=stop)

            def turn_over(q, tiles):
                for c in range(2):
                    n = CH + c
                    at = 0
                    for z in tiles:
                        m = z.shape[0]
                        last = pe.transpose(ps[0:n, 6 + c, at:at + m], z[:, c * CH:c * CH + n], ident[0:m, 0:m])
                        at += m
                    last.then_inc(*q.adds("turned"))

            def rows(z, im):
                return [z[:, 2 * im + i, :] for i in range(2)]

            def wait_xt(q):
                pe.wait_ge(*q.next("xt0_ready"))
                pe.wait_ge(*q.next("xt1_ready"))

            def qkv(q, l, im):
                w = wts[l.name]
                xi = xt[:, :, im * NTOK:(im + 1) * NTOK]

                def quad(s, bank, at):
                    for c in range(2):
                        last = mm(ps[:, bank, at:at + NTOK], w[:, c, s * 128:(s + 1) * 128], xi[:, c, :],
                                  c == 0, c == 1)
                    return last
                wait_xt(q)
                quad(0, 6, 0)
                quad(1, 6, NTOK).then_inc(*q.adds("q01_mm"))
                quad(2, 7, 0)
                quad(3, 7, NTOK).then_inc(*q.adds("q2k0_mm"))
                yield
                pe.wait_ge(*q.next("q01_ready"))
                quad(4, 6, 0)
                quad(5, 6, NTOK).then_inc(*q.adds("k12_mm"))
                pe.wait_ge(*q.next("q2k0_ready"))
                if l.pad:
                    tiles = [xp[:, c, at:min(at + HALF0, NTOK)] for at in range(0, NTOK, HALF0) for c in range(2)]
                else:
                    tiles = [xi[:, c, i * 128:(i + 1) * 128] for i in range(2) for c in range(2)]
                for i in range(2):
                    for c in range(2):
                        z = tiles[2 * i + c]
                        m = HALF0 if l.pad else 128
                        last = mm(ps[0:m, 7, i * D:(i + 1) * D], z, w[:, c, 768:768 + D], c == 0, c == 1)
                last.then_inc(*q.adds("v_mm"))
                yield
                pe.wait_ge(*q.next("k12_ready"))
                pe.wait_ge(*q.next("v_ready"))
                if l.pad:
                    pe.sem_inc(*q.adds("waited"))
                    for c in range(2):
                        last = mm(ps[0:EDGE, 6, 0:D], tiles[4 + c], w[:, c, 768:768 + D], c == 0, c == 1)
                    last.then_inc(*q.adds("v_mm"))
                    yield
                    pe.wait_ge(*q.next("v_ready"))
                if l.rel:
                    rwt = relw[l.name]
                    pe.wait_ge(ld_rel, 16 * len(loads_rel))
                    qi = (qn if l.pad else qt[:, im]).rearrange("p s (h w) -> p s h w", h=HH)
                    for half in range(2):
                        oh_, ow = (ps[64 * a:64 * a + 64, 6 + half, 0:QUADS * 128] for a in range(2))
                        oh_ = oh_.rearrange("p (s h w) -> p s h w", s=QUADS, h=8)
                        ow = ow.rearrange("p (s h w) -> p s h w", s=QUADS, h=HH)
                        for k in range(8):
                            at = 8 * half + k
                            pe.matmul(oh_[:, :, k, :], rwt[:, 0, at % l.rel, :], qi[:, :, at, :],
                                      start=k == 0, stop=True, skip_group_check=True)
                        for k in range(8):
                            at = 8 * half + k
                            last = pe.matmul(ow[:, :, :, k], rwt[:, 1, at % l.rel, :], qi[:, :, :, at],
                                             start=k == 0, stop=True, skip_group_check=True)
                        last.then_inc(*q.adds("rel_mm"))
                    yield

            def attention(q, l, im):
                n = len(l.tiles)
                ez = ez0 if l.pad else ez1

                def where(head):
                    j = head % QH
                    return slice(64 * (j // 2), 64 * (j // 2) + 64), head // QH, j % 2

                def scores(i):
                    head, edge = l.tiles[i]
                    r, s, c = where(head)
                    if i >= RING:
                        if q.behind("exp_done", i - RING + 1):
                            pe.wait_ge(*q.to("exp_done", i - RING + 1))
                    bank = ps[:, i % RING, :]
                    rl, qi, ki, j = relt[:, im, s, :], qt[r, im, s, :], kz[r, im, c, s, :], head % QH
                    if edge:
                        pe.sem_inc(*q.adds("waited"))
                        o = bank[0:EDGE, :]
                        mm(o[:, 0:EDGE], qi[:, INNER:], ke[r, im, c, s, :], True, False)
                        mm(o[:, 0:EDGE], rl[:, INNER:], eze[:, j, 0:EDGE], False, True)
                        mm(o[:, EDGE:NTOK], qi[:, INNER:], kpadz[r, c, s, :], True, False)
                        last = mm(o[:, EDGE:NTOK], rl[:, INNER:], eze[:, j, EDGE:NTOK], False, True)
                    elif l.pad:
                        for half in range(2):
                            o = bank[0:HALF0, half * INNER:(half + 1) * INNER]
                            hs = slice(HALF0 * half, HALF0 * half + HALF0)
                            mm(o, qi[:, hs], image(ki)[:, 0:WS, 0:WS], True, False)
                            last = mm(o, rl[:, hs], image(ez[:, j, :])[:, 0:WS, 0:WS], False, True)
                    elif l.causal:
                        mm(bank[:, 0:NTOK], qi[:, 128:256], ki, True, False)
                        mm(bank[:, 128:256], ident16[:, :], tri16[:, :], False, True)
                        mm(bank[:, NTOK:NTOK + 128], qi[:, 0:128], ki[:, 0:128], True, False)
                        last = mm(bank[:, NTOK:NTOK + 128], ident16[:, :], tri16[:, :], False, True)
                    else:
                        for half in range(2):
                            o = bank[:, half * NTOK:(half + 1) * NTOK]
                            hs = slice(128 * half, 128 * half + 128)
                            last = mm(o, qi[:, hs], ki, True, not l.rel)
                            if l.rel:
                                last = mm(o, rl[:, hs], ez[:, j, :], False, True)
                    last.then_inc(*q.adds("sc_mm"))

                def blocks(i):
                    if l.tiles[i][1]:
                        return [(EDGE, 0, 0, EDGE), (EDGE, EDGE, EDGE, 98), (EDGE, EDGE + 98, 2 * EDGE, 98)]
                    if l.causal:
                        return [(128, NTOK, 0, 128), (128, 0, 128, 128), (128, 128, 256, 128)]
                    m = HALF0 if l.pad else 128
                    return [(m, (2 * half + k) * m, (2 * k + half) * m, m) for k in range(2) for half in range(2)]

                def products(i):
                    head, edge = l.tiles[i]
                    if edge:
                        return [(v[0:EDGE, im, 2, head, :], 0, EDGE, INNER),
                                (vpad[:, head, :], EDGE, EDGE, INNER), (vpad[:, head, :], 2 * EDGE, EDGE, INNER)]
                    if l.causal:
                        return [(v[:, im, 0, head, :], 0, NTOK, 0), (v[:, im, 1, head, :], NTOK, 128, 128)]
                    m = HALF0 if l.pad else 128
                    return [(v[0:m, im, k, head, :], 2 * k * m, 2 * m, 0) for k in range(2)]

                def turn_p(i):
                    if q.behind("exp_done", i + 1):
                        pe.wait_ge(*q.to("exp_done", i + 1))
                    if i >= 2:
                        if q.behind("pt_done", i - 1):
                            pe.wait_ge(*q.to("pt_done", i - 1))
                    if l.tiles[i][1]:
                        pe.sem_inc(*q.adds("waited"))
                    for m, c0, to, nk in blocks(i):
                        last = pe.transpose(ps[0:nk, 3 + i % 2, to:to + m], p[0:m, i % P_RING, c0:c0 + nk],
                                            ident[0:m, 0:m])
                    last.then_inc(*q.adds("pt_mm"))

                def values(i):
                    head, edge = l.tiles[i]
                    if q.behind("pt_done", i + 1):
                        pe.wait_ge(*q.to("pt_done", i + 1))
                    if edge:
                        pe.sem_inc(*q.adds("waited"))
                    j, s = head % QH, head // QH
                    bank, t0 = (2, s * NTOK) if s < 2 else (5, 0)
                    todo = products(i)
                    for n_, (vv, c0, k, tok) in enumerate(todo):
                        last = mm(ps[32 * j:32 * j + 32, bank, t0 + tok:t0 + tok + k], vv,
                                  pt[0:vv.shape[0], i % PV_LAG, c0:c0 + k], n_ == 0, n_ == len(todo) - 1)
                    last.then_inc(*q.adds("pv_mm"))

                def step(i):
                    if i == 0:
                        if l.pad:
                            pe.wait_ge(const_ready, 1)
                            pe.wait_ge(*q.next("rel0_ready"))
                            pe.wait_ge(*q.next("rel1_ready"))
                            pe.wait_ge(*q.next("edge_ready"))
                        elif l.rel:
                            pe.wait_ge(*q.next("rel0_ready"))
                            pe.wait_ge(*q.next("rel1_ready"))
                        q.mark()
                    if i < n:
                        scores(i)
                    if TURN_LAG <= i < n + TURN_LAG:
                        turn_p(i - TURN_LAG)
                    if PV_LAG <= i:
                        values(i - PV_LAG)
                    if i == n + PV_LAG - 1:
                        q.ended(("exp_done", "pt_done"), n)
                return step

            def run(q, l, im, side, hops):
                slot(len(l.tiles) + PV_LAG, attention(q, l, im), side, hops)

            def turn_back(q):
                pe.wait_ge(*q.next("at_ready"))
                for i in range(2):
                    for s in range(QUADS):
                        last = pe.transpose(ps[:, 6 + i, s * 128:(s + 1) * 128], ou[:, s, i * 128:(i + 1) * 128],
                                            ident[:, :])
                last.then_inc(*q.adds("back_mm"))
                yield
                pe.wait_ge(*q.next("div_done"))
                turn_over(q, [att[:, i, :] for i in range(2)])
                yield

            def project(q, l, im):
                yield from turn_back(q)
                wait_xt(q)
                for i in range(2):
                    t0 = im * NTOK + i * 128
                    for c in range(2):
                        last = mm(ps[:, 6, i * D:(i + 1) * D], xt[:, c, t0:t0 + 128], wp[:, LAYERS.index(l), c, :],
                                  c == 0, c == 1)
                last.then_inc(*q.adds("proj_mm"))
                yield

            def hidden(q, w, im):
                wait_xt(q)
                for m in range(NM):
                    if m >= 4 and m % 2 == 0:
                        pe.wait_ge(*q.next("h_ready"))
                    for c in range(2):
                        last = mm(ps[:, 6 + m // 2 % 2, m % 2 * NTOK:(m % 2 + 1) * NTOK],
                                  w[:, c, m * 128:(m + 1) * 128], xt[:, c, im * NTOK:(im + 1) * NTOK], c == 0, c == 1)
                    if m % 2:
                        last.then_inc(*q.adds("fc1_mm"))
                yield
                pe.wait_ge(*q.next("h_ready", 2))

            def gate_logits(q, w, im):
                n = w.shape[2]
                wait_xt(q)
                for i in range(2):
                    t0 = im * NTOK + i * 128
                    for c in range(2):
                        last = mm(ps[:, 6, i * n:(i + 1) * n], xt[0:CH, c, t0:t0 + 128], w[:, c, :], c == 0, c == 1)
                last.then_inc(*q.adds("gate_mm"))
                yield

            def side_a0(q, im):
                yield
                pe.wait_ge(*q.next("rows_ready"))
                turn_over(q, rows(xn, im))
                yield
                yield from qkv(q, L0, im)

            def side_a1(q, im):
                yield from project(q, L0, im)
                pe.wait_ge(*q.next("rows_ready"))
                turn_over(q, rows(xn, im))
                yield
                yield from hidden(q, fc1, im)
                for i in range(2):
                    o = ps[:, 6, i * D:(i + 1) * D]
                    mm(o, ones[0:1, :], fc2b[:, :], True, False)
                    for m in range(NM):
                        last = mm(o, hid[:, m, i * 128:(i + 1) * 128], fc2[:, m, :], False, m == NM - 1)
                last.then_inc(*q.adds("fc2_mm"))
                yield
                pe.wait_ge(*q.next("rows_ready"))
                turn_over(q, rows(x, im))
                yield
                pe.wait_ge(*q.next("stat_ready"))
                mm(ps[0:CH, 6, NTOK:NTOK + 2], ggrp[:, :], gst[:, 0, :]).then_inc(*q.adds("stat_mm"))
                yield
                pe.wait_ge(*q.next("stat_ready"))
                mm(ps[0:CH, 6, NTOK + 2:NTOK + 4], ggrp[:, :], gst[:, 1, :]).then_inc(*q.adds("stat_mm"))
                q.passed("stat_ready", 1)
                yield
                yield from qkv(q, L1, im)

            def side_a2(q, im):
                yield from project(q, L1, im)
                pe.wait_ge(*q.next("rows_ready"))
                turn_over(q, rows(xn, im))
                yield
                yield from qkv(q, L2, im)

            def side_a3(q, im):
                yield from project(q, L2, im)
                pe.wait_ge(*q.next("rows_ready"))
                turn_over(q, rows(xn, im))
                yield
                yield from gate_logits(q, rout[:, :, 0:E2], im)

            def side_b0(q, im):
                yield
                pe.wait_ge(*q.next("rows_ready"))
                turn_over(q, rows(xn, im))
                yield
                yield from qkv(q, L3, im)

            def side_b1(q, im):
                yield from project(q, L3, im)
                pe.wait_ge(*q.next("rows_ready"))
                turn_over(q, rows(lx, im))
                yield
                yield from gate_logits(q, rout[:, :, E2:E2 + E3], im)
                pe.wait_ge(*q.next("choice_in"))
                pe.sem_inc(*q.adds("waited"))
                for e in range(E3):
                    for half in range(2):
                        at = (e % 2) * NTOK + half * 128
                        last = pe.transpose(ps[:, 6 + e // 2, at:at + 128],
                                            p4[:, half, e:e + 1].to_broadcast([128, 128]), ident[:, :])
                last.then_inc(*q.adds("choice_mm"))
                yield
                yield
                yield
                pe.wait_ge(*q.next("choice_in"))
                pe.sem_inc(*q.adds("waited"))
                for half in range(2):
                    for e in range(E3):
                        for k in range(3):
                            last = mm(ps[:, 6, half * E3 + e:half * E3 + e + 1], ahead[:, e, 2 * k + half, :],
                                      ones16[:, :], k == 0, k == 2)
                last.then_inc(*q.adds("choice_mm"))
                yield
                pe.wait_ge(*q.next("rows_ready"))
                turn_over(q, rows(xg, im))
                yield
                yield from hidden(q, ffn1, im)
                q.passed("xt0_ready", -1)
                q.passed("xt1_ready", -1)
                yield from qkv(q, L4, im)

            def side_b2(q, im):
                yield from turn_back(q)
                wait_xt(q)
                for i in range(2):
                    o = ps[:, 6, i * D:(i + 1) * D]
                    for m in range(NM):
                        mm(o, hids[im][:, m, i * 128:(i + 1) * 128], ffn2[:, m, 0, :], m == 0, False)
                    for c in range(2):
                        t0 = im * NTOK + i * 128
                        last = mm(o, xt[:, c, t0:t0 + 128], ffn2a[:, c, 0, :], False, c == 1)
                last.then_inc(*q.adds("proj_mm"))
                yield

            pe.wait_ge(ld_qkv, 16 * len(loads_qkv))
            pe.wait_ge(set_up, 1)
            jobs = side_a0, side_a1, side_a2, side_a3
            q = Port(sa)
            start_a(q, run, jobs)
            pe.wait_ge(ld_rest, 16 * len(loads_rest))
            with pe.Fori(0, TURNS - 1) as t:
                q.stage(t, t + 1, t, True)
                round_a(q, run, jobs, True)
            q.stage(TURNS - 1, rounds=TURNS - 2)
            round_a(q, run, jobs, False)
            pe.wait_ge(imp_in, 1)
            mm(ps[:, 0, 0:E2], ones[:, :], imp[:, :]).then_inc(imp_mm, 1)
            def over(q):
                pe.wait_ge(*q.next("rows_ready"))
                for c in range(2):
                    n = CH + c
                    for i in range(TT):
                        last = pe.transpose(ps[0:n, c, i * 128:(i + 1) * 128], xn[:, i, c * CH:c * CH + n],
                                            ident[:, :])
                    last.then_inc(*q.adds("turned"))

            def up(q, e):
                for m in range(4):
                    if e:
                        pe.wait_ge(*q.next("h_ready"))
                    for c in range(2):
                        last = mm(ps[:, m, :], moe1[:, c, e, m * 128:(m + 1) * 128], xt[0:CH, c, :],
                                  c == 0, c == 1)
                    last.then_inc(*q.adds("fc1_mm"))

            def down(q, e, more):
                if e + 1 == E2:
                    pe.wait_ge(*q.next("h_ready", 2))
                    if more:
                        over(q)
                    pe.wait_ge(*q.next("h_ready", 2))
                if e == EARLY:
                    pe.wait_ge(ld_late, 16)
                pe.wait_ge(*q.next("acc_done"))
                for i in range(TT):
                    o = ps[:, 4 + 2 * (e % 2) + i // 2, (i % 2) * D:(i % 2 + 1) * D]
                    for m in range(4):
                        last = mm(o, hid2[:, 4 * (e % 2) + m, i * 128:(i + 1) * 128], moe2[:, e, m, :],
                                  m == 0, m == 3)
                last.then_inc(*q.adds("fc2_mm"))

            def experts(q, more):
                wait_xt(q)
                up(q, 0)
                for e in range(E2):
                    if e + 1 < E2:
                        up(q, e + 1)
                    down(q, e, more)

            pe.wait_ge(ld_moe, 32)
            pe.wait_ge(imp_done, 1)
            q = Port(sm)
            over(q)
            pe.sem_inc(*q.adds("fc2_mm"))
            pe.sem_inc(*q.adds("fc2_mm"))
            with pe.Fori(0, TURNS - 1) as t:
                q.stage(t, t + 1, t, True)
                experts(q, True)
            q.stage(TURNS - 1, rounds=TURNS - 2)
            experts(q, False)

            pe.wait_ge(ld_b, 16 * len(loads_b))
            jobs = side_b0, side_b1, side_b2
            q = Port(sbb)
            start_b(q, run, jobs)
            pe.wait_ge(ld_ffn, 16 * len(loads_ffn))
            pe.wait_ge(ffn2_summed, 1)
            with pe.Fori(0, TURNS - 1) as t:
                q.stage(t, t + 1, t, True)
                round_b(q, run, jobs, True)
            q.stage(TURNS - 1, rounds=TURNS - 2)
            round_b(q, run, jobs, False)

        @block.scalar
        def _(act):
            def xt0(q, im, w=None):
                act.wait_ge(*q.next("turned", 1))
                q.passed("turned", 1)
                dst, src = xt[0:CH, 0, im * NTOK:(im + 1) * NTOK], ps[0:CH, 6, 0:NTOK]
                sc = {} if w is None else {"scale": cols[0:CH, 0, w:w + 1], "bias": cols[0:CH, 0, w + 1:w + 2]}
                f = ACT.Copy if w is None else ACT.Identity
                ins = act.activation(dst, src, f, **sc)
                if w == 0:
                    for z, pk in by_window(src, xp[0:CH, 0, :]):
                        ins = act.activation(pk, z, f, **sc)
                ins.then_inc(*q.adds("xt0_ready"))

            def qkv(q, l, im):
                sc = 1 if l is L3 else 0
                act.wait_ge(*q.next("q01_mm"))
                dst = qn[:, :, :] if l.pad else qt[:, im]
                act.activation(dst[:, 0:2, :].rearrange("p s t -> p (s t)"), ps[:, 6, :], ACT.Copy)\
                    .then_inc(*q.adds("q01_ready"))
                yield
                act.wait_ge(*q.next("k12_mm"))
                for c in range(2):
                    ins = act.activation(kz[:, im, c, 1:3, :].rearrange("p s t -> p (s t)"), ps[:, 6, :], ACT.Copy,
                                         scale=par[:, sc, c:c + 1])
                ins.then_inc(*q.adds("k12_ready"))
                yield
                if l.pad:
                    yield
                if l.rel:
                    for half in range(2):
                        act.wait_ge(*q.next("rel_mm"))
                        src = ps[0:64, 6 + half, 0:QUADS * 128].rearrange("p (s t) -> p s t", s=QUADS)
                        dst = relt[0:64, im, :, half * 128:(half + 1) * 128]
                        if l.pad:
                            n = 8 - 2 * half
                            src = src.rearrange("p s (h w) -> p s h w", h=8)[:, :, 0:n, 0:WS]
                            dst = relt[0:64, im, :, 8 * half * WS:(8 * half + n) * WS]
                            dst = dst.rearrange("p s (h w) -> p s h w", h=n)
                        ins = act.activation(dst, src, ACT.Copy)
                    ins.then_inc(*q.adds("rel0_ready"))
                    yield

            def attention(q, l):
                n = len(l.tiles)

                def keep_turned(i):
                    if q.behind("pt_mm", i + 1):
                        act.wait_ge(*q.to("pt_mm", i + 1))
                    if i >= PV_LAG:
                        if q.behind("pv_mm", i - PV_LAG + 1):
                            act.wait_ge(*q.to("pv_mm", i - PV_LAG + 1))
                    bank = ps[:, 3 + i % 2, :]
                    if l.tiles[i][1]:
                        act.activation(pt[0:EDGE, i % PV_LAG, 0:EDGE], bank[0:EDGE, 0:EDGE], ACT.Copy)
                        ins = act.activation(pt[0:98, i % PV_LAG, EDGE:3 * EDGE], bank[0:98, EDGE:3 * EDGE], ACT.Copy)
                    else:
                        m, k = (HALF0, 4 * HALF0) if l.pad else (128, NTOK + 128 if l.causal else T)
                        ins = act.activation(pt[0:m, i % PV_LAG, 0:k], bank[0:m, 0:k], ACT.Copy)
                    ins.then_inc(*q.adds("pt_done"))

                def step(i):
                    if i == 0:
                        q.mark()
                    if TURN_LAG <= i < n + TURN_LAG and l.act_keeps:
                        keep_turned(i - TURN_LAG)
                    if i < n:
                        if q.behind("max_done", i + 1):
                            act.wait_ge(*q.to("max_done", i + 1))
                        if i >= P_RING:
                            if q.behind("pt_mm", i - P_RING + 1):
                                act.wait_ge(*q.to("pt_mm", i - P_RING + 1))
                        bank = ps[:, i % RING, :]
                        if l.tiles[i][1]:
                            parts = [(EDGE, 0, NTOK, 0)]
                        elif l.pad:
                            parts = [(HALF0, 0, INNER, 0), (HALF0, INNER, INNER, 1)]
                        elif l.causal:
                            parts = [(128, 0, NTOK, 0), (128, NTOK, 128, 1)]
                        else:
                            parts = [(128, 0, NTOK, 0), (128, NTOK, NTOK, 1)]
                        for m, at, k, c in parts:
                            ins = act.activation(p[0:m, i % P_RING, at:at + k], bank[0:m, at:at + k], ACT.Exp,
                                                 bias=negmax[0:m, i % P_RING, c:c + 1])
                        ins.then_inc(*q.adds("exp_done"))
                    if i == n + PV_LAG - 1:
                        act.wait_ge(*q.to("pv_mm", n))
                        quads01 = ps[:, 2, :].rearrange("p (s t) -> p s t", s=2)
                        quad2 = ps[:, 5, 0:NTOK].rearrange("p (s t) -> p s t", s=1)
                        for dst, src in ((ou[:, 0:2, :], quads01), (ou[:, 2:3, :], quad2)):
                            for z, pk in by_window(dst, src) if l.pad else [(dst, src)]:
                                ins = act.activation(z, pk, ACT.Copy)
                        ins.then_inc(*q.adds("at_ready"))
                        q.ended(("max_done", "pt_mm", "pv_mm"), n)
                return step

            def run(q, l, im, side, hops):
                slot(len(l.tiles) + PV_LAG, attention(q, l), side, hops)

            def hidden(q, z, func):
                for m in range(0, NM, 2):
                    act.wait_ge(*q.next("fc1_mm"))
                    act.activation(z[:, m:m + 2, :].rearrange("p m t -> p (m t)"), ps[:, 6 + m // 2 % 2, :],
                                   func).then_inc(*q.adds("h_ready"))
                yield

            def gate_exp(q, im):
                act.wait_ge(*q.next("gate_in"))
                act.activation(ge[:, 2 * im:2 * im + 2, :], gl[:, 2 * im:2 * im + 2, :], ACT.Exp)\
                    .then_inc(*q.adds("gate_exp"))
                yield

            def side_a0(q, im):
                yield
                xt0(q, im, 0)
                yield
                yield from qkv(q, L0, im)

            def side_a1(q, im):
                yield
                xt0(q, im)
                yield
                yield
                xt0(q, im, 2)
                yield
                yield from hidden(q, hid, ACT.Gelu)
                yield
                yield
                yield
                act.wait_ge(*q.next("stat_ready", 3))
                act.activation(xt[0:CH, 0, im * NTOK:(im + 1) * NTOK], ps[0:CH, 6, 0:NTOK], ACT.Identity,
                               scale=gsc[0:CH, 0:1], bias=gbi[0:CH, 0:1]).then_inc(*q.adds("xt0_ready"))
                q.passed("turned", 2)
                yield
                yield from qkv(q, L1, im)

            def side_a2(q, im):
                yield
                xt0(q, im)
                yield
                yield
                xt0(q, im)
                yield
                yield from qkv(q, L2, im)

            def side_a3(q, im):
                yield
                xt0(q, im)
                yield
                yield
                xt0(q, im)
                yield
                yield from gate_exp(q, im)

            def side_b0(q, im):
                yield
                xt0(q, im)
                yield
                yield from qkv(q, L3, im)

            def side_b1(q, im):
                yield
                xt0(q, im)
                yield
                yield
                xt0(q, im)
                yield
                yield from gate_exp(q, im)
                for _ in range(4):
                    yield
                xt0(q, im)
                yield
                yield from hidden(q, hids[im], ACT.Gelu)
                yield from qkv(q, L4, im)

            def side_b2(q, im):
                yield
                xt0(q, im)
                yield
                yield

            act.wait_ge(ld_qkv, 16 * len(loads_qkv))
            act.wait_ge(set_up, 1)
            jobs = side_a0, side_a1, side_a2, side_a3
            q = Port(sa)
            start_a(q, run, jobs)
            with act.Fori(0, TURNS - 1) as t:
                q.stage(t, t + 1, t, True)
                round_a(q, run, jobs, True)
            q.stage(TURNS - 1, rounds=TURNS - 2)
            round_a(q, run, jobs, False)
            def over(q):
                act.wait_ge(*q.next("turned"))
                q.passed("turned", 1)
                act.activation(xt[0:CH, 0, :], ps[0:CH, 0, :], ACT.Copy).then_inc(*q.adds("xt0_ready"))

            def experts(q, more):
                for e in range(E2):
                    for m in range(4):
                        act.wait_ge(*q.next("fc1_mm"))
                        if m == 0:
                            act.wait_ge(*q.next("fc2_mm"))
                        act.activation(hid2[:, 4 * (e % 2) + m, :], ps[:, m, :], ACT.Silu).then_inc(*q.adds("h_ready"))
                if more:
                    over(q)

            q = Port(sm)
            over(q)
            with act.Fori(0, TURNS - 1) as t:
                q.stage(t, t + 1, t, True)
                experts(q, True)
            q.stage(TURNS - 1, rounds=TURNS - 2)
            experts(q, False)
            act.wait_ge(set_b, 1)
            jobs = side_b0, side_b1, side_b2
            q = Port(sbb)
            start_b(q, run, jobs)
            with act.Fori(0, TURNS - 1) as t:
                q.stage(t, t + 1, t, True)
                round_b(q, run, jobs, True)
            q.stage(TURNS - 1, rounds=TURNS - 2)
            round_b(q, run, jobs, False)

        @block.gpsimd
        def _(pool):
            def rstds(q, n):
                for _ in range(n):
                    pool.wait_ge(*q.next("var_ready"))
                    pool.tensor_tensor(rstd[:, :], ve[:, :], nhalf[:, :], ALU.pow).then_inc(*q.adds("rstd_ready"))

            def pack(q, im):
                pool.wait_ge(*q.next("q01_ready"))
                pool.wait_ge(*q.next("q2k0_ready"))
                pool.sem_inc(*q.adds("waited"))
                for z, pk in by_window(qn[:, :, :], qt[:, im, :, :]):
                    pool.tensor_copy(pk, z)
                pool.wait_ge(*q.next("k12_ready"))
                pool.sem_inc(*q.adds("waited"))
                for c in range(2):
                    z = kz[:, im, c, :, :].rearrange("p s (h w) -> p s h w", h=HH)
                    pool.tensor_copy(ke[:, im, c, :, 0:EB].rearrange("p s (h w) -> p s h w", h=WS),
                                     z[:, :, 0:WS, WS:WW])
                    ins = pool.tensor_copy(ke[:, im, c, :, EB:EDGE], kz[:, im, c, :, WS * WW:NTOK])
                ins.then_inc(*q.adds("edge_ready"))

            def first_norms(q):
                rstds(q, 1)
                pack(q, 0)
                rstds(q, 2 if q.looping else 1)
                pack(q, 1)

            pool.wait_ge(set_up, 1)
            q = Port(sa)
            first_norms(q)
            with pool.Fori(0, TURNS - 1) as t:
                q.stage(t, t + 1, t, True)
                rstds(q, 2 * 2 + 1 * 2 + 1)
                for name in ("q01_ready", "q2k0_ready", "k12_ready"):
                    q.passed(name, 2 * IMGS)
                first_norms(q)
            q.stage(TURNS - 1, rounds=TURNS - 2)
            rstds(q, 2 * 2 + 1 * 2 + 1 * 2)
            q = Port(sm)
            rstds(q, 1)
            with pool.Fori(0, TURNS - 1) as t:
                q.stage(t, t + 1, t, True)
                rstds(q, 1)
            q = Port(sbb)
            rstds(q, 2)
            with pool.Fori(0, TURNS - 1) as t:
                q.stage(t, t + 1, t, True)
                rstds(q, 2 * 2 + 2)
            q.stage(TURNS - 1, rounds=TURNS - 2)
            rstds(q, 2 * 2)

        @block.vector
        def _(dve):
            def norm(q, tiles, src, dst, eps, signal=None):
                i0 = tiles[0]
                for i in tiles:
                    ins = dve.bn_stats(stats[:, i, :], src[:, i, 0:D])
                ins.then_inc(*q.adds("dve_step"))
                dve.wait_ge(*q.own("dve_step"))
                for i in tiles:
                    ins = dve.bn_aggr(mv[:, i, :], stats[:, i, :])
                ins.then_inc(*q.adds("dve_step"))
                dve.wait_ge(*q.own("dve_step"))
                dve.tensor_scalar(ve[:, i0:i0 + len(tiles)], mv[:, i0:i0 + len(tiles), 1], eps, None, ALU.add)\
                    .then_inc(*q.adds("var_ready"))
                dve.wait_ge(*q.next("rstd_ready"))
                for i in tiles:
                    ins = dve.tensor_scalar(dst[:, i, 0:D], src[:, i, 0:D], mv[:, i, 0:1], rstd[:, i:i + 1],
                                            ALU.subtract, ALU.mult)
                if signal:
                    ins.then_inc(*q.adds(signal))
                else:
                    ins.then_inc(*q.adds("dve_step"))
                    dve.wait_ge(*q.own("dve_step"))

            def tiles_of(im):
                return [2 * im, 2 * im + 1]

            def xt1(q, im, w=None):
                dve.wait_ge(*q.next("turned", 2))
                dst, src = xt[:, 1, im * NTOK:(im + 1) * NTOK], ps[0:CH + 1, 7, 0:NTOK]

                def move(o, i):
                    if w is None:
                        return dve.tensor_copy(o, i)
                    return dve.tensor_scalar(o, i, cols[:, 1, w:w + 1], cols[:, 1, w + 1:w + 2], ALU.mult, ALU.add)
                ins = move(dst, src)
                if w == 0:
                    for z, pk in by_window(src, xp[:, 1, :]):
                        ins = move(pk, z)
                ins.then_inc(*q.adds("xt1_ready"))

            def divide(q):
                dve.wait_ge(*q.next("back_mm"))
                z = ps[:, 6:8, 0:QUADS * 128].rearrange("p i (h d) -> p i h d", h=HEADS)
                dve.reciprocal(rsum[:, :, :], z[:, :, :, HD]).then_inc(*q.adds("dve_step"))
                dve.wait_ge(*q.own("dve_step"))
                dve.tensor_tensor(att[:, :, 0:D].rearrange("p i (h d) -> p i h d", h=HEADS), z[:, :, :, 0:HD],
                                  rsum[:, :, :].unsqueeze(3).to_broadcast([128, 2, HEADS, HD]),
                                  ALU.mult).then_inc(*q.adds("div_done"))

            def qkv(q, l, im):
                sc = 1 if l is L3 else 0
                dve.wait_ge(*q.next("q2k0_mm"))
                dve.tensor_copy((qn if l.pad else qt[:, im])[:, 2, :], ps[:, 7, 0:NTOK])
                for c in range(2):
                    ins = dve.tensor_scalar(kz[:, im, c, 0, :], ps[:, 7, NTOK:T], par[:, sc, c:c + 1], None, ALU.mult)
                ins.then_inc(*q.adds("q2k0_ready"))
                yield
                dve.wait_ge(*q.next("v_mm"))
                m = HALF0 if l.pad else 128
                dve.tensor_copy(v[0:m, im, 0:2, :, 0:HD],
                                ps[0:m, 7, 0:2 * D].rearrange("p (i h d) -> p i h d", i=2, h=HEADS))\
                                    .then_inc(*q.adds("v_ready"))
                yield
                if l.pad:
                    dve.wait_ge(*q.next("v_mm"))
                    dve.tensor_copy(v[0:EDGE, im, 2, :, 0:HD],
                                    ps[0:EDGE, 6, 0:D].rearrange("p (h d) -> p h d", h=HEADS))\
                                        .then_inc(*q.adds("v_ready"))
                    yield
                if l.rel:
                    if q.starting and im == 0:
                        dve.wait_ge(ld_rel, 16 * len(loads_rel))
                        dve.tensor_copy(tri16[:, :], tri[:, :])
                        dve.tensor_copy(ident16[:, :], ident[:, :])
                        dve.tensor_scalar(kpadz, kpadz, L0.scale, None, ALU.mult).then_inc(const_ready, 1)
                    dve.wait_ge(*q.next("rel_mm"))
                    c0, c1 = (ps[64:128, b, 0:QUADS * 128].rearrange("p (s h w) -> p s h w", s=QUADS, h=HH)
                              for b in (6, 7))
                    if not l.pad:
                        dst = relt[64:128, im, :, :].rearrange("p s (h w) -> p s h w", h=HH)
                        dve.tensor_copy(dst[:, :, :, 0:8], c0)
                        dve.wait_ge(*q.next("rel_mm"))
                        ins = dve.tensor_copy(dst[:, :, :, 8:16], c1)
                        q.passed("rel0_ready", 1)
                    else:
                        inner = relt[64:128, im, :, 0:INNER].rearrange("p s (h w) -> p s h w", h=WS)
                        dve.tensor_copy(inner[:, :, :, 0:8], c0[:, :, 0:WS, :])
                        dve.wait_ge(*q.next("rel_mm"))
                        dve.tensor_copy(inner[:, :, :, 8:WS], c1[:, :, 0:WS, 0:WS - 8])

                        def edge(r, z, hs, ws, below):
                            at, n, w = (INNER + EB, 2, WW) if below else (INNER, WS, 2)
                            dst = relt[r, im, :, at:at + n * w].rearrange("p s (h w) -> p s h w", h=n)[:, :, hs, ws]
                            wr = winrow[r, at - INNER:at - INNER + n * w].rearrange("p (h w) -> p h w", h=n)
                            wr = wr[:, hs, ws].unsqueeze(1).to_broadcast([64, QUADS] + list(z.shape[2:]))
                            return dve.tensor_tensor(dst, z, wr, ALU.add)
                        up, lo = slice(64, 128), slice(0, 64)
                        edge(up, c0[:, :, WS:, :], slice(0, 2), slice(0, 8), True)
                        edge(up, c1[:, :, WS:, :], slice(0, 2), slice(8, 16), True)
                        edge(up, c1[:, :, 0:WS, WS - 8:], slice(0, WS), slice(0, 2), False)
                        dve.wait_ge(*q.next("rel0_ready"))
                        r0, r1 = (ps[lo, b, 0:QUADS * 128].rearrange("p (s h w) -> p s h w", s=QUADS, h=8)
                                  for b in (6, 7))
                        edge(lo, r0[:, :, :, WS:], slice(0, 8), slice(0, 2), False)
                        edge(lo, r1[:, :, 0:6, WS:], slice(8, WS), slice(0, 2), False)
                        ins = edge(lo, r1[:, :, 6:8, :], slice(0, 2), slice(0, WW), True)
                    ins.then_inc(*q.adds("rel1_ready"))
                    yield

            def attention(q, l):
                n = len(l.tiles)

                def row_max(i):
                    if q.behind("sc_mm", i + 1):
                        dve.wait_ge(*q.to("sc_mm", i + 1))
                    bank = ps[:, i % RING, :]
                    if l.tiles[i][1]:
                        parts = [(EDGE, bank[0:EDGE, 0:NTOK], 0, 1)]
                    elif l.pad:
                        parts = [(HALF0, bank[0:HALF0, 0:2 * INNER].rearrange("p (h k) -> p h k", h=2), 0, 2)]
                    elif l.causal:
                        parts = [(128, bank[:, 0:NTOK], 0, 1), (128, bank[:, NTOK:NTOK + 128], 1, 1)]
                    else:
                        parts = [(128, bank.rearrange("p (h k) -> p h k", h=2), 0, 2)]
                    for m, z, c, k in parts:
                        ins = dve.tensor_reduce(negmax[0:m, i % P_RING, c:c + k], z, AX.X, ALU.max, negate=True)
                    ins.then_inc(*q.adds("max_done"))

                def keep_turned(i):
                    if q.behind("pt_mm", i + 1):
                        dve.wait_ge(*q.to("pt_mm", i + 1))
                    if i >= PV_LAG:
                        if q.behind("pv_mm", i - PV_LAG + 1):
                            dve.wait_ge(*q.to("pv_mm", i - PV_LAG + 1))
                    bank = ps[:, 3 + i % 2, :]
                    if l.tiles[i][1]:
                        dve.tensor_copy(pt[0:EDGE, i % PV_LAG, 0:EDGE], bank[0:EDGE, 0:EDGE])
                        ins = dve.tensor_copy(pt[0:98, i % PV_LAG, EDGE:3 * EDGE], bank[0:98, EDGE:3 * EDGE])
                    else:
                        m, k = (HALF0, 4 * HALF0) if l.pad else (128, NTOK + 128 if l.causal else T)
                        ins = dve.tensor_copy(pt[0:m, i % PV_LAG, 0:k], bank[0:m, 0:k])
                    ins.then_inc(*q.adds("pt_done"))

                def step(i):
                    if i == 0:
                        q.mark()
                    if i < n:
                        row_max(i)
                    if TURN_LAG <= i < n + TURN_LAG and not l.act_keeps:
                        keep_turned(i - TURN_LAG)
                    if i == n + PV_LAG - 1:
                        q.ended(("sc_mm", "pt_mm", "pv_mm"), n)
                return step

            def run(q, l, im, side, hops):
                slot(len(l.tiles) + PV_LAG, attention(q, l), side, hops)

            def residual(q, name, im):
                dve.wait_ge(*q.next(name))
                dst = x[:, 2 * im:2 * im + 2, 0:D]
                return dve.tensor_tensor(dst, ps[:, 6, 0:2 * D].rearrange("p (i d) -> p i d", i=2), dst, ALU.add)

            def probabilities(q, n, im):
                i2 = slice(2 * im, 2 * im + 2)
                dve.wait_ge(*q.next("gate_mm"))
                lg = ps[:, 6, 0:2 * n].rearrange("p (i e) -> p i e", i=2)
                dve.tensor_reduce(gm[:, i2], lg, AX.X, ALU.max).then_inc(*q.adds("dve_step"))
                dve.wait_ge(*q.own("dve_step"))
                dve.tensor_tensor(gl[:, i2, 0:n], lg, gm[:, i2].unsqueeze(2).to_broadcast([128, 2, n]),
                                  ALU.subtract).then_inc(*q.adds("gate_in"))
                dve.wait_ge(*q.next("gate_exp"))
                dve.tensor_reduce(gs[:, i2], ge[:, i2, 0:n], AX.X, ALU.add).then_inc(*q.adds("dve_step"))
                dve.wait_ge(*q.own("dve_step"))
                dve.reciprocal(gs[:, i2], gs[:, i2]).then_inc(*q.adds("dve_step"))
                dve.wait_ge(*q.own("dve_step"))
                return gs[:, i2].unsqueeze(2).to_broadcast([128, 2, n])

            def side_a0(q, im):
                dve.sem_inc(*q.adds("waited"))
                dve.tensor_copy(x[:, 2 * im:2 * im + 2, 0:D], image_x(q.coming, im)).then_inc(*q.adds("dve_step"))
                dve.wait_ge(*q.own("dve_step"))
                norm(q, tiles_of(im), x, xn, 1e-5, "rows_ready")
                yield
                xt1(q, im, 0)
                yield
                yield from qkv(q, L0, im)

            def side_a1(q, im):
                divide(q)
                yield
                xt1(q, im)
                yield
                residual(q, "proj_mm", im).then_inc(*q.adds("dve_step"))
                dve.wait_ge(*q.own("dve_step"))
                norm(q, tiles_of(im), x, xn, 1e-5, "rows_ready")
                yield
                xt1(q, im, 2)
                yield
                yield
                residual(q, "fc2_mm", im).then_inc(*q.adds("rows_ready"))
                yield
                dve.wait_ge(*q.next("turned", 2))
                for c in range(2):
                    ins = dve.bn_stats(stats[0:CH, c, :], ps[0:CH, 6 + c, 0:NTOK])
                ins.then_inc(*q.adds("dve_step"))
                dve.wait_ge(*q.own("dve_step"))
                for c in range(2):
                    ins = dve.bn_aggr(mv[0:CH, c, :], stats[0:CH, c, :])
                ins.then_inc(*q.adds("dve_step"))
                dve.wait_ge(*q.own("dve_step"))
                dve.tensor_copy(gst[:, 0, :], mv[0:CH, 0:2, 0]).then_inc(*q.adds("stat_ready"))
                yield
                gmean, gvar = ps[0:CH, 6, NTOK:NTOK + 2], ps[0:CH, 6, NTOK + 2:NTOK + 4]
                dve.wait_ge(*q.next("stat_mm"))
                dve.tensor_tensor(gbi[0:CH, :], gst[:, 0, :], gmean, ALU.subtract).then_inc(*q.adds("dve_step"))
                dve.wait_ge(*q.own("dve_step"))
                dve.tensor_tensor(gbi[0:CH, :], gbi[0:CH, :], gbi[0:CH, :], ALU.mult).then_inc(*q.adds("dve_step"))
                dve.wait_ge(*q.own("dve_step"))
                dve.tensor_tensor(gst[:, 1, :], gbi[0:CH, :], mv[0:CH, 0:2, 1], ALU.add).then_inc(*q.adds("stat_ready"))
                yield
                dve.wait_ge(*q.next("stat_mm"))
                dve.tensor_scalar(ve[0:CH, 0:2], gvar, 1e-5, None, ALU.add).then_inc(*q.adds("var_ready"))
                dve.wait_ge(*q.next("rstd_ready"))
                dve.tensor_copy(gsc[0:CH, :], rstd[0:CH, 0:2]).then_inc(*q.adds("dve_step"))
                dve.wait_ge(*q.own("dve_step"))
                dve.scalar_tensor_tensor(out=gbi[0:CH, :], in0=gmean, scalar=-1.0, in1=gsc[0:CH, :],
                                         op0=ALU.mult, op1=ALU.mult).then_inc(*q.adds("stat_ready"))
                dve.wait_ge(*q.next("stat_ready", 3))
                dve.tensor_scalar(xt[:, 1, im * NTOK:(im + 1) * NTOK], ps[0:CH + 1, 7, 0:NTOK],
                                  gsc[:, 1:2], gbi[:, 1:2], ALU.mult, ALU.add).then_inc(*q.adds("xt1_ready"))
                yield
                yield from qkv(q, L1, im)

            def side_a2(q, im):
                divide(q)
                yield
                xt1(q, im)
                yield
                residual(q, "proj_mm", im).then_inc(*q.adds("dve_step"))
                dve.wait_ge(*q.own("dve_step"))
                norm(q, tiles_of(im), x, xn, 1e-5, "rows_ready")
                yield
                xt1(q, im)
                yield
                yield from qkv(q, L2, im)

            def side_a3(q, im):
                divide(q)
                yield
                xt1(q, im)
                yield
                residual(q, "proj_mm", im).then_inc(*q.adds("dve_step"))
                dve.wait_ge(*q.own("dve_step"))
                dve.tensor_copy(image_x(q.turn, im), x[:, 2 * im:2 * im + 2, 0:D])
                norm(q, tiles_of(im), x, xn, 1e-5, "rows_ready")
                yield
                xt1(q, im)
                yield
                r = probabilities(q, E2, im)
                dve.tensor_tensor(pall[:, bass.ds(q.turn * TT + 2 * im, 2), :], ge[:, 2 * im:2 * im + 2, :], r,
                                  ALU.mult).then_inc(*q.adds("turn_end"))
                yield

            def side_b0(q, im):
                dve.sem_inc(*q.adds("waited"))
                dve.tensor_copy(x[:, 2 * im:2 * im + 2, 0:D], image_x(q.coming, im)).then_inc(*q.adds("dve_step"))
                dve.wait_ge(*q.own("dve_step"))
                norm(q, tiles_of(im), x, xn, 1e-5, "rows_ready")
                q.passed("rows_ready", 1)
                yield
                xt1(q, im)
                yield
                yield from qkv(q, L3, im)

            def side_b1(q, im):
                i2 = slice(2 * im, 2 * im + 2)
                divide(q)
                yield
                xt1(q, im)
                yield
                residual(q, "proj_mm", im).then_inc(*q.adds("dve_step"))
                dve.wait_ge(*q.own("dve_step"))
                norm(q, tiles_of(im), x, lx, 1e-5, "rows_ready")
                yield
                xt1(q, im)
                yield
                r = probabilities(q, E3, im)
                dve.tensor_tensor(p4[:, :, :], ge[:, i2, 0:E3], r, ALU.mult).then_inc(*q.adds("choice_in"))
                yield
                dve.wait_ge(*q.next("rows_ready"))
                norm(q, tiles_of(im), lx, yb, 1e-6)
                yield
                dve.wait_ge(*q.next("choice_mm"))
                for e in range(E3):
                    if e == 2:
                        yield
                    row = ps[:, 6 + e // 2, (e % 2) * NTOK:(e % 2 + 1) * NTOK]
                    dve.scalar_tensor_tensor(out=ahead[:, e, 0:2, :], in0=row, scalar=p4[:, 0, e:e + 1],
                                             in1=ties[:, 0, :], op0=ALU.is_le, op1=ALU.mult)
                    dve.scalar_tensor_tensor(out=ahead[:, e, 2, :], in0=row[:, 0:128], scalar=p4[:, 0, e:e + 1],
                                             in1=ties[:, 1, 128:NTOK], op0=ALU.is_lt, op1=ALU.mult)
                    dve.scalar_tensor_tensor(out=ahead[:, e, 3, :], in0=row[:, 128:NTOK],
                                             scalar=p4[:, 1, e:e + 1], in1=ties[:, 0, 0:128],
                                             op0=ALU.is_le, op1=ALU.mult)
                    ins = dve.scalar_tensor_tensor(out=ahead[:, e, 4:6, :], in0=row, scalar=p4[:, 1, e:e + 1],
                                                   in1=ties[:, 1, :], op0=ALU.is_lt, op1=ALU.mult)
                ins.then_inc(*q.adds("choice_in"))
                g3 = gb3[:, :, :].unsqueeze(2).to_broadcast([128, 2, 2, D])
                dve.tensor_tensor(yb[:, i2, :], yb[:, i2, :], g3[:, 0], ALU.mult).then_inc(*q.adds("dve_step"))
                dve.wait_ge(*q.own("dve_step"))
                dve.tensor_tensor(yb[:, i2, :], yb[:, i2, :], g3[:, 1], ALU.add).then_inc(*q.adds("dve_step"))
                dve.wait_ge(*q.own("dve_step"))
                yield
                dve.wait_ge(*q.next("choice_mm"))
                dve.tensor_scalar(sel[:, :, :], ps[:, 6, 0:2 * E3].rearrange("p (f e) -> p f e", f=2), float(CAP),
                                  None, ALU.is_lt).then_inc(*q.adds("dve_step"))
                dve.wait_ge(*q.own("dve_step"))
                g = gate[:, im]
                dve.tensor_tensor(g, sel[:, :, :], p4[:, :, :], ALU.mult).then_inc(*q.adds("dve_step"))
                dve.wait_ge(*q.own("dve_step"))
                for e in range(E3 - 2, -1, -1):
                    for z in (sel[:, :, :], g):
                        ins = dve.tensor_tensor(z[:, :, e], z[:, :, e], z[:, :, e + 1], ALU.add)
                    ins.then_inc(*q.adds("dve_step"))
                    dve.wait_ge(*q.own("dve_step"))
                dve.tensor_copy(xg[:, i2, D], sel[:, :, 0])
                for e, (c0, c1) in enumerate(SEGS):
                    ins = dve.tensor_tensor(xg[:, i2, c0:c1], yb[:, i2, c0:c1],
                                            sel[:, :, e:e + 1].to_broadcast([128, 2, c1 - c0]), ALU.mult)
                ins.then_inc(*q.adds("rows_ready"))
                q.passed("rows_ready", 1)
                yield
                xt1(q, im)
                yield
                yield
                yield from qkv(q, L4, im)

            def side_b2(q, im):
                i2 = slice(2 * im, 2 * im + 2)
                divide(q)
                yield
                xt1(q, im)
                dve.tensor_tensor(x[:, i2, 0:D], x[:, i2, 0:D], lx[:, i2, 0:D], ALU.add).then_inc(*q.adds("dve_step"))
                dve.wait_ge(*q.own("dve_step"))
                yield
                dve.wait_ge(*q.next("proj_mm"))
                for e, (c0, c1) in enumerate(SEGS):
                    ins = dve.tensor_tensor(yb[:, i2, c0:c1],
                                            ps[:, 6, 0:2 * D].rearrange("p (i d) -> p i d", i=2)[:, :, c0:c1],
                                            gate[:, im, :, e:e + 1].to_broadcast([128, 2, c1 - c0]), ALU.mult)
                ins.then_inc(*q.adds("dve_step"))
                dve.wait_ge(*q.own("dve_step"))
                dve.tensor_tensor(image_x(q.turn, im), x[:, i2, 0:D], yb[:, i2, :], ALU.add)\
                    .then_inc(*q.adds("turn_end"))
                dve.wait_ge(*q.next("turn_end"))
                yield

            dve.memset(nhalf[:, :], -0.5)
            dve.memset(ve[:, :], 1.0)
            dve.memset(ones[:, :], 1.0)
            dve.memset(ones16[:, :], 1.0)
            for e in range(E2):
                dve.memset(order[:, e:e + 1], float(E2 - e))
            for z in (x, xn, att):
                dve.memset(z[:, :, D:D + 1], 1.0)
            dve.memset(xt[CH:CH + 1, 0, :], 0.0)
            dve.memset(xp[CH:CH + 1, 0, :], 0.0)
            dve.memset(gsc[CH:CH + 1, :], 1.0)
            dve.memset(gbi[CH:CH + 1, :], 0.0)
            dve.memset(gl[:, :, :], 0.0)
            dve.memset(v[:, :, :, :, HD:VW], 1.0).then_inc(set_up, 1)
            dve.wait_ge(ld_qkv, 16 * len(loads_qkv))
            dve.wait_ge(ld_x, 16)
            jobs = side_a0, side_a1, side_a2, side_a3
            q = Port(sa)
            start_a(q, run, jobs)
            dve.wait_ge(ld_rest, 16 * len(loads_rest))
            dve.wait_ge(ld_x_rest, 16)
            with dve.Fori(0, TURNS - 1) as t:
                q.stage(t, t + 1, t, True)
                dve.sem_clear(q.s.sem["dve_step"])
                round_a(q, run, jobs, True)
            q.stage(TURNS - 1, rounds=TURNS - 2)
            dve.sem_clear(q.s.sem["dve_step"])
            round_a(q, run, jobs, False)

            dve.wait_ge(sa.sem["turn_end"], TURNS * IMGS)
            dve.tensor_reduce(imp[:, :], pall[:, :, :].rearrange("p t e -> p e t"), AX.X, ALU.add)\
                .then_inc(imp_in, 1)
            dve.wait_ge(imp_mm, 1)
            dve.tensor_scalar(rrun[:, :], ps[:, 0, 0:E2], 1.0, 1.0 - 0.9, ALU.subtract, ALU.mult)\
                .then_inc(imp_step, 1)
            dve.wait_ge(imp_step, 1)
            dve.tensor_scalar(imp[:, :], rrun[:, :], 1.0, 0.01, ALU.add, ALU.add).then_inc(imp_step, 1)
            dve.wait_ge(imp_step, 2)
            dve.reciprocal(rrun[:, :], imp[:, :]).then_inc(imp_done, 1)
            dve.wait_ge(imp_done, 1)
            ob = order[:, :].unsqueeze(1).to_broadcast([128, TT, E2])
            def over(q):
                dve.wait_ge(*q.next("turned", 2))
                dve.tensor_copy(xt[:, 1, :], ps[0:CH + 1, 1, :]).then_inc(*q.adds("xt1_ready"))

            def gates(q):
                dve.tensor_copy(gl[:, :, :], pall[:, bass.ds(q.turn * TT, TT), :]).then_inc(*q.adds("dve_step"))
                dve.wait_ge(*q.own("dve_step"))
                dve.tensor_copy(cw[:, :, :], gl[:, :, :]).then_inc(*q.adds("dve_step"))
                dve.wait_ge(*q.own("dve_step"))
                for k in range(2):
                    dve.tensor_reduce(gm[:, :], cw[:, :, :], AX.X, ALU.max).then_inc(*q.adds("dve_step"))
                    dve.wait_ge(*q.own("dve_step"))
                    gmb = gm[:, :].unsqueeze(2).to_broadcast([128, TT, E2])
                    dve.tensor_tensor(oh[:, k], cw[:, :, :], gmb, ALU.is_equal).then_inc(*q.adds("dve_step"))
                    dve.wait_ge(*q.own("dve_step"))
                    dve.tensor_tensor(oh[:, k], oh[:, k], ob, ALU.mult).then_inc(*q.adds("dve_step"))
                    dve.wait_ge(*q.own("dve_step"))
                    dve.tensor_reduce(gm[:, :], oh[:, k], AX.X, ALU.max).then_inc(*q.adds("dve_step"))
                    dve.wait_ge(*q.own("dve_step"))
                    dve.tensor_tensor(oh[:, k], ob, gmb, ALU.is_equal).then_inc(*q.adds("dve_step"))
                    dve.wait_ge(*q.own("dve_step"))
                    if k == 0:
                        dve.scalar_tensor_tensor(out=cw[:, :, :], in0=oh[:, 0], scalar=-2.0,
                                                  in1=cw[:, :, :], op0=ALU.mult, op1=ALU.add)\
                                                      .then_inc(*q.adds("dve_step"))
                        dve.wait_ge(*q.own("dve_step"))
                dve.tensor_tensor(oh[:, 2], oh[:, 0], oh[:, 1], ALU.add).then_inc(*q.adds("dve_step"))
                dve.wait_ge(*q.own("dve_step"))
                dve.tensor_tensor(cw[:, :, :], oh[:, 2], gl[:, :, :], ALU.mult).then_inc(*q.adds("dve_step"))
                dve.wait_ge(*q.own("dve_step"))
                dve.tensor_tensor(cw[:, :, :], cw[:, :, :],
                                   rrun[:, :].unsqueeze(1).to_broadcast([128, TT, E2]), ALU.mult)\
                                       .then_inc(*q.adds("dve_step"))
                dve.wait_ge(*q.own("dve_step"))
                dve.tensor_reduce(gs[:, :], cw[:, :, :], AX.X, ALU.add).then_inc(*q.adds("dve_step"))
                dve.wait_ge(*q.own("dve_step"))
                dve.reciprocal(gs[:, :], gs[:, :]).then_inc(*q.adds("dve_step"))
                dve.wait_ge(*q.own("dve_step"))
                dve.tensor_tensor(cw[:, :, :], cw[:, :, :],
                                   gs[:, :].unsqueeze(2).to_broadcast([128, TT, E2]), ALU.mult)\
                                       .then_inc(*q.adds("dve_step"))
                dve.wait_ge(*q.own("dve_step"))

            def experts(q, more):
                dve.tensor_copy(x[:, :, 0:D], turn_x(q.turn)).then_inc(*q.adds("dve_step"))
                dve.wait_ge(*q.own("dve_step"))
                gates(q)
                for e in range(E2):
                    dve.wait_ge(*q.next("fc2_mm"))
                    for i in range(TT):
                        dst = x[:, i, 0:D]
                        ins = dve.scalar_tensor_tensor(
                            out=dst, in0=ps[:, 4 + 2 * (e % 2) + i // 2, (i % 2) * D:(i % 2 + 1) * D],
                            scalar=cw[:, i, e:e + 1], in1=dst, op0=ALU.mult, op1=ALU.add)
                    ins.then_inc(*q.adds("acc_done"))
                    dve.wait_ge(*q.next("acc_done"))
                    if more and e == 3:
                        norm(q, range(TT), turn_x(q.coming), xn, 1e-5, "rows_ready")
                    if more and e == 6:
                        over(q)
                dve.sem_inc(*q.adds("waited"))
                dve.tensor_copy(turn_x(q.turn), x[:, :, 0:D]).then_inc(*q.adds("turn_end"))
                dve.wait_ge(*q.next("turn_end"))

            q = Port(sm)
            norm(q, range(TT), turn_x(0), xn, 1e-5, "rows_ready")
            dve.sem_inc(*q.adds("acc_done"))
            dve.sem_inc(*q.adds("acc_done"))
            q.passed("acc_done", 2)
            q.passed("fc2_mm", 2)
            over(q)
            with dve.Fori(0, TURNS - 1) as t:
                q.stage(t, t + 1, t, True)
                dve.sem_clear(q.s.sem["dve_step"])
                experts(q, True)
            q.stage(TURNS - 1, rounds=TURNS - 2)
            dve.sem_clear(q.s.sem["dve_step"])
            experts(q, False)

            for z in (lx, xg):
                dve.memset(z[:, :, D:D + 1], 1.0)
            dve.memset(gl[:, :, :], 0.0).then_inc(set_b, 1)
            dve.wait_ge(set_b, 1)
            jobs = side_b0, side_b1, side_b2
            dve.wait_ge(ld_b, 16 * len(loads_b))
            q = Port(sbb)
            start_b(q, run, jobs)
            dve.wait_ge(ld_ffn, 16 * len(loads_ffn))
            dve.tensor_tensor(ffn2[:, :, 0, :], ffn2[:, :, 0, :], ffn2[:, :, 1, :], ALU.add)
            dve.tensor_tensor(ffn2a[:, :, 0, :], ffn2a[:, :, 0, :], ffn2a[:, :, 1, :], ALU.add)\
                .then_inc(ffn2_summed, 1)
            with dve.Fori(0, TURNS - 1) as t:
                q.stage(t, t + 1, t, True)
                dve.sem_clear(q.s.sem["dve_step"])
                round_b(q, run, jobs, True)
            q.stage(TURNS - 1, rounds=TURNS - 2)
            dve.sem_clear(q.s.sem["dve_step"])
            round_b(q, run, jobs, False)

        return {"a": sa.made, "m": sm.made, "b": sbb.made}


def attention_weights(w, b):
    o = np.zeros((CH + 1, 2, WL), np.float32)
    qk = o[:, :, 0:2 * QUADS * 128].reshape(CH + 1, 2, 2, HEADS, 32)
    for c in range(2):
        rows = slice(c * CH, (c + 1) * CH)
        qk[0:CH, c, :, :, 0:HD] = w[rows, 0:2 * D].reshape(CH, 2, HEADS, HD)
        o[0:CH, c, 768:] = w[rows, 2 * D:3 * D]
    if b is not None:
        qk[CH, 1, :, :, 0:HD] = b[0:2 * D].reshape(2, HEADS, HD)
        o[CH, 1, 768:] = b[2 * D:3 * D]
    return o


def by_chunk(w, b=None):
    o = np.zeros((CH + (b is not None), 2, w.shape[1]), np.float32)
    o[0:CH] = w.reshape(2, CH, -1).transpose(1, 0, 2)
    if b is not None:
        o[CH, 1] = b
    return o


def rel_weights(rh, rw, n):
    o = np.zeros((QH, 32, 2, n, QH, RR), np.float32)
    idx = np.arange(n)[:, None] - np.arange(n)[None, :] + n - 1
    for j in range(QH):
        for axis, table in enumerate((rh, rw)):
            o[j, 0:HD, axis, :, j, 0:n] = table[idx].transpose(2, 0, 1)
    return o.reshape(128, -1)


def constants():
    h, w = np.divmod(np.arange(NTOK), WW)
    window = (h // WS) * 2 + w // WS
    t = np.arange(NTOK)
    e1, e0 = np.zeros((2, 2, RR, NTOK), np.float32)
    e1[0, h, t] = e1[1, w, t] = 1
    e0[0, h % WS, t] = e0[1, w % WS, t] = 1
    edge = np.concatenate([t.reshape(HH, WW)[0:WS, WS:].ravel(), t[WS * WW:]])
    a, b = np.divmod(np.arange(NPAD), WS)
    ee = np.zeros((2, RR, EDGE + NPAD), np.float32)
    ee[:, :, 0:EDGE] = e0[:, :, edge]
    ee[0, a, EDGE + np.arange(NPAD)] = ee[1, b, EDGE + np.arange(NPAD)] = 1
    winrow = np.zeros((2, QH, RR, EDGE), np.float32)
    for n in range(4):
        row = n // 2, WS + n % 2
        real_h, real_w = (WS if n // 2 == 0 else HH - WS), (WS if n % 2 == 0 else WW - WS)
        ee[row][0:EDGE] = window[edge] != n
        ee[row][EDGE:] = (a < real_h) & (b < real_w)
        winrow[n // 2, :, WS + n % 2] = np.where(window[edge] == n, MASKED, 0)
    i = np.arange(128)
    c = np.arange(CH) // 6
    even = (i // 32 % 2 == 0).astype(np.float32)
    par = np.stack([even, 1 - even], 1)
    par = np.stack([par * np.float32(L0.scale), par * np.float32(L3.scale)], 1).astype(np.float32)
    all_ones = np.ones((128, 128))
    ties = np.stack([np.hstack([i[:, None] < i[None, :], all_ones]),
                     np.hstack([all_ones, i[:, None] > i[None, :]])], 1).astype(np.float32)
    return {"ez0": by_head(e0), "ez1": by_head(e1), "eze": by_head(ee), "winrow": winrow.reshape(128, EDGE),
            "par": par, "ties": ties, "tri": np.where(i[None, :] > i[:, None], MASKED, 0).astype(np.float32),
            "ident": np.eye(128, dtype=np.float32),
            "ggrp": np.where(c[:, None] == c[None, :], 1 / 6, 0).astype(np.float32)}


def by_head(z):
    o = np.zeros((2, QH, RR, QH, z.shape[2]), np.float32)
    for j in range(QH):
        o[:, j, :, j] = z
    return o.reshape(128, -1)


def kernel(**inputs):
    import concourse.bacc as bacc
    from concourse.bass_utils import run_bass_kernel_spmd as run

    i = {n: np.asarray(z) for n, z in inputs.items()}
    a = constants()
    a["x"] = i["x"].reshape(B * NTOK, D)
    l0 = attention_weights(i["L0_conv_qkv_w"], i["L0_conv_qkv_b"])
    l1 = attention_weights(i["L1_conv_w_qkv"], i["L1_conv_b_qkv"])
    perm = np.r_[D:2 * D, 0:D, 2 * D:3 * D]
    l2 = attention_weights(i["L2_attn_W_kqv"][:, perm], i["L2_attn_b_kqv"][perm])
    l3 = attention_weights(i["L3_attn_w_qkv"], None)
    a["wp"] = np.stack([by_chunk(i[w], i[b]) for w, b in (("L0_conv_proj_w", "L0_conv_proj_b"),
                                                         ("L1_conv_w_proj", "L1_conv_b_proj"),
                                                         ("L2_attn_W_proj", "L2_attn_b_proj"),
                                                         ("L3_attn_w_out", "L3_attn_b_out"))], 1)
    w1t = i["L3_ffn_w1"].T
    l4 = attention_weights(w1t[:, MLP:], i["L3_ffn_b1"][MLP:])
    a["lw0"], a["lw1"], a["lw2"] = l0, l1, l2
    a["lwb"] = np.stack([l3, l4], 1)
    a["relw0"] = rel_weights(i["L0_conv_rel_pos_h"], i["L0_conv_rel_pos_w"], WS)
    a["relw1"] = rel_weights(i["L1_conv_rel_pos_h"], i["L1_conv_rel_pos_w"], HH)
    a["fc1"] = by_chunk(i["L0_conv_fc1_w"], i["L0_conv_fc1_b"])
    a["fc2"] = i["L0_conv_fc2_w"].reshape(MLP // 128, 128, D).transpose(1, 0, 2)
    a["fc2b"] = i["L0_conv_fc2_b"].reshape(1, D)
    cols = np.zeros((CH + 1, 2, 4), np.float32)
    cols[CH, :, 0::2] = 1
    for n, name in enumerate(("norm1_w", "norm1_b", "norm2_w", "norm2_b")):
        cols[0:CH, :, n] = i["L0_conv_" + name].reshape(2, CH).T
    a["cols"] = cols
    kpad = np.zeros((QUADS, QH, 32, 2, NPAD), np.float32)
    for j in range(QH):
        kpad[:, j, 0:HD, j % 2] = i["L0_conv_qkv_b"][D:2 * D].reshape(QUADS, QH, HD, 1)[:, j]
    a["kpadz"] = kpad.reshape(QUADS, 128, 2, NPAD).transpose(1, 2, 0, 3)
    vpad = np.ones((98, HEADS, VW), np.float32)
    vpad[:, :, 0:HD] = i["L0_conv_qkv_b"][2 * D:].reshape(1, HEADS, HD)
    a["vpad"] = vpad
    a["rout"] = np.concatenate([by_chunk(i["L2_ffn_router_w"].T), by_chunk(i["L3_ffn_w_router"].T)], 2)
    a["moe1"] = i["L2_ffn_w1"].transpose(2, 0, 1).reshape(2, CH, E2, I2).transpose(1, 0, 2, 3)
    a["moe2"] = i["L2_ffn_w2"].transpose(0, 2, 1).reshape(E2, 4, 128, D).transpose(2, 0, 1, 3)
    a["ffn1"] = by_chunk(w1t[:, 0:MLP], i["L3_ffn_b1"][0:MLP])
    w2t = i["L3_ffn_w2"].T.reshape(MLP + D, 2, D)
    a["ffn2"] = w2t[0:MLP].reshape(MLP // 128, 128, 2, D).transpose(1, 0, 2, 3)
    a["ffn2a"] = by_chunk(w2t[MLP:].reshape(D, 2 * D), i["L3_ffn_b2"]).reshape(CH + 1, 2, 2, D)
    a["gb3"] = np.broadcast_to(np.stack([i["L3_ffn_gamma1"], i["L3_ffn_beta1"]])[None], (128, 2, D))
    a = {n: np.ascontiguousarray(z) for n, z in a.items()}

    per = {}
    for _ in range(2):
        nc = bacc.Bacc("TRN2", target_bir_lowering=False, num_devices=1)
        aps = {n: nc.dram_tensor("in_" + n, z.shape, F32, kind="ExternalInput").ap() for n, z in a.items()}
        out = nc.dram_tensor("out", (B * NTOK, D), F32, kind="ExternalOutput").ap()
        per = program(nc, aps, out, per)
    r = run(nc, [{"in_" + n: z for n, z in a.items()}], core_ids=[0])
    return r.results[0]["out"].reshape(B, HH, WW, D)
```
